# Optimizing a Trainium2 kernel written in Bass

```python
import numpy as np
import jax
import jax.numpy as jnp

def _softmax(x, axis=-1):
    return jax.nn.softmax(x, axis=axis)

def _gelu(x):
    return jax.nn.gelu(x, approximate=True)

def _silu(x):
    return jax.nn.silu(x)

def _sigmoid(x):
    return jax.nn.sigmoid(x)

def _layernorm(x, axis=-1, eps=1e-05):
    m = jnp.mean(x, axis=axis, keepdims=True)
    v = jnp.var(x, axis=axis, keepdims=True)
    return (x - m) / jnp.sqrt(v + eps)

def _scatter_add(tgt, idx, src, axis=0):
    return tgt.at[idx].add(src)

def _segment_sum(src, seg, n):
    return jax.ops.segment_sum(src, seg, n)
kernel_name = 'mk_gnn_preln_d4_gnn_r64_bc19e7'

def setup_inputs(seed: int=0):
    np.random.seed(seed)
    _w = jnp.asarray

    def _rec_inputs():
        import jax
        import jax.numpy as jnp
        _gk = jax.random.key(seed)
        x = -0.000202 + 1 * jax.random.normal(jax.random.fold_in(_gk, 1), (50000, 128), jnp.float32)
        src = jax.random.randint(jax.random.fold_in(_gk, 2), (25000,), 0, 50000, jnp.int32)
        dst = jnp.minimum((50000 * jax.random.uniform(jax.random.fold_in(_gk, 3), (25000,)) ** 2.0).astype(jnp.int32), 49999)
        _o = jnp.argsort(dst, stable=True)
        src = src[_o]
        dst = dst[_o]
        edge_type_3 = jax.random.randint(jax.random.fold_in(_gk, 14), (25000,), 0, 3, jnp.int32)
        node_type_3 = jax.random.randint(jax.random.fold_in(_gk, 15), (50000,), 0, 3, jnp.int32)
        return (x, src, dst, edge_type_3, node_type_3)
    x, src, dst, edge_type_3, node_type_3 = _rec_inputs()

    def _L0_gnn_setup():
        import jax, jax.numpy as jnp
        import numpy as np
        N_NODES = 50000
        N_EDGES = 12500
        IN_FEATS = 128
        OUT_FEATS = 128
        key = jax.random.key(seed)
        k1, k2, k3, k4 = jax.random.split(key, 4)
        feature = jax.random.normal(k1, (N_NODES, IN_FEATS), dtype=jnp.float32)
        src = jax.random.randint(k2, (N_EDGES,), 0, N_NODES, dtype=jnp.int32)
        dst = jax.random.randint(k3, (N_EDGES,), 0, N_NODES, dtype=jnp.int32)
        W = jax.random.normal(k4, (IN_FEATS, OUT_FEATS), dtype=jnp.float32) * (1.0 / np.sqrt(IN_FEATS))
        b = jnp.zeros((OUT_FEATS,), dtype=jnp.float32)
        return {'feature': feature, 'src': src, 'dst': dst, 'W': W, 'b': b}
    _L0_gnn_all = _L0_gnn_setup()
    _L0_gnn_in = {k: v for k, v in _L0_gnn_all.items() if k in ('W', 'b')}
    del _L0_gnn_all

    def _L1_gnn_setup():
        import jax, jax.numpy as jnp
        import numpy as np
        N_NODES = 50000
        N_EDGES = 12500
        D_IN = 128
        D_OUT = 128
        key = jax.random.key(seed)
        ks = jax.random.split(key, 8)
        x = jax.random.normal(ks[0], (N_NODES, D_IN), dtype=jnp.float32)
        edge_index = jax.random.randint(ks[1], (2, N_EDGES), 0, N_NODES, dtype=jnp.int64)
        s = 1.0 / np.sqrt(D_IN)
        so = 1.0 / np.sqrt(D_OUT)
        W1 = jax.random.uniform(ks[2], (D_IN, D_OUT), jnp.float32, -s, s)
        b1 = jax.random.uniform(ks[3], (D_OUT,), jnp.float32, -s, s)
        W2 = jax.random.uniform(ks[4], (D_OUT, D_OUT), jnp.float32, -so, so)
        b2 = jax.random.uniform(ks[5], (D_OUT,), jnp.float32, -so, so)
        Wres = jax.random.uniform(ks[6], (D_IN, D_OUT), jnp.float32, -s, s)
        bres = jax.random.uniform(ks[7], (D_OUT,), jnp.float32, -s, s)
        return {'x': x, 'edge_index': edge_index, 'W1': W1, 'b1': b1, 'W2': W2, 'b2': b2, 'Wres': Wres, 'bres': bres}
    _L1_gnn_all = _L1_gnn_setup()
    _L1_gnn_in = {k: v for k, v in _L1_gnn_all.items() if k in ('W1', 'b1', 'W2', 'b2', 'Wres', 'bres')}
    del _L1_gnn_all

    def _L2_gnn_setup():
        import jax, jax.numpy as jnp
        import numpy as np
        N, E, HID, H, DK, KN, KR = (50000, 500000, 128, 8, 16, 3, 3)
        SQRT_DK = np.sqrt(DK).astype(np.float32)
        LN_EPS = 1e-05

        def _typed_proj(x, W, b, tp):
            out = jnp.zeros((x.shape[0], W.shape[-1]), x.dtype)
            for k in range(W.shape[0]):
                m = (tp == k)[:, None]
                out = out + jnp.where(m, x @ W[k] + b[k], 0.0)
            return out

        def _forward(x, Wq, bq, Wk, bk, Wv, bv, rel_pri, rel_att, rel_msg, W_upd, b_upd, ln_gamma, ln_beta, edge_src, edge_dst, node_type, edge_type):
            n = x.shape[0]
            q = _typed_proj(x, Wq, bq, node_type).reshape(n, H, DK)
            kk = _typed_proj(x, Wk, bk, node_type).reshape(n, H, DK)
            vv = _typed_proj(x, Wv, bv, node_type).reshape(n, H, DK)
            qe = q[edge_dst]
            ke = kk[edge_src]
            ve = vv[edge_src]
            k_rel = jnp.zeros_like(ke)
            msg = jnp.zeros_like(ve)
            for r in range(rel_att.shape[0]):
                m = (edge_type == r)[:, None, None]
                k_rel = k_rel + jnp.where(m, jnp.einsum('ehd,hdf->ehf', ke, rel_att[r]), 0.0)
                msg = msg + jnp.where(m, jnp.einsum('ehd,hdf->ehf', ve, rel_msg[r]), 0.0)
            pri_e = rel_pri[edge_type]
            att = jnp.sum(qe * k_rel, axis=-1) * pri_e / SQRT_DK
            seg_max = jax.ops.segment_max(att, edge_dst, num_segments=n)
            att_exp = jnp.exp(att - seg_max[edge_dst])
            denom = jax.ops.segment_sum(att_exp, edge_dst, num_segments=n)
            alpha = att_exp / (denom[edge_dst] + 1e-16)
            aggr = jax.ops.segment_sum(alpha[:, :, None] * msg, edge_dst, num_segments=n)
            aggr = aggr.reshape(n, HID)
            h_new = _typed_proj(jax.nn.gelu(aggr, approximate=False), W_upd, b_upd, node_type)
            out = h_new + x
            mu = jnp.mean(out, axis=-1, keepdims=True)
            var = jnp.var(out, axis=-1, keepdims=True)
            out = (out - mu) * jax.lax.rsqrt(var + LN_EPS)
            out = out * ln_gamma[node_type] + ln_beta[node_type]
            return out
        key = jax.random.key(seed)
        ks = jax.random.split(key, 20)
        f = jnp.float32
        inp = {'x': jax.random.normal(ks[0], (N, HID), f), 'Wq': jax.random.normal(ks[1], (KN, HID, HID), f) * 0.05, 'bq': jnp.zeros((KN, HID), f), 'Wk': jax.random.normal(ks[2], (KN, HID, HID), f) * 0.05, 'bk': jnp.zeros((KN, HID), f), 'Wv': jax.random.normal(ks[3], (KN, HID, HID), f) * 0.05, 'bv': jnp.zeros((KN, HID), f), 'rel_pri': jnp.ones((KR, H), f), 'rel_att': jax.random.normal(ks[4], (KR, H, DK, DK), f) * (6.0 / (DK + DK)) ** 0.5, 'rel_msg': jax.random.normal(ks[5], (KR, H, DK, DK), f) * (6.0 / (DK + DK)) ** 0.5, 'W_upd': jax.random.normal(ks[6], (KN, HID, HID), f) * 0.05, 'b_upd': jnp.zeros((KN, HID), f), 'ln_gamma': jnp.ones((KN, HID), f), 'ln_beta': jnp.zeros((KN, HID), f), 'edge_src': jax.random.randint(ks[7], (E,), 0, N), 'edge_dst': jax.random.randint(ks[8], (E,), 0, N), 'node_type': jax.random.randint(ks[9], (N,), 0, KN), 'edge_type': jax.random.randint(ks[10], (E,), 0, KR)}
        return inp
    _L2_gnn_all = _L2_gnn_setup()
    _L2_gnn_in = {k: v for k, v in _L2_gnn_all.items() if k in ('Wq', 'bq', 'Wk', 'bk', 'Wv', 'bv', 'rel_pri', 'rel_att', 'rel_msg', 'W_upd', 'b_upd', 'ln_gamma', 'ln_beta')}
    del _L2_gnn_all

    def _L3_gnn_setup():
        import jax, jax.numpy as jnp
        import numpy as np
        N_NODES = 100000
        N_EDGES = 25000
        D_FEAT = 128
        UNITS = 128
        LEAKY_ALPHA = 0.2
        key = jax.random.key(seed)
        k1, k2, k3, k4 = jax.random.split(key, 4)
        node_states = jax.random.normal(k1, (N_NODES, D_FEAT), dtype=jnp.float32)
        edges = jax.random.randint(k2, (N_EDGES, 2), 0, N_NODES, dtype=jnp.int64)
        kernel = jax.random.normal(k3, (D_FEAT, UNITS), dtype=jnp.float32) * (1.0 / np.sqrt(D_FEAT))
        kernel_attention = jax.random.normal(k4, (2 * UNITS, 1), dtype=jnp.float32) * (1.0 / np.sqrt(2 * UNITS))
        return {'node_states': node_states, 'edges': edges, 'kernel': kernel, 'kernel_attention': kernel_attention}
    _L3_gnn_all = _L3_gnn_setup()
    _L3_gnn_in = {k: v for k, v in _L3_gnn_all.items() if k in ('kernel', 'kernel_attention')}
    del _L3_gnn_all
    return {'x': x, 'src': src, 'dst': dst, 'edge_type_3': edge_type_3, 'node_type_3': node_type_3, 'L0_gnn_W': _L0_gnn_in['W'], 'L0_gnn_b': _L0_gnn_in['b'], 'L1_gnn_W1': _L1_gnn_in['W1'], 'L1_gnn_b1': _L1_gnn_in['b1'], 'L1_gnn_W2': _L1_gnn_in['W2'], 'L1_gnn_b2': _L1_gnn_in['b2'], 'L1_gnn_Wres': _L1_gnn_in['Wres'], 'L1_gnn_bres': _L1_gnn_in['bres'], 'L2_gnn_Wq': _L2_gnn_in['Wq'], 'L2_gnn_bq': _L2_gnn_in['bq'], 'L2_gnn_Wk': _L2_gnn_in['Wk'], 'L2_gnn_bk': _L2_gnn_in['bk'], 'L2_gnn_Wv': _L2_gnn_in['Wv'], 'L2_gnn_bv': _L2_gnn_in['bv'], 'L2_gnn_rel_pri': _L2_gnn_in['rel_pri'], 'L2_gnn_rel_att': _L2_gnn_in['rel_att'], 'L2_gnn_rel_msg': _L2_gnn_in['rel_msg'], 'L2_gnn_W_upd': _L2_gnn_in['W_upd'], 'L2_gnn_b_upd': _L2_gnn_in['b_upd'], 'L2_gnn_ln_gamma': _L2_gnn_in['ln_gamma'], 'L2_gnn_ln_beta': _L2_gnn_in['ln_beta'], 'L3_gnn_kernel': _L3_gnn_in['kernel'], 'L3_gnn_kernel_attention': _L3_gnn_in['kernel_attention']}

def reference(x, src, dst, edge_type_3, node_type_3, L0_gnn_W, L0_gnn_b, L1_gnn_W1, L1_gnn_b1, L1_gnn_W2, L1_gnn_b2, L1_gnn_Wres, L1_gnn_bres, L2_gnn_Wq, L2_gnn_bq, L2_gnn_Wk, L2_gnn_bk, L2_gnn_Wv, L2_gnn_bv, L2_gnn_rel_pri, L2_gnn_rel_att, L2_gnn_rel_msg, L2_gnn_W_upd, L2_gnn_b_upd, L2_gnn_ln_gamma, L2_gnn_ln_beta, L3_gnn_kernel, L3_gnn_kernel_attention):
    import jax
    import jax.numpy as jnp

    def _L0_gnn_ref(feature, src, dst, W, b):
        import jax, jax.numpy as jnp
        import numpy as np
        N_NODES = 50000
        N_EDGES = 12500
        IN_FEATS = 128
        OUT_FEATS = 128
        msgs = feature[src]
        agg = jax.ops.segment_sum(msgs, dst, num_segments=feature.shape[0])
        h = jnp.dot(agg, W) + b
        return jax.nn.relu(h)

    def _L1_gnn_ref(x, edge_index, W1, b1, W2, b2, Wres, bres):
        import jax, jax.numpy as jnp
        import numpy as np
        N_NODES = 50000
        N_EDGES = 12500
        D_IN = 128
        D_OUT = 128
        src = edge_index[0]
        dst = edge_index[1]
        agg = jax.ops.segment_sum(x[src], dst, num_segments=x.shape[0])
        h = x + agg
        h = jnp.maximum(h @ W1 + b1, 0.0) @ W2 + b2
        res = x @ Wres + bres
        return res + h

    def _L2_gnn_ref(x, Wq, bq, Wk, bk, Wv, bv, rel_pri, rel_att, rel_msg, W_upd, b_upd, ln_gamma, ln_beta, edge_src, edge_dst, node_type, edge_type):
        import jax, jax.numpy as jnp
        import numpy as np
        N, E, HID, H, DK, KN, KR = (50000, 500000, 128, 8, 16, 3, 3)
        SQRT_DK = np.sqrt(DK).astype(np.float32)
        LN_EPS = 1e-05

        def _typed_proj(x, W, b, tp):
            out = jnp.zeros((x.shape[0], W.shape[-1]), x.dtype)
            for k in range(W.shape[0]):
                m = (tp == k)[:, None]
                out = out + jnp.where(m, x @ W[k] + b[k], 0.0)
            return out

        def _forward(x, Wq, bq, Wk, bk, Wv, bv, rel_pri, rel_att, rel_msg, W_upd, b_upd, ln_gamma, ln_beta, edge_src, edge_dst, node_type, edge_type):
            n = x.shape[0]
            q = _typed_proj(x, Wq, bq, node_type).reshape(n, H, DK)
            kk = _typed_proj(x, Wk, bk, node_type).reshape(n, H, DK)
            vv = _typed_proj(x, Wv, bv, node_type).reshape(n, H, DK)
            qe = q[edge_dst]
            ke = kk[edge_src]
            ve = vv[edge_src]
            k_rel = jnp.zeros_like(ke)
            msg = jnp.zeros_like(ve)
            for r in range(rel_att.shape[0]):
                m = (edge_type == r)[:, None, None]
                k_rel = k_rel + jnp.where(m, jnp.einsum('ehd,hdf->ehf', ke, rel_att[r]), 0.0)
                msg = msg + jnp.where(m, jnp.einsum('ehd,hdf->ehf', ve, rel_msg[r]), 0.0)
            pri_e = rel_pri[edge_type]
            att = jnp.sum(qe * k_rel, axis=-1) * pri_e / SQRT_DK
            seg_max = jax.ops.segment_max(att, edge_dst, num_segments=n)
            att_exp = jnp.exp(att - seg_max[edge_dst])
            denom = jax.ops.segment_sum(att_exp, edge_dst, num_segments=n)
            alpha = att_exp / (denom[edge_dst] + 1e-16)
            aggr = jax.ops.segment_sum(alpha[:, :, None] * msg, edge_dst, num_segments=n)
            aggr = aggr.reshape(n, HID)
            h_new = _typed_proj(jax.nn.gelu(aggr, approximate=False), W_upd, b_upd, node_type)
            out = h_new + x
            mu = jnp.mean(out, axis=-1, keepdims=True)
            var = jnp.var(out, axis=-1, keepdims=True)
            out = (out - mu) * jax.lax.rsqrt(var + LN_EPS)
            out = out * ln_gamma[node_type] + ln_beta[node_type]
            return out
        return _forward(x, Wq, bq, Wk, bk, Wv, bv, rel_pri, rel_att, rel_msg, W_upd, b_upd, ln_gamma, ln_beta, edge_src, edge_dst, node_type, edge_type)

    def _L3_gnn_ref(node_states, edges, kernel, kernel_attention):
        import jax, jax.numpy as jnp
        import numpy as np
        N_NODES = 100000
        N_EDGES = 25000
        D_FEAT = 128
        UNITS = 128
        LEAKY_ALPHA = 0.2
        n = node_states.shape[0]
        tgt_idx = edges[:, 0]
        src_idx = edges[:, 1]
        h = node_states @ kernel
        ka_t = kernel_attention[:UNITS, 0]
        ka_s = kernel_attention[UNITS:, 0]
        score_t = h @ ka_t
        score_s = h @ ka_s
        e = score_t[tgt_idx] + score_s[src_idx]
        e = jax.nn.leaky_relu(e, negative_slope=LEAKY_ALPHA)
        e = jnp.exp(jnp.clip(e, -2.0, 2.0))
        sum_e = jax.ops.segment_sum(e, tgt_idx, num_segments=n)
        attention = e / (sum_e[tgt_idx] + 1e-09)
        messages = h[src_idx] * attention[:, None]
        output = jax.ops.segment_sum(messages, tgt_idx, num_segments=n)
        return output
    edge_index = jnp.stack([src, dst])
    edge_index_t = jnp.stack([src, dst], axis=1)
    h = jnp.maximum(_layernorm(x, axis=-1), 0.0)
    x = x + _L0_gnn_ref(h, src, dst, L0_gnn_W, L0_gnn_b)
    h = jnp.maximum(_layernorm(x, axis=-1), 0.0)
    x = x + _L1_gnn_ref(h, edge_index, L1_gnn_W1, L1_gnn_b1, L1_gnn_W2, L1_gnn_b2, L1_gnn_Wres, L1_gnn_bres)
    h = jnp.maximum(_layernorm(x, axis=-1), 0.0)
    x = x + _L2_gnn_ref(h, L2_gnn_Wq, L2_gnn_bq, L2_gnn_Wk, L2_gnn_bk, L2_gnn_Wv, L2_gnn_bv, L2_gnn_rel_pri, L2_gnn_rel_att, L2_gnn_rel_msg, L2_gnn_W_upd, L2_gnn_b_upd, L2_gnn_ln_gamma, L2_gnn_ln_beta, src, dst, node_type_3, edge_type_3)
    h = jnp.maximum(_layernorm(x, axis=-1), 0.0)
    x = x + _L3_gnn_ref(h, edge_index_t, L3_gnn_kernel, L3_gnn_kernel_attention)
    return x

_drawn_inputs = setup_inputs


def setup_inputs(seed=0):
    import zlib

    import numpy as np

    out = dict(_drawn_inputs(seed))
    spreads = {'L0_gnn_b': (0.0, 0.1),
     'L2_gnn_bq': (0.0, 2.0),
     'L2_gnn_bk': (0.0, 2.0),
     'L2_gnn_bv': (0.0, 0.316),
     'L2_gnn_rel_pri': (1.0, 0.6),
     'L2_gnn_b_upd': (0.0, 0.1),
     'L2_gnn_ln_gamma': (1.0, 0.2),
     'L2_gnn_ln_beta': (0.0, 0.1)}
    factors = {'L1_gnn_b1': 3.13,
     'L2_gnn_Wq': 7.1,
     'L2_gnn_Wk': 7.109,
     'L2_gnn_rel_att': 7.004,
     'L3_gnn_kernel_attention': 11.914}
    for name, (base, spread) in spreads.items():
        noise = np.random.default_rng([zlib.crc32(name.encode()), seed]).standard_normal(out[name].shape)
        drawn = base * np.exp(spread * noise) if base else spread * noise
        out[name] = jnp.asarray(drawn.astype(out[name].dtype))
    for name, factor in factors.items():
        out[name] = (out[name] * factor).astype(out[name].dtype)
    return out
```

```python
import concourse.bass as bass
from concourse import mybir
from concourse.alu_op_type import AluOpType as ALU
from contextlib import ExitStack

F32 = mybir.dt.float32
I32 = mybir.dt.int32
BF16 = mybir.dt.bfloat16
ACT = mybir.ActivationFunctionType

P = 128
D = 128
T = 4
G = P * T
H = 8
DK = D // H
K = 3
EPS = 1e-5
FAR = 1 << 17
NEVER = -1e30


class Signal:

    def __init__(self, sem, past=0):
        self.sem, self.past = sem, past

    def count(self, value):
        return self.sem, self.past + value


class Own:

    def __init__(self, eng, sem, base=0):
        self.eng, self.sem, self.n, self.base = eng, sem, 0, base

    def step(self, ins):
        ins.then_inc(self.sem, 1)
        self.n += 1
        self.eng.wait_ge(self.sem, self.base + self.n)


def freed(eng, sem, value):
    if isinstance(sem, Signal):
        sem, value = sem.count(value)
    if not isinstance(value, int) or value > 0:
        eng.wait_ge(sem, value)


def turns(eng, n, body):
    body(0, True)
    with eng.Fori(1, n - 1) as i:
        body(i, True)
    body(n - 1, False)


def gnn(nc, NP, EP, src_cols, x, eidx, keys, skeys, etypes, ntype, w, scratch, out):
    NGN, NGE = NP // G, EP // G
    NT = EP // P
    NHI = max(NP // P, P)
    HALF = NGE // 2
    assert NGN == 2 * NGE
    x1, x2, x2n, x3, rec = (scratch[n] for n in ("x1", "x2", "x2n", "x3", "rec"))
    ctx = ExitStack()
    with ctx:
        def sb(name, shape, dt=F32):
            return ctx.enter_context(nc.sbuf_tensor(name, shape, dt))

        def sem(name):
            return ctx.enter_context(nc.semaphore(name))

        def pair(name):
            return [sem(name + "_0"), sem(name + "_1")]

        ident = sb("ident", [P, P])
        ones1 = sb("ones1", [1, P])
        epsc = sb("epsc", [P, 1])
        kinds = sb("kinds", [P, T, K])
        rowno = sb("rowno", [P, 1], I32); rownof = sb("rownof", [P, 1])
        head = sb("head", [P, H]); headT = sb("headT", [H, P])
        W0 = sb("W0", [P, D]); W1 = sb("W1", [P, D]); W2 = sb("W2", [P, D]); Wr = sb("Wr", [P, D])
        b0r = sb("b0r", [1, D]); b1c = sb("b1c", [P, 1]); b2r = sb("b2r", [1, D]); brr = sb("brr", [1, D])
        b0x = sb("b0x", [P, D])
        Wq = sb("Wq", [P, K, D]); Wk = sb("Wk", [P, K, D]); Wv = sb("Wv", [P, K, D]); Wu = sb("Wu", [P, K, D])
        bq = sb("bq", [K, D]); bk = sb("bk", [K, D]); bv = sb("bv", [K, D])
        ubg = sb("ubg", [K, 3, D])
        Ra = sb("Ra", [P, K, D]); Rm = sb("Rm", [P, K, D])
        pri = sb("pri", [H, K]); pric = sb("pric", [P, K])
        W3 = sb("W3", [P, D]); W3T = sb("W3T", [P, P]); ka = sb("ka", [P, 2])
        wsc = sb("wsc", [P, 2]); wtx = sb("wtx", [P, P]); wsx = sb("wsx", [P, P])
        zeros = sb("zeros", [P, P])
        idx_all = sb("idx_all", [P, NGE * 12], I32)

        xs = sb("xs", [P, 2, T, D]); xd = sb("xd", [P, 2, T, D])
        gidx = sb("gidx", [P, 2, 8], I32); sidx = sb("sidx", [P, 2, T], I32)
        same = sb("same", [P, 2, T])
        kb = sb("kb", [P, 2, G + 1], I32); gate = sb("gate", [P, 2, G])
        stats = sb("stats", [P, T, 6]); mv = sb("mv", [P, 2, 2, T, 2])
        sd = sb("sd", [P, 2, 2, T]); rs = sb("rs", [P, 2, 2, T]); nb = sb("nb", [P, 2, 2, T])
        hs = sb("hs", [P, 2, T, D]); hd = sb("hd", [P, 2, T, D])
        agg = sb("agg", [P, 2, G])
        hdT = sb("hdT", [P, G]); sumT = sb("sumT", [P, G]); uT = sb("uT", [P, G])
        row = sb("row", [P, 2, T, D])

        xn = sb("xn", [P, 2, T, D]); yn = sb("yn", [P, 2, T, D]); on = sb("on", [P, 2, T, D])
        hn = sb("hn", [P, 2, T, D]); hnT = sb("hnT", [P, G]); unT = sb("unT", [P, G])
        statn = sb("statn", [P, T, 6]); mvn = sb("mvn", [P, 2, 2, T, 2])
        sdn = sb("sdn", [P, 2, 2, T]); rsn = sb("rsn", [P, 2, 2, T]); nbn = sb("nbn", [P, 2, 2, T])
        ntb = sb("ntb", [K, 2, G], I32); ohn = sb("ohn", [K, 2, G])

        tyi = sb("tyi", [P, 2, 2, T], I32); tyf = sb("tyf", [P, 2, T])
        msk = sb("msk", [P, 2, T, K])
        Dm = sb("Dm", [P, 2, T * K, P])
        sT = sb("sT", [P, T, K, P]); dT = sb("dT", [P, T, K, P])
        ohT = sb("ohT", [K, 2, G])
        eb = sb("eb", [P, 2, G], I32)
        km = sb("km", [P, K, G]); vm = sb("vm", [P, K, G])
        qT = sb("qT", [P, G]); prod = sb("prod", [P, G])
        rst = sb("rst", [H, G]); mx = sb("mx", [H, 2, G + 1])
        ein = sb("ein", [H, 2, G]); eo = sb("eo", [H, 2, G]); den = sb("den", [H, 2, G]); rden = sb("rden", [H, G])
        aS = sb("aS", [P, G]); vA = sb("vA", [P, G]); nrm = sb("nrm", [P, G]); gT = sb("gT", [P, G])
        o2 = sb("o2", [P, T, D]); y2 = sb("y2", [P, T, D])

        scol = sb("scol", [P, NT], I32); dcol = sb("dcol", [P, NT], I32)
        lo = sb("lo", [P, NT]); hi = sb("hi", [P, NT]); digit = sb("digit", [P, NT], I32); keyf = sb("keyf", [P, NT])
        cnt_i = sb("cnt_i", [P, NHI], I32); cnt = sb("cnt", [P, NHI])
        below = sb("below", [P, P])
        above = sb("above", [P, P])
        OL = sb("OL", [P, 2, P]); OH = sb("OH", [P, 2, NHI]); OLT = sb("OLT", [P, P])
        table = sb("table", [P, NHI]); incl = sb("incl", [P, NHI]); onesn = sb("onesn", [P, NHI])
        offs = sb("offs", [P, 1]); skb = sb("skb", [P, 2, P], I32)
        pick = sb("pick", [P, NHI]); pickr = sb("pickr", [P, P])
        pos0 = sb("pos0", [P, 2]); rank = sb("rank", [P, 2])
        posi = sb("posi", [P, 2], I32); recs = sb("recs", [P, 2, 2], I32)
        edge_rec = sb("edge_rec", [P, 2, T, 6], I32); gcol = sb("gcol", [P, 2, T])
        sentinel = sb("sentinel", [1, 2], I32)
        sc3 = sb("sc3", [P, G]); ex = sb("ex", [P, 2, G]); hE = sb("hE", [P, G]); den3 = sb("den3", [P, 2, G])
        rd3 = sb("rd3", [P, G])

        bank = ctx.enter_context(nc.psum_tensor("bank", [P, 8, G], F32))

        w_in, consts, weights = sem("w_in"), sem("consts"), sem("weights")
        prep = {n: sem("prep_" + n) for n in ("pri", "mix", "t", "copy", "wsc")}
        p_in, p_out, p_sum = pair("p_in"), pair("p_out"), sem("p_sum")
        singles, pairs = {}, {}

        def stage(prefix, groups, names, transfers):
            signals = {}
            for n in names.split():
                if prefix + n not in singles:
                    singles[prefix + n] = [sem(prefix + n), 0]
                s, past = singles[prefix + n]
                signals[n] = Signal(s, past)
                singles[prefix + n][1] += groups
            for n, total in transfers.items():
                if prefix + n not in pairs:
                    pairs[prefix + n] = [pair(prefix + n), 0]
                s, past = pairs[prefix + n]
                signals[n] = [Signal(s[b], past) for b in range(2)]
                pairs[prefix + n][1] += total
            return signals

        A = stage("node_", NGN, "var sd ln h t tc u uc z x2", {"in": 16 * NGE, "out": 32 * NGE})
        B = stage("node_", NGN, "var sd ln h oh aff var2 sd2 ln2 y x3", {"in": 16 * NGE, "ty": 16 * NGE, "out": 32 * NGE})
        four = 16 * T * HALF
        L = {}
        L["l0"] = stage("edge_", NGE, "gidx gate var sd ln h t agg z row",
                        {"src": four, "dst": four, "scat": four, "keys": 16 * HALF})
        L["l1"] = stage("edge_", NGE, "gidx gate var sd ln vard sdd lnd h hd t td tdc agg sum u uc z row",
                        {"src": four, "dst": four, "scat": four, "keys": 16 * HALF})
        L["l2"] = stage("edge_", NGE, "gidx gate var sd ln vard sdd lnd h hd diag diagd s sc d dc oh ohc k v km vm q qc kr m "
                        "prod att ein eo a ac c r rden agg nrm g u ubg var3 sd3 ln3 y row",
                        {"src": four, "dst": four, "scat": 2 * four, "keys": 16 * HALF, "types": 2 * four,
                         "etypes": 16 * HALF})
        L["l3"] = stage("edge_", NGE, "gidx gate var sd ln vard sdd lnd h hd t sco scc clip ex gcol he td tdc agg nrm z row",
                        {"src": four, "dst": four, "scat": four, "rec": 48 * HALF})
        R = {n: sem("r_" + n) for n in ("digits", "one", "hist", "rowsum", "offs", "table", "olt", "oltc", "look",
                                         "tile", "tab", "pos", "sent", "row")}
        R.update({n: pair("r_" + n) for n in ("keys", "scat")})
        own_dve = {n: sem("dve_" + n) for n in ("prep", "r1", "r2", "l0", "l1", "l2", "l3")}
        turn, pool_turn = sem("dve_turn"), sem("pool_turn")
        block = ctx.enter_context(nc.Block())

        def rows(dram, g):
            return dram[bass.ds(g * G, G), :].rearrange("(t p) d -> p t d", p=P)

        def tiles(ap):
            return ap.rearrange("p (t d) -> p t d", t=T)

        def at(i, b):
            return i * 2 + b

        def stage_done(eng, l, scatters=1):
            for b in range(2):
                eng.wait_ge(*L[l]["scat"][b].count(16 * T * scatters * HALF))

        LOADS = [(W0[:], w["L0_gnn_W"]), (W1[:], w["L1_gnn_W1"]), (W2[:], w["L1_gnn_W2"]), (Wr[:], w["L1_gnn_Wres"]),
                 (b0r[:], w["L0_gnn_b"].rearrange("(a n) -> a n", a=1)),
                 (b1c[:], w["L1_gnn_b1"].rearrange("(n a) -> n a", a=1)),
                 (b2r[:], w["L1_gnn_b2"].rearrange("(a n) -> a n", a=1)),
                 (brr[:], w["L1_gnn_bres"].rearrange("(a n) -> a n", a=1)),
                 (b0x[:], w["L0_gnn_b"].partition_broadcast(P)),
                 (Wq[:], w["L2_gnn_Wq"].rearrange("k i o -> i k o")), (Wk[:], w["L2_gnn_Wk"].rearrange("k i o -> i k o")),
                 (Wv[:], w["L2_gnn_Wv"].rearrange("k i o -> i k o")), (Wu[:], w["L2_gnn_W_upd"].rearrange("k i o -> i k o")),
                 (bq[:], w["L2_gnn_bq"]), (bk[:], w["L2_gnn_bk"]), (bv[:], w["L2_gnn_bv"]),
                 (ubg[:, 0, :], w["L2_gnn_b_upd"]), (ubg[:, 1, :], w["L2_gnn_ln_gamma"]), (ubg[:, 2, :], w["L2_gnn_ln_beta"]),
                 (pri[:], w["L2_gnn_rel_pri"]),
                 (W3[:], w["L3_gnn_kernel"]), (ka[:], w["L3_gnn_kernel_attention"]),
                 (idx_all[:], eidx), (scol[:], src_cols[0]), (dcol[:], src_cols[1])]
        REL = [(dst[DK * h:DK * (h + 1), :, DK * h:DK * (h + 1)], w[name][:, h, :, :].rearrange("r d f -> d r f"))
               for dst, name in ((Ra, "L2_gnn_rel_att"), (Rm, "L2_gnn_rel_msg")) for h in range(H)]
        N_IN = 16 * (len(LOADS) + len(REL))
        N_CONST = 19

        @block.sync
        def _(sp):
            for dst, src in LOADS:
                sp.dma_start(dst, src).then_inc(w_in, 16)
            sp.wait_ge(consts, N_CONST)
            for dst, src in REL:
                sp.dma_start(dst, src).then_inc(w_in, 16)
            sp.dma_start(rec[0:1, :], sentinel[:]).then_inc(R["sent"], 16)
            sp.dma_start(rec[EP + 1:EP + 2, :], sentinel[:]).then_inc(R["sent"], 16)

            def sort_keys(i, more):
                for b in range(2):
                    freed(sp, R["pos"], at(i, b) - 1)
                    sp.dma_start(skb[:, b, :], skeys[bass.ds(at(i, b) * P, P)].partition_broadcast(P))\
                      .then_inc(R["keys"][b], 16)
            turns(sp, NT // 2, sort_keys)

            def load_p(i, more):
                for b in range(2):
                    freed(sp, p_sum, at(i, b) - 1)
                    sp.dma_start(xn[:, b], rows(x, at(i, b))).then_inc(p_in[b], 16)
            turns(sp, NGN // 2, load_p)
            for b in range(2):
                sp.wait_ge(p_out[b], 16 * (NGN // 2))

            def load_keys(S, i, b):
                freed(sp, S["gate"], at(i, b) - 1)
                sp.dma_start(kb[:, b, :], keys[bass.ds(at(i, b) * G, G + 1)].partition_broadcast(P))\
                  .then_inc(S["keys"][b].sem, 16)

            def load_l0_a(i, more):
                for b in range(2):
                    load_keys(L["l0"], i, b)
                    for c in range(2):
                        freed(sp, A["out"][c], 32 * at(i, b))
                        sp.dma_start(xn[:, c], rows(x, at(at(i, b), c))).then_inc(A["in"][c].sem, 16)
            turns(sp, HALF, load_l0_a)
            stage_done(sp, "l0")
            for c in range(2):
                sp.wait_ge(*A["out"][c].count(32 * NGE))

            def load_l1_b(i, more):
                for b in range(2):
                    load_keys(L["l1"], i, b)
                    for c in range(2):
                        freed(sp, B["out"][c], 32 * at(i, b))
                        sp.dma_start(xn[:, c], rows(x2n, at(at(i, b), c))).then_inc(B["in"][c].sem, 16)
                        sp.dma_start(ntb[:, c, :], ntype[bass.ds(at(at(i, b), c) * G, G), :].rearrange("n a -> (n a)")
                                     .partition_broadcast(K)).then_inc(B["ty"][c].sem, 16)
            turns(sp, HALF, load_l1_b)
            stage_done(sp, "l1")

            def load_l2(i, more):
                for b in range(2):
                    load_keys(L["l2"], i, b)
                    freed(sp, L["l2"]["vm"], at(i, b) - 1)
                    sp.dma_start(eb[:, b, :], etypes[bass.ds(at(i, b) * G, G)].partition_broadcast(P))\
                      .then_inc(L["l2"]["etypes"][b].sem, 16)
            turns(sp, HALF, load_l2)
            for b in range(2):
                sp.wait_ge(R["scat"][b], 16 * (NT // 2))
            sp.wait_ge(R["sent"], 32)

            def load_l3(i, more):
                for b in range(2):
                    freed(sp, L["l3"]["row"], at(i, b) - 1)
                    window = rec[bass.ds(at(i, b) * G, G), :]
                    for k in range(3):
                        sp.dma_start(edge_rec[:, b, :, 2 * k:2 * k + 2],
                                     rec[bass.ds(at(i, b) * G + k, G), :].rearrange("(t p) c -> p t c", p=P))\
                          .then_inc(L["l3"]["rec"][b].sem, 16)
            turns(sp, HALF, load_l3)

        @block.gpsimd
        def _(pool):
            def const(ins):
                ins.then_inc(consts, 1)
            for tile_, value in ((ident, 0.0), (ones1, 1.0), (epsc, EPS), (head, 1.0), (headT, 1.0), (Ra, 0.0), (Rm, 0.0),
                                 (zeros, 0.0), (below, 1.0), (above, 1.0), (onesn, 1.0), (sentinel, -1)):
                const(nc.gpsimd.memset(tile_[:], value))
            for k in range(K):
                last = nc.gpsimd.memset(kinds[:, :, k], float(k))
            const(nc.gpsimd.iota(rowno[:], pattern=[[0, 1]], base=0, channel_multiplier=1))
            const(nc.gpsimd.iota(cnt_i[:], pattern=[[1, NHI]], base=0, channel_multiplier=0))
            pool.wait_ge(consts, 14)

            def select(buf, op, base, pattern, mult, fill):
                return nc.gpsimd.affine_select(out=buf[:], in_=buf[:], compare_op=op, fill=fill, base=base,
                                               pattern=pattern, channel_multiplier=mult)
            const(select(ident, ALU.not_equal, 0, [[-1, P]], 1, 1.0))
            const(select(below, ALU.is_ge, -1, [[-1, P]], 1, 0.0))
            const(select(above, ALU.is_ge, -1, [[1, P]], -1, 0.0))
            select(head, ALU.is_ge, 0, [[-DK, H]], 1, 0.0)
            const(select(headT, ALU.is_ge, 0, [[1, P]], -DK, 0.0))
            pool.wait_ge(consts, 18)
            select(head, ALU.is_ge, DK - 1, [[DK, H]], -1, 0.0)
            const(select(headT, ALU.is_ge, DK - 1, [[-1, P]], DK, 0.0))

            def sort_scatter(i, more):
                for b in range(2):
                    pool.wait_ge(R["pos"], at(i, b) + 1)
                    pool.sem_inc(pool_turn, 1)
                    pool.indirect_dma_start(out=rec, out_offset=bass.IndirectOffsetOnAxis(ap=posi[:, b:b + 1], axis=0),
                                            in_=recs[:, b, :], in_offset=None).then_inc(R["scat"][b], 16)
            turns(pool, NT // 2, sort_scatter)

            def gather(table, index, dst, bound, done):
                for t in range(T):
                    pool.indirect_dma_start(out=dst[:, t, :], out_offset=None, in_=table,
                                            in_offset=bass.IndirectOffsetOnAxis(ap=index[:, t:t + 1], axis=0),
                                            bounds_check=bound, oob_is_err=False).then_inc(done.sem, 16)

            def scatter(S, table, i, b):
                for t in range(T):
                    pool.indirect_dma_start(out=table, out_offset=bass.IndirectOffsetOnAxis(ap=sidx[:, b, t:t + 1], axis=0),
                                            in_=row[:, b, t, :], in_offset=None, bounds_check=NP - 1,
                                            oob_is_err=False).then_inc(S["scat"][b].sem, 16)

            def edge_stage(l, table, targets, types=False):
                S = L[l]

                def gathers(i, b):
                    pool.wait_ge(*S["gidx"].count(at(i, b) + 1))
                    freed(pool, S["row"], at(i, b) - 1)
                    pool.sem_inc(pool_turn, 1)
                    gather(table, gidx[:, b, 0:4], xs[:, b], NP - 1, S["src"][b])
                    gather(table, gidx[:, b, 4:8], xd[:, b], NP - 1, S["dst"][b])
                    if types:
                        for k in range(2):
                            gather(ntype, gidx[:, b, 4 * k:4 * k + 4], tyi[:, b, k, :].unsqueeze(2), NP - 1, S["types"][b])

                def scatters(i, b):
                    pool.wait_ge(*S["row"].count(at(i, b) + 1))
                    pool.sem_inc(pool_turn, 1)
                    for target in targets:
                        scatter(S, target, i, b)

                gathers(0, 0)

                def both(i, more):
                    gathers(i, 1)
                    scatters(i, 0)
                    if more:
                        gathers(i + 1, 0)
                    scatters(i, 1)
                turns(pool, HALF, both)
                stage_done(pool, l, len(targets))

            for b in range(2):
                pool.wait_ge(p_out[b], 16 * (NGN // 2))
            edge_stage("l0", x, [x1])
            for c in range(2):
                pool.wait_ge(*A["out"][c].count(32 * NGE))
            edge_stage("l1", x1, [x2])
            for c in range(2):
                pool.wait_ge(*B["out"][c].count(32 * NGE))
            edge_stage("l2", x2, [x3, out], types=True)
            edge_stage("l3", x3, [out])

        @block.vector
        def _(dve):
            def ln_stats(own, src, st, m, ready):
                for t in range(T):
                    last = nc.vector.bn_stats(out=st[:, t, :], in_=src[:, t, :])
                own.step(last)
                dve.sem_inc(turn, 1)
                for t in range(T):
                    last = nc.vector.bn_aggr(out=m[:, t, :], in_=st[:, t, :])
                last.then_inc(ready.sem, 1)

            def ln_shift(own, S, std_ready, g, b, which, m, s_, r_, n_, ready):
                dve.wait_ge(*S[std_ready].count(g + 1))
                own.step(nc.vector.reciprocal(r_[:, b, which, :], s_[:, b, which, :]))
                nc.vector.scalar_tensor_tensor(out=n_[:, b, which, :], in0=m[:, b, which, :, 0], scalar=-1.0,
                                               in1=r_[:, b, which, :], op0=ALU.mult, op1=ALU.mult).then_inc(S[ready].sem, 1)

            dve.wait_ge(w_in, N_IN)
            dve.wait_ge(consts, N_CONST)
            own = Own(dve, own_dve["prep"])
            nc.vector.tensor_copy(rownof[:], rowno[:])
            nc.vector.tensor_copy(cnt[:], cnt_i[:])
            nc.vector.tensor_tensor(out=b2r[:], in0=b2r[:], in1=brr[:], op=ALU.add)
            nc.vector.tensor_copy(keyf[:], scol[:])
            own.step(nc.vector.tensor_scalar_max(b0x[:], b0x[:], 0.0))
            dve.wait_ge(prep["pri"], 1)
            own.step(nc.vector.tensor_scalar(pric[:], bank[:, 0, 0:K], 1.0 / DK ** 0.5, None, ALU.mult))
            for r in range(K):
                own.step(nc.vector.tensor_scalar(Ra[:, r, :], Ra[:, r, :], pric[:, r:r + 1], None, ALU.mult))
            dve.wait_ge(prep["t"], 1)
            nc.vector.tensor_copy(W3T[:], bank[:, 1, 0:P]).then_inc(prep["copy"], 1)
            dve.wait_ge(prep["wsc"], 1)
            own.step(nc.vector.tensor_copy(wsc[:], bank[:, 2, 0:2]))
            own.step(nc.vector.tensor_scalar(wtx[:], zeros[:], wsc[:, 0:1], None, ALU.add))
            nc.vector.tensor_scalar(wsx[:], zeros[:], wsc[:, 1:2], None, ALU.add).then_inc(weights, 1)
            dve.wait_ge(weights, 1)

            def digits(op, value, dst):
                own.step(nc.vector.tensor_single_scalar(digit[:], scol[:], value, op))
                own.step(nc.vector.tensor_copy(dst[:], digit[:]))
            digits(ALU.bitwise_and, P - 1, lo)
            digits(ALU.logical_shift_right, P.bit_length() - 1, hi)

            def one_hots(t, b):
                nc.vector.tensor_scalar(OL[:, b, :], cnt[:, 0:P], lo[:, bass.ds(t, 1)], None, ALU.is_equal)
                nc.vector.tensor_scalar(OH[:, b, :], cnt[:], hi[:, bass.ds(t, 1)], None, ALU.is_equal)\
                  .then_inc(R["one"], 1)

            def count(i, more):
                for b in range(2):
                    freed(dve, R["hist"], at(i, b) - 1)
                    one_hots(at(i, b), b)
            turns(dve, NT // 2, count)
            dve.wait_ge(R["hist"], NT)
            own = Own(dve, own_dve["r1"])
            own.step(nc.vector.tensor_copy(table[:], bank[:, 5, 0:NHI]))
            own.step(nc.vector.tensor_tensor_scan(out=incl[:], data0=onesn[:], data1=table[:], initial=0.0,
                                                  op0=ALU.mult, op1=ALU.add))
            nc.vector.tensor_copy(offs[:], incl[:, NHI - 1:NHI]).then_inc(R["rowsum"], 1)
            dve.wait_ge(R["offs"], 1)
            own.step(nc.vector.tensor_copy(offs[:], bank[:, 6, 0:1]))
            nc.vector.scalar_tensor_tensor(out=table[:], in0=incl[:], scalar=offs[:, 0:1], in1=table[:],
                                           op0=ALU.add, op1=ALU.subtract).then_inc(R["tab"], 1)

            def place(i, more):
                own = Own(dve, own_dve["r2"], i * 6)
                for b in range(2):
                    t = at(i, b)
                    one_hots(t, b)
                    dve.wait_ge(R["olt"], t + 1)
                    nc.vector.tensor_copy(OLT[:], bank[:, 6, 0:P]).then_inc(R["oltc"], 1)
                    dve.wait_ge(R["keys"][b], 16 * i + 16)
                    own.step(nc.vector.scalar_tensor_tensor(
                        out=pickr[:], in0=skb[:, b, :], scalar=keyf[:, bass.ds(t, 1)], in1=below[:],
                        op0=ALU.is_equal, op1=ALU.mult, accum_out=rank[:, b:b + 1]))
                    dve.wait_ge(R["look"], t + 1)
                    own.step(nc.vector.scalar_tensor_tensor(
                        out=pick[:], in0=cnt[:], scalar=hi[:, bass.ds(t, 1)], in1=bank[:, 7, 0:NHI],
                        op0=ALU.is_equal, op1=ALU.mult, accum_out=pos0[:, b:b + 1]))
                    dve.wait_ge(R["tile"], t + 1)
                    dve.wait_ge(R["tab"], t + 1)
                    nc.vector.tensor_tensor(out=table[:], in0=table[:], in1=bank[:, 5, 0:NHI], op=ALU.add)\
                      .then_inc(R["tab"], 1)
                    freed(dve, R["scat"][b], 16 * i)
                    nc.vector.tensor_copy(recs[:, b, 0:1], scol[:, bass.ds(t, 1)])
                    nc.vector.tensor_copy(recs[:, b, 1:2], dcol[:, bass.ds(t, 1)])
                    own.step(nc.vector.tensor_tensor(out=pos0[:, b:b + 1], in0=pos0[:, b:b + 1], in1=rank[:, b:b + 1],
                                                     op=ALU.add))
                    nc.vector.tensor_scalar(posi[:, b:b + 1], pos0[:, b:b + 1], 1.0, None, ALU.add).then_inc(R["pos"], 1)
                assert own.n == 6
            turns(dve, NT // 2, place)

            relu_b0 = b0x[:, :].unsqueeze(1).to_broadcast([P, T, D])

            def sum_p(i, more):
                for b in range(2):
                    dve.wait_ge(p_in[b], 16 * i + 16)
                    freed(dve, p_out[b], 16 * i)
                    nc.vector.tensor_tensor(out=yn[:, b], in0=xn[:, b], in1=relu_b0, op=ALU.add).then_inc(p_sum, 1)
            turns(dve, NGN // 2, sum_p)
            for b in range(2):
                dve.wait_ge(p_out[b], 16 * (NGN // 2))

            def next_gather(S, i, b, index):
                freed(dve, S["src"][b], 16 * T * i)
                freed(dve, S["dst"][b], 16 * T * i)
                if "types" in S:
                    freed(dve, S["types"][b], 32 * T * i)
                if index is None:
                    nc.vector.tensor_copy(gidx[:, b, :], idx_all[:, bass.ds(at(i, b) * 12, 8)]).then_inc(S["gidx"].sem, 1)
                else:
                    dve.wait_ge(*S["rec"][b].count(48 * i + 48))
                    nc.vector.tensor_copy(gidx[:, b, 0:4], edge_rec[:, b, :, 3])
                    nc.vector.tensor_copy(gidx[:, b, 4:8], edge_rec[:, b, :, 2]).then_inc(S["gidx"].sem, 1)

            def scatter_idx(own, S, i, b, targets, key, following):
                freed(dve, S["scat"][b], 16 * T * targets * i)
                own.step(nc.vector.tensor_tensor(out=same[:, b, :], in0=key, in1=following, op=ALU.is_equal))
                own.step(nc.vector.scalar_tensor_tensor(out=sidx[:, b, :], in0=same[:, b, :], scalar=float(FAR),
                                                        in1=key, op0=ALU.mult, op1=ALU.add))

            def edge_keys(i, b):
                return (idx_all[:, bass.ds(at(i, b) * 12 + 4, 4)], idx_all[:, bass.ds(at(i, b) * 12 + 8, 4)])

            def gates(S, i, b, parts, buf):
                dve.wait_ge(*S["keys"][b].count(16 * i + 16))
                nc.vector.tensor_tensor(out=buf, in0=kb[0:parts, b, 1:G + 1], in1=kb[0:parts, b, 0:G], op=ALU.is_equal)\
                  .then_inc(S["gate"].sem, 1)

            def segment_sum(S, i, b, values):
                g = at(i, b)
                dve.wait_ge(*S["gate"].count(g + 1))
                dve.wait_ge(*S["t"].count(g + 1))
                freed(dve, S["agg"], g)
                nc.vector.tensor_tensor_scan(out=agg[:, b, :], data0=gate[:, b, :], data1=values,
                                             initial=agg[:, 1 - b, G - 1:G], op0=ALU.mult, op1=ALU.add)\
                  .then_inc(S["agg"].sem, 1)

            def l0_sums(own, i, b):
                S, g = L["l0"], at(i, b)
                dve.wait_ge(*S["src"][b].count(16 * T * (i + 1)))
                ln_stats(own, xs[:, b], stats, mv[:, b, 0], S["var"])
                scatter_idx(own, S, i, b, 1, *edge_keys(i, b))
                ln_shift(own, S, "sd", g, b, 0, mv, sd, rs, nb, "ln")
                gates(S, i, b, P, gate[:, b, :])
                segment_sum(S, i, b, bank[:, 3, :])

            def l0_rows(i, b):
                S, g = L["l0"], at(i, b)
                dve.wait_ge(*S["dst"][b].count(16 * T * (i + 1)))
                dve.wait_ge(*S["z"].count(g + 1))
                nc.vector.scalar_tensor_tensor(out=row[:, b], in0=tiles(bank[:, 4, :]), scalar=0.0, in1=xd[:, b],
                                               op0=ALU.max, op1=ALU.add).then_inc(S["row"].sem, 1)

            def a_norm(own, j, c):
                g = at(j, c)
                dve.wait_ge(*A["in"][c].count(16 * j + 16))
                freed(dve, A["x2"], g - 1)
                own.step(nc.vector.tensor_tensor(out=yn[:, c], in0=xn[:, c], in1=relu_b0, op=ALU.add))
                ln_stats(own, yn[:, c], statn, mvn[:, c, 0], A["var"])
                ln_shift(own, A, "sd", g, c, 0, mvn, sdn, rsn, nbn, "ln")

            def a_rows(j, c):
                g = at(j, c)
                dve.wait_ge(*A["z"].count(g + 1))
                nc.vector.tensor_tensor(out=xn[:, c], in0=yn[:, c], in1=tiles(bank[:, 2, :]), op=ALU.add)\
                  .then_inc(A["x2"].sem, 1)

            def l0_a(i, more):
                own = Own(dve, own_dve["l0"], i * 20)
                for b in range(2):
                    if b == 0:
                        next_gather(L["l0"], i, 1, None)
                    elif more:
                        next_gather(L["l0"], i + 1, 0, None)
                    a_norm(own, at(i, b), 0)
                    l0_sums(own, i, b)
                    a_rows(at(i, b), 0)
                    a_norm(own, at(i, b), 1)
                    l0_rows(i, b)
                    a_rows(at(i, b), 1)
                assert own.n == 20, own.n
            nc.vector.memset(agg[:, 1, :], 0.0).then_inc(weights, 1)
            dve.wait_ge(weights, 2)
            next_gather(L["l0"], 0, 0, None)
            turns(dve, HALF, l0_a)
            stage_done(dve, "l0")
            for c in range(2):
                dve.wait_ge(*A["out"][c].count(32 * NGE))

            def l1_sums(own, i, b):
                S, g = L["l1"], at(i, b)
                dve.wait_ge(*S["src"][b].count(16 * T * (i + 1)))
                ln_stats(own, xs[:, b], stats, mv[:, b, 0], S["var"])
                dve.wait_ge(*S["dst"][b].count(16 * T * (i + 1)))
                dve.wait_ge(*S["var"].count(g + 1))
                ln_stats(own, xd[:, b], stats, mv[:, b, 1], S["vard"])
                scatter_idx(own, S, i, b, 1, *edge_keys(i, b))
                ln_shift(own, S, "sd", g, b, 0, mv, sd, rs, nb, "ln")
                ln_shift(own, S, "sdd", g, b, 1, mv, sd, rs, nb, "lnd")
                gates(S, i, b, P, gate[:, b, :])
                segment_sum(S, i, b, bank[:, 0, :])
                dve.wait_ge(*S["agg"].count(g + 1))
                dve.wait_ge(*S["tdc"].count(g + 1))
                nc.vector.tensor_tensor(out=sumT[:], in0=agg[:, b, :], in1=hdT[:], op=ALU.add).then_inc(S["sum"].sem, 1)

            def l1_rows(i, b):
                S, g = L["l1"], at(i, b)
                dve.wait_ge(*S["z"].count(g + 1))
                nc.vector.tensor_tensor(out=row[:, b], in0=tiles(bank[:, 3, :]), in1=xd[:, b], op=ALU.add)\
                  .then_inc(S["row"].sem, 1)

            def affine(own, S, g, y, x_in, out_, ready):
                own.step(nc.vector.tensor_tensor(out=y, in0=y, in1=bank[:, 4:8, P:2 * P], op=ALU.mult))
                own.step(nc.vector.tensor_tensor(out=y, in0=y, in1=bank[:, 4:8, 2 * P:3 * P], op=ALU.add))
                nc.vector.tensor_tensor(out=out_, in0=y, in1=x_in, op=ALU.add).then_inc(S[ready].sem, 1)

            def b_norm(own, j, c):
                g = at(j, c)
                dve.wait_ge(*B["in"][c].count(16 * j + 16))
                ln_stats(own, xn[:, c], statn, mvn[:, c, 0], B["var"])
                dve.wait_ge(*B["ty"][c].count(16 * j + 16))
                freed(dve, B["aff"], g - 1)
                nc.vector.tensor_scalar(ohn[:, c, :], ntb[:, c, :], rownof[0:K, 0:1], None, ALU.is_equal)\
                  .then_inc(B["oh"].sem, 1)
                ln_shift(own, B, "sd", g, c, 0, mvn, sdn, rsn, nbn, "ln")

            def b_mid(own, j, c):
                g = at(j, c)
                dve.wait_ge(*B["h"].count(g + 1))
                dve.wait_ge(*B["aff"].count(g + 1))
                own.step(nc.vector.tensor_tensor(out=on[:, c], in0=hn[:, c], in1=bank[:, 4:8, 0:P], op=ALU.add))
                ln_stats(own, on[:, c], statn, mvn[:, c, 1], B["var2"])
                ln_shift(own, B, "sd2", g, c, 1, mvn, sdn, rsn, nbn, "ln2")

            def b_rows(own, j, c):
                g = at(j, c)
                dve.wait_ge(*B["y"].count(g + 1))
                freed(dve, B["out"][c], 32 * j)
                affine(own, B, g, yn[:, c], xn[:, c], on[:, c], "x3")

            def l1_b(i, more):
                own = Own(dve, own_dve["l1"], i * 40)
                for b in range(2):
                    if b == 0:
                        next_gather(L["l1"], i, 1, None)
                    elif more:
                        next_gather(L["l1"], i + 1, 0, None)
                    b_norm(own, at(i, b), 0)
                    l1_sums(own, i, b)
                    b_mid(own, at(i, b), 0)
                    b_rows(own, at(i, b), 0)
                    b_norm(own, at(i, b), 1)
                    l1_rows(i, b)
                    b_mid(own, at(i, b), 1)
                    b_rows(own, at(i, b), 1)
                assert own.n == 40, own.n
            nc.vector.memset(agg[:, 1, :], 0.0).then_inc(weights, 1)
            dve.wait_ge(weights, 3)
            next_gather(L["l1"], 0, 0, None)
            turns(dve, HALF, l1_b)
            stage_done(dve, "l1")
            for c in range(2):
                dve.wait_ge(*B["out"][c].count(32 * NGE))

            def l2_group(own, i, b):
                S, g = L["l2"], at(i, b)
                dve.wait_ge(*S["src"][b].count(16 * T * (i + 1)))
                ln_stats(own, xs[:, b], stats, mv[:, b, 0], S["var"])
                dve.wait_ge(*S["dst"][b].count(16 * T * (i + 1)))
                dve.wait_ge(*S["var"].count(g + 1))
                ln_stats(own, xd[:, b], stats, mv[:, b, 1], S["vard"])
                scatter_idx(own, S, i, b, 2, *edge_keys(i, b))
                ln_shift(own, S, "sd", g, b, 0, mv, sd, rs, nb, "ln")
                ln_shift(own, S, "sdd", g, b, 1, mv, sd, rs, nb, "lnd")
                dve.wait_ge(*S["types"][b].count(32 * T * (i + 1)))
                own.step(nc.vector.tensor_copy(tyf[:], tyi[:, b]))
                for k in range(2):
                    last = nc.vector.tensor_tensor(out=msk[:, k], in0=tyf[:, k, :].unsqueeze(2).to_broadcast([P, T, K]),
                                                   in1=kinds[:], op=ALU.is_equal)
                own.step(last)
                for k, ready in ((0, "diag"), (1, "diagd")):
                    nc.vector.tensor_tensor(
                        out=Dm[:, k], in0=ident[:, :].unsqueeze(1).to_broadcast([P, T * K, P]),
                        in1=msk[:, k].rearrange("p t k -> p (t k)").unsqueeze(2).to_broadcast([P, T * K, P]),
                        op=ALU.mult).then_inc(S[ready].sem, 1)
                gates(S, i, b, H, gate[0:H, b, :])
                dve.wait_ge(*S["gate"].count(g + 1))
                own.step(nc.vector.tensor_scalar(rst[:], gate[0:H, b, :], -NEVER, NEVER, ALU.mult, ALU.add))
                dve.wait_ge(*S["etypes"][b].count(16 * i + 16))
                for src_bank, dst_, ready, done in ((6, km, "k", "km"), (7, vm, "v", "vm")):
                    dve.wait_ge(*S[ready].count(g + 1))
                    for r in range(K):
                        last = nc.vector.scalar_tensor_tensor(out=dst_[:, r, :], in0=eb[:, b, :], scalar=float(r),
                                                              in1=bank[:, src_bank, :], op0=ALU.is_equal, op1=ALU.mult)
                    last.then_inc(S[done].sem, 1)
                dve.wait_ge(*S["kr"].count(g + 1))
                dve.wait_ge(*S["qc"].count(g + 1))
                nc.vector.tensor_tensor(out=prod[:], in0=bank[:, 5, :], in1=qT[:], op=ALU.mult).then_inc(S["prod"].sem, 1)
                dve.wait_ge(*S["att"].count(g + 1))
                att = bank[0:H, 7, :]
                own.step(nc.vector.tensor_copy(mx[:, b, 0:1], mx[:, 1 - b, G:G + 1]))
                own.step(nc.vector.tensor_tensor_scan(out=mx[:, b, 1:G + 1], data0=rst[:], data1=att,
                                                      initial=mx[:, b, 0:1], op0=ALU.add, op1=ALU.max))
                nc.vector.tensor_tensor(out=ein[:, 0, :], in0=att, in1=mx[:, b, 1:G + 1], op=ALU.subtract)
                own.step(nc.vector.tensor_tensor(out=ein[:, 1, :], in0=mx[:, b, 0:G], in1=mx[:, b, 1:G + 1],
                                                 op=ALU.subtract))
                nc.vector.tensor_tensor(out=ein[:, 1, :], in0=ein[:, 1, :], in1=rst[:], op=ALU.add).then_inc(S["ein"].sem, 1)
                dve.wait_ge(*S["eo"].count(g + 1))
                own.step(nc.vector.tensor_tensor_scan(out=den[:, b, :], data0=eo[:, 1, :], data1=eo[:, 0, :],
                                                      initial=den[:, 1 - b, G - 1:G], op0=ALU.mult, op1=ALU.add))
                own.step(nc.vector.tensor_scalar(rden[:], den[:, b, :], 1e-16, None, ALU.add))
                nc.vector.reciprocal(rden[:], rden[:]).then_inc(S["rden"].sem, 1)
                dve.wait_ge(*S["ac"].count(g + 1))
                dve.wait_ge(*S["m"].count(g + 1))
                own.step(nc.vector.tensor_tensor(out=vA[:], in0=bank[:, 6, :], in1=aS[:], op=ALU.mult))
                dve.wait_ge(*S["c"].count(g + 1))
                freed(dve, S["agg"], g)
                nc.vector.tensor_tensor_scan(out=agg[:, b, :], data0=bank[:, 5, :], data1=vA[:],
                                             initial=agg[:, 1 - b, G - 1:G], op0=ALU.mult, op1=ALU.add)\
                  .then_inc(S["agg"].sem, 1)
                dve.wait_ge(*S["agg"].count(g + 1))
                dve.wait_ge(*S["r"].count(g + 1))
                nc.vector.tensor_tensor(out=nrm[:], in0=bank[:, 7, :], in1=agg[:, b, :], op=ALU.mult).then_inc(S["nrm"].sem, 1)
                dve.wait_ge(*S["u"].count(g + 1))
                for k in range(K):
                    for t in range(T):
                        last = nc.vector.scalar_tensor_tensor(
                            out=o2[:, t, :], in0=bank[:, t, k * P:(k + 1) * P], scalar=msk[:, 1, t, k:k + 1],
                            in1=hd[:, b, t, :] if k == 0 else o2[:, t, :], op0=ALU.mult, op1=ALU.add)
                    own.step(last)
                dve.wait_ge(*S["ubg"].count(g + 1))
                own.step(nc.vector.tensor_tensor(out=o2[:], in0=o2[:], in1=bank[:, 4:8, 0:P], op=ALU.add))
                ln_stats(own, o2, stats, mv[:, b, 0], S["var3"])
                ln_shift(own, S, "sd3", g, b, 0, mv, sd, rs, nb, "ln3")
                dve.wait_ge(*S["y"].count(g + 1))
                affine(own, S, g, y2[:], xd[:, b], row[:, b], "row")

            def l2(i, more):
                n2 = 23
                own = Own(dve, own_dve["l2"], i * 2 * n2)
                for b in range(2):
                    if b == 0:
                        next_gather(L["l2"], i, 1, None)
                    elif more:
                        next_gather(L["l2"], i + 1, 0, None)
                    l2_group(own, i, b)
                assert own.n == 2 * n2, own.n
            nc.vector.memset(agg[:, 1, :], 0.0)
            nc.vector.memset(mx[:, 1, :], 0.0)
            nc.vector.memset(den[:, 1, :], 0.0).then_inc(weights, 1)
            dve.wait_ge(weights, 4)
            next_gather(L["l2"], 0, 0, None)
            turns(dve, HALF, l2)
            stage_done(dve, "l2", 2)

            def l3_group(own, i, b):
                S, g = L["l3"], at(i, b)
                dve.wait_ge(*S["src"][b].count(16 * T * (i + 1)))
                ln_stats(own, xs[:, b], stats, mv[:, b, 0], S["var"])
                dve.wait_ge(*S["dst"][b].count(16 * T * (i + 1)))
                dve.wait_ge(*S["var"].count(g + 1))
                ln_stats(own, xd[:, b], stats, mv[:, b, 1], S["vard"])
                key = edge_rec[:, b, :, 2]
                scatter_idx(own, S, i, b, 1, key, edge_rec[:, b, :, 4])
                nc.vector.tensor_tensor(out=gcol[:, b, :], in0=key, in1=edge_rec[:, b, :, 0], op=ALU.is_equal)\
                  .then_inc(S["gcol"].sem, 1)
                ln_shift(own, S, "sd", g, b, 0, mv, sd, rs, nb, "ln")
                ln_shift(own, S, "sdd", g, b, 1, mv, sd, rs, nb, "lnd")
                dve.wait_ge(*S["scc"].count(g + 1))
                own.step(nc.vector.scalar_tensor_tensor(out=sc3[:], in0=sc3[:], scalar=0.2, in1=sc3[:],
                                                        op0=ALU.mult, op1=ALU.max))
                nc.vector.tensor_scalar(sc3[:], sc3[:], -2.0, 2.0, ALU.max, ALU.min).then_inc(S["clip"].sem, 1)
                dve.wait_ge(*S["ex"].count(g + 1))
                dve.wait_ge(*S["t"].count(g + 1))
                own.step(nc.vector.tensor_tensor(out=hE[:], in0=bank[:, 0, :], in1=ex[:, b, :], op=ALU.mult))
                dve.wait_ge(*S["gate"].count(g + 1))
                freed(dve, S["agg"], g)
                nc.vector.tensor_tensor_scan(out=agg[:, b, :], data0=bank[:, 3, :], data1=hE[:],
                                             initial=agg[:, 1 - b, G - 1:G], op0=ALU.mult, op1=ALU.add)
                nc.vector.tensor_tensor_scan(out=den3[:, b, :], data0=bank[:, 3, :], data1=ex[:, b, :],
                                             initial=den3[:, 1 - b, G - 1:G], op0=ALU.mult, op1=ALU.add)\
                  .then_inc(S["agg"].sem, 1)
                dve.wait_ge(*S["agg"].count(g + 1))
                own.step(nc.vector.tensor_scalar(rd3[:], den3[:, b, :], 1e-9, None, ALU.add))
                own.step(nc.vector.reciprocal(rd3[:], rd3[:]))
                nc.vector.tensor_tensor(out=nrm[:], in0=agg[:, b, :], in1=rd3[:], op=ALU.mult).then_inc(S["nrm"].sem, 1)
                dve.wait_ge(*S["z"].count(g + 1))
                nc.vector.tensor_tensor(out=row[:, b], in0=tiles(bank[:, 4, :]), in1=xd[:, b], op=ALU.add)\
                  .then_inc(S["row"].sem, 1)

            def l3(i, more):
                own = Own(dve, own_dve["l3"], i * 20)
                for b in range(2):
                    if b == 0:
                        next_gather(L["l3"], i, 1, True)
                    elif more:
                        next_gather(L["l3"], i + 1, 0, True)
                    l3_group(own, i, b)
                assert own.n == 20, own.n
            nc.vector.memset(agg[:, 1, :], 0.0)
            nc.vector.memset(den3[:, 1, :], 0.0).then_inc(weights, 1)
            dve.wait_ge(weights, 5)
            next_gather(L["l3"], 0, 0, True)
            turns(dve, HALF, l3)

        @block.scalar
        def _(act):
            def std(S, var_ready, g, m, s_, ready):
                act.wait_ge(*S[var_ready].count(g + 1))
                nc.scalar.activation(s_, m[:, :, 1], ACT.Sqrt, bias=epsc[:, 0:1]).then_inc(S[ready].sem, 1)

            def normed(S, ln_ready, g, dst, src, r_, n_, func, ready):
                act.wait_ge(*S[ln_ready].count(g + 1))
                for t in range(T):
                    last = nc.scalar.activation(dst[:, t, :], src[:, t, :], func, bias=n_[:, t:t + 1], scale=r_[:, t:t + 1])
                last.then_inc(S[ready].sem, 1)

            def copy(S, wanted, g, dst, src, ready, func=ACT.Copy, **kw):
                act.wait_ge(*S[wanted].count(g + 1))
                nc.scalar.activation(dst, src, func, **kw).then_inc(S[ready].sem, 1)

            act.wait_ge(w_in, N_IN)
            act.wait_ge(consts, N_CONST)

            def store_p(i, more):
                for b in range(2):
                    act.wait_ge(p_sum, at(i, b) + 1)
                    act.dma_start(rows(x1, at(i, b)), yn[:, b]).then_inc(p_out[b], 16)
            turns(act, NGN // 2, store_p)

            def a_group(j, c):
                g = at(j, c)
                std(A, "var", g, mvn[:, c, 0], sdn[:, c, 0, :], "sd")
                freed(act, A["t"], g - 1)
                normed(A, "ln", g, hn[:, c], yn[:, c], rsn[:, c, 0], nbn[:, c, 0], ACT.Relu, "h")
                freed(act, A["z"], g)
                copy(A, "t", g, hnT[:], bank[:, 0, :], "tc")
                copy(A, "u", g, unT[:], bank[:, 1, :], "uc", ACT.Relu, bias=b1c[:, 0:1])

            def a_store(j, c):
                act.wait_ge(*A["x2"].count(at(j, c) + 1))
                for target in (x2, x2n):
                    act.dma_start(rows(target, at(j, c)), xn[:, c]).then_inc(A["out"][c].sem, 16)

            def l0_a(i, more):
                S = L["l0"]
                for b in range(2):
                    g = at(i, b)
                    a_group(g, 0)
                    std(S, "var", g, mv[:, b, 0], sd[:, b, 0, :], "sd")
                    freed(act, S["t"], g - 1)
                    normed(S, "ln", g, hs[:, b], xs[:, b], rs[:, b, 0], nb[:, b, 0], ACT.Relu, "h")
                    a_store(g, 0)
                    a_group(g, 1)
                    a_store(g, 1)
            turns(act, HALF, l0_a)
            stage_done(act, "l0")
            for c in range(2):
                act.wait_ge(*A["out"][c].count(32 * NGE))

            def b_norm(j, c):
                g = at(j, c)
                std(B, "var", g, mvn[:, c, 0], sdn[:, c, 0, :], "sd")
                freed(act, B["var2"], g - 1)
                normed(B, "ln", g, hn[:, c], xn[:, c], rsn[:, c, 0], nbn[:, c, 0], ACT.Relu, "h")

            def b_rows(j, c):
                g = at(j, c)
                std(B, "var2", g, mvn[:, c, 1], sdn[:, c, 1, :], "sd2")
                freed(act, B["x3"], g - 1)
                normed(B, "ln2", g, yn[:, c], on[:, c], rsn[:, c, 1], nbn[:, c, 1], ACT.Identity, "y")
                act.wait_ge(*B["x3"].count(g + 1))
                for target in (x3, out):
                    act.dma_start(rows(target, g), on[:, c]).then_inc(B["out"][c].sem, 16)

            def l1_b(i, more):
                S = L["l1"]
                for b in range(2):
                    g = at(i, b)
                    b_norm(g, 0)
                    std(S, "var", g, mv[:, b, 0], sd[:, b, 0, :], "sd")
                    std(S, "vard", g, mv[:, b, 1], sd[:, b, 1, :], "sdd")
                    normed(S, "ln", g, hs[:, b], xs[:, b], rs[:, b, 0], nb[:, b, 0], ACT.Relu, "h")
                    normed(S, "lnd", g, hd[:, b], xd[:, b], rs[:, b, 1], nb[:, b, 1], ACT.Relu, "hd")
                    copy(S, "td", g, hdT[:], bank[:, 1, :], "tdc")
                    copy(S, "u", g, uT[:], bank[:, 2, :], "uc", ACT.Relu, bias=b1c[:, 0:1])
                    b_rows(g, 0)
                    b_norm(g, 1)
                    b_rows(g, 1)
            turns(act, HALF, l1_b)
            stage_done(act, "l1")
            for c in range(2):
                act.wait_ge(*B["out"][c].count(32 * NGE))

            def l2(i, more):
                S = L["l2"]
                for b in range(2):
                    g = at(i, b)
                    std(S, "var", g, mv[:, b, 0], sd[:, b, 0, :], "sd")
                    std(S, "vard", g, mv[:, b, 1], sd[:, b, 1, :], "sdd")
                    normed(S, "ln", g, hs[:, b], xs[:, b], rs[:, b, 0], nb[:, b, 0], ACT.Relu, "h")
                    normed(S, "lnd", g, hd[:, b], xd[:, b], rs[:, b, 1], nb[:, b, 1], ACT.Relu, "hd")
                    copy(S, "s", g, sT[:], bank[:, 0:4, 0:K * P].rearrange("p t (k e) -> p t k e", k=K), "sc")
                    copy(S, "oh", g, ohT[:], bank[0:K, 4:6, :], "ohc")
                    copy(S, "d", g, dT[:], bank[:, 0:4, 0:K * P].rearrange("p t (k e) -> p t k e", k=K), "dc")
                    copy(S, "q", g, qT[:], bank[:, 4, :], "qc")
                    copy(S, "ein", g, eo[:], ein[:], "eo", ACT.Exp)
                    copy(S, "a", g, aS[:], bank[:, 4, :], "ac")
                    copy(S, "nrm", g, gT[:], nrm[:], "g", ACT.Gelu)
                    std(S, "var3", g, mv[:, b, 0], sd[:, b, 0, :], "sd3")
                    normed(S, "ln3", g, y2, o2, rs[:, b, 0], nb[:, b, 0], ACT.Identity, "y")
            turns(act, HALF, l2)
            stage_done(act, "l2", 2)

            def l3(i, more):
                S = L["l3"]
                for b in range(2):
                    g = at(i, b)
                    std(S, "var", g, mv[:, b, 0], sd[:, b, 0, :], "sd")
                    std(S, "vard", g, mv[:, b, 1], sd[:, b, 1, :], "sdd")
                    normed(S, "ln", g, hs[:, b], xs[:, b], rs[:, b, 0], nb[:, b, 0], ACT.Relu, "h")
                    normed(S, "lnd", g, hd[:, b], xd[:, b], rs[:, b, 1], nb[:, b, 1], ACT.Relu, "hd")
                    copy(S, "t", g, uT[:], bank[:, 0, :], "he")
                    copy(S, "td", g, hdT[:], bank[:, 1, :], "tdc")
                    copy(S, "sco", g, sc3[:], bank[:, 2, :], "scc")
                    copy(S, "clip", g, ex[:, b, :], sc3[:], "ex", ACT.Exp)
            turns(act, HALF, l3)

        @block.tensor
        def _(pe):
            def transposes(dst, src, ready):
                for t in range(T):
                    last = nc.tensor.transpose(dst[:, t * P:(t + 1) * P], src[:, t, :], ident[:])
                last.then_inc(ready.sem, 1)

            def project(dst, terms, bias, ready):
                for t in range(T):
                    c = slice(t * P, (t + 1) * P)
                    for n, (colsT, W) in enumerate(terms):
                        last = nc.tensor.matmul(dst[:, c], colsT[:, c], W[:], start=(n == 0),
                                                stop=(bias is None and n == len(terms) - 1))
                    if bias is not None:
                        last = nc.tensor.matmul(dst[:, c], ones1[:], bias[:], start=False, stop=True)
                last.then_inc(ready.sem, 1)

            pe.wait_ge(w_in, N_IN)
            pe.wait_ge(consts, N_CONST)
            nc.tensor.matmul(bank[:, 0, 0:K], headT[:], pri[:], start=True, stop=True).then_inc(prep["pri"], 1)
            nc.tensor.transpose(bank[:, 1, 0:P], W3[:], ident[:]).then_inc(prep["t"], 1)
            pe.wait_ge(prep["copy"], 1)
            nc.tensor.matmul(bank[:, 2, 0:2], W3T[:], ka[:], start=True, stop=True).then_inc(prep["wsc"], 1)
            pe.wait_ge(weights, 1)

            def count(i, more):
                for b in range(2):
                    first = isinstance(i, int) and i == 0 and b == 0
                    pe.wait_ge(R["one"], at(i, b) + 1)
                    nc.tensor.matmul(bank[:, 5, 0:NHI], OL[:, b, :], OH[:, b, :], start=first,
                                     stop=(not more and b == 1)).then_inc(R["hist"], 1)
            turns(pe, NT // 2, count)
            pe.wait_ge(R["rowsum"], 1)
            nc.tensor.matmul(bank[:, 6, 0:1], above[:], offs[:], start=True, stop=True).then_inc(R["offs"], 1)

            def place(i, more):
                for b in range(2):
                    t = at(i, b)
                    pe.wait_ge(R["one"], t + 1 + NT)
                    pe.wait_ge(R["tab"], t + 1)
                    nc.tensor.transpose(bank[:, 6, 0:P], OL[:, b, :], ident[:]).then_inc(R["olt"], 1)
                    nc.tensor.matmul(bank[:, 5, 0:NHI], OL[:, b, :], OH[:, b, :], start=True, stop=True)\
                      .then_inc(R["tile"], 1)
                    pe.wait_ge(R["oltc"], t + 1)
                    nc.tensor.matmul(bank[:, 7, 0:NHI], OLT[:], table[:], start=True, stop=True).then_inc(R["look"], 1)
            turns(pe, NT // 2, place)

            def a_hidden(j, c):
                g = at(j, c)
                pe.wait_ge(*A["h"].count(g + 1))
                freed(pe, A["tc"], g)
                transposes(bank[:, 0, :], hn[:, c], A["t"])
                pe.wait_ge(*A["tc"].count(g + 1))
                freed(pe, A["uc"], g)
                nc.tensor.matmul(bank[:, 1, :], W1[:], hnT[:], start=True, stop=True).then_inc(A["u"].sem, 1)

            def a_rows(j, c):
                g = at(j, c)
                pe.wait_ge(*A["uc"].count(g + 1))
                freed(pe, A["x2"], g)
                project(bank[:, 2, :], [(unT, W2), (hnT, Wr)], b2r, A["z"])

            def l0_a(i, more):
                S = L["l0"]
                for b in range(2):
                    g = at(i, b)
                    a_hidden(g, 0)
                    pe.wait_ge(*S["h"].count(g + 1))
                    freed(pe, S["agg"], g)
                    transposes(bank[:, 3, :], hs[:, b], S["t"])
                    a_rows(g, 0)
                    a_hidden(g, 1)
                    pe.wait_ge(*S["agg"].count(g + 1))
                    freed(pe, S["row"], g)
                    project(bank[:, 4, :], [(agg[:, b, :], W0)], b0r, S["z"])
                    a_rows(g, 1)
            turns(pe, HALF, l0_a)
            stage_done(pe, "l0")
            for c in range(2):
                pe.wait_ge(*A["out"][c].count(32 * NGE))

            def type_rows(oh, ready):
                for t in range(T):
                    last = nc.tensor.matmul(bank[:, 4 + t, 0:3 * P], oh[:, t * P:(t + 1) * P],
                                            ubg[:].rearrange("k a d -> k (a d)"), start=True, stop=True)
                last.then_inc(ready.sem, 1)

            def b_types(j, c):
                g = at(j, c)
                pe.wait_ge(*B["oh"].count(g + 1))
                freed(pe, B["x3"], g)
                type_rows(ohn[:, c, :], B["aff"])

            def l1_b(i, more):
                S = L["l1"]
                for b in range(2):
                    g = at(i, b)
                    b_types(g, 0)
                    pe.wait_ge(*S["h"].count(g + 1))
                    freed(pe, S["agg"], g)
                    transposes(bank[:, 0, :], hs[:, b], S["t"])
                    pe.wait_ge(*S["hd"].count(g + 1))
                    transposes(bank[:, 1, :], hd[:, b], S["td"])
                    pe.wait_ge(*S["sum"].count(g + 1))
                    nc.tensor.matmul(bank[:, 2, :], W1[:], sumT[:], start=True, stop=True).then_inc(S["u"].sem, 1)
                    pe.wait_ge(*S["uc"].count(g + 1))
                    freed(pe, S["row"], g)
                    project(bank[:, 3, :], [(uT, W2), (hdT, Wr)], b2r, S["z"])
                    b_types(g, 1)
            turns(pe, HALF, l1_b)
            stage_done(pe, "l1")
            for c in range(2):
                pe.wait_ge(*B["out"][c].count(32 * NGE))

            def masked(src, diag, ready):
                for t in range(T):
                    last = nc.tensor.matmul(bank[:, t, 0:K * P], src[:, t, :],
                                            diag[:, t * K:(t + 1) * K, :].rearrange("p k e -> p (k e)"),
                                            start=True, stop=True)
                last.then_inc(ready.sem, 1)

            def typed(n, W, bias, cols, oh, ready):
                for k in range(K):
                    nc.tensor.matmul(tiles(bank[:, n, :]), W[:, k, :], cols[:, :, k, :], start=(k == 0), stop=False)
                nc.tensor.matmul(bank[:, n, :], bias[:], oh, start=False, stop=True).then_inc(ready.sem, 1)

            def related(n, W, cols, ready):
                for r in range(K):
                    last = nc.tensor.matmul(bank[:, n, :], W[:, r, :], cols[:, r, :], start=(r == 0), stop=(r == K - 1))
                last.then_inc(ready.sem, 1)

            def l2(i, more):
                S = L["l2"]
                for b in range(2):
                    g = at(i, b)
                    pe.wait_ge(*S["diag"].count(g + 1))
                    pe.wait_ge(*S["h"].count(g + 1))
                    masked(hs[:, b], Dm[:, 0], S["s"])
                    for k in range(2):
                        for t in range(T):
                            last = nc.tensor.transpose(bank[0:K, 4 + k, t * P:(t + 1) * P], msk[:, k, t, :], ident[:])
                    last.then_inc(S["oh"].sem, 1)
                    pe.wait_ge(*S["diagd"].count(g + 1))
                    pe.wait_ge(*S["hd"].count(g + 1))
                    pe.wait_ge(*S["sc"].count(g + 1))
                    masked(hd[:, b], Dm[:, 1], S["d"])
                    pe.wait_ge(*S["ohc"].count(g + 1))
                    typed(6, Wk, bk, sT, ohT[:, 0, :], S["k"])
                    typed(7, Wv, bv, sT, ohT[:, 0, :], S["v"])
                    pe.wait_ge(*S["dc"].count(g + 1))
                    typed(4, Wq, bq, dT, ohT[:, 1, :], S["q"])
                    pe.wait_ge(*S["km"].count(g + 1))
                    related(5, Ra, km, S["kr"])
                    pe.wait_ge(*S["vm"].count(g + 1))
                    related(6, Rm, vm, S["m"])
                    pe.wait_ge(*S["prod"].count(g + 1))
                    nc.tensor.matmul(bank[0:H, 7, :], head[:], prod[:], start=True, stop=True).then_inc(S["att"].sem, 1)
                    pe.wait_ge(*S["eo"].count(g + 1))
                    nc.tensor.matmul(bank[:, 4, :], headT[:], eo[:, 0, :], start=True, stop=True).then_inc(S["a"].sem, 1)
                    nc.tensor.matmul(bank[:, 5, :], headT[:], eo[:, 1, :], start=True, stop=True).then_inc(S["c"].sem, 1)
                    pe.wait_ge(*S["rden"].count(g + 1))
                    nc.tensor.matmul(bank[:, 7, :], headT[:], rden[:], start=True, stop=True).then_inc(S["r"].sem, 1)
                    pe.wait_ge(*S["g"].count(g + 1))
                    for t in range(T):
                        last = nc.tensor.matmul(bank[:, t, 0:K * P], gT[:, t * P:(t + 1) * P],
                                                Wu[:].rearrange("p k d -> p (k d)"), start=True, stop=True)
                    last.then_inc(S["u"].sem, 1)
                    type_rows(ohT[:, 1, :], S["ubg"])
                    pe.wait_ge(*S["row"].count(g + 1))
            turns(pe, HALF, l2)
            stage_done(pe, "l2", 2)

            def l3(i, more):
                S = L["l3"]
                for b in range(2):
                    g = at(i, b)
                    pe.wait_ge(*S["gcol"].count(g + 1))
                    freed(pe, S["agg"], g)
                    for t in range(T):
                        last = nc.tensor.matmul(bank[:, 3, t * P:(t + 1) * P], gcol[:, b, t:t + 1].to_broadcast([P, P]),
                                                ident[:], start=True, stop=True)
                    last.then_inc(S["gate"].sem, 1)
                    pe.wait_ge(*S["h"].count(g + 1))
                    transposes(bank[:, 0, :], hs[:, b], S["t"])
                    pe.wait_ge(*S["hd"].count(g + 1))
                    transposes(bank[:, 1, :], hd[:, b], S["td"])
                    pe.wait_ge(*S["he"].count(g + 1))
                    pe.wait_ge(*S["tdc"].count(g + 1))
                    nc.tensor.matmul(bank[:, 2, :], wtx[:], hdT[:], start=True, stop=False)
                    nc.tensor.matmul(bank[:, 2, :], wsx[:], uT[:], start=False, stop=True).then_inc(S["sco"].sem, 1)
                    pe.wait_ge(*S["nrm"].count(g + 1))
                    freed(pe, S["row"], g)
                    project(bank[:, 4, :], [(nrm, W3)], None, S["z"])
            turns(pe, HALF, l3)


def kernel(**inputs):
    import numpy as np
    import concourse.bacc as bacc
    from concourse.bass_utils import run_bass_kernel_spmd as run

    x, src, dst = (np.asarray(inputs[n]) for n in ("x", "src", "dst"))
    N, E = x.shape[0], src.shape[0]
    EP = 2 * G * max(-(-E // (2 * G)), -(-(N + 1) // (4 * G)))
    NP = 2 * EP

    def pad(a, n, value):
        return np.concatenate([a, np.full((n - len(a),) + a.shape[1:], value, a.dtype)])

    srcp, dstp = pad(src, EP, NP - 1), pad(dst, EP, NP - 1)
    etype = pad(np.asarray(inputs["edge_type_3"]), EP, 0)
    ntype = pad(np.asarray(inputs["node_type_3"]), NP, 0)
    end = np.full(1, -1, dst.dtype)
    following = np.concatenate([dstp[1:], end])

    def columns(a):
        return a.reshape(EP // P, P).T

    eidx = np.stack([a.reshape(EP // G, T, P).transpose(2, 0, 1) for a in (srcp, dstp, following)], axis=2).reshape(P, -1)
    feed = {"x": pad(x, NP, 0), "eidx": eidx, "keys": np.concatenate([end, dstp]), "skeys": srcp, "scol": columns(srcp),
            "dcol": columns(dstp), "etype": etype, "ntype": ntype.reshape(NP, 1)}
    names = [n for n in inputs if n[0] == "L"]
    feed.update({n: np.asarray(inputs[n]) for n in names})
    feed["L2_gnn_rel_pri"] = feed["L2_gnn_rel_pri"].T
    feed["L3_gnn_kernel_attention"] = feed["L3_gnn_kernel_attention"].reshape(2, D).T
    feed = {k: np.ascontiguousarray(v) for k, v in feed.items()}

    nc = bacc.Bacc("TRN2", target_bir_lowering=False, num_devices=1)
    ap = {k: nc.dram_tensor("in_" + k, v.shape, mybir.dt.from_np(v.dtype), kind="ExternalInput").ap() for k, v in feed.items()}
    scratch = {n: nc.dram_tensor("mem_" + n, (NP, D), F32, kind="Internal").ap() for n in ("x1", "x2", "x2n", "x3")}
    scratch["rec"] = nc.dram_tensor("mem_rec", (EP + 2, 2), I32, kind="Internal").ap()
    out = nc.dram_tensor("out_x", (NP, D), F32, kind="ExternalOutput").ap()
    gnn(nc, NP, EP, (ap["scol"], ap["dcol"]), ap["x"], ap["eidx"], ap["keys"], ap["skeys"], ap["etype"], ap["ntype"],
        {n: ap[n] for n in names}, scratch, out)
    r = run(nc, [{"in_" + k: v for k, v in feed.items()}], core_ids=[0])
    return r.results[0]["out_x"][:N]
```

```python
import concourse.bass as bass
from concourse import mybir
from concourse.alu_op_type import AluOpType as ALU
from contextlib import ExitStack

F32 = mybir.dt.float32
I32 = mybir.dt.int32
BF16 = mybir.dt.bfloat16
ACT = mybir.ActivationFunctionType

P = 128
D = 128
T = 4
G = P * T
H = 8
DK = D // H
K = 3
EPS = 1e-5
FAR = 1 << 17
NEVER = -1e30


class Signal:

    def __init__(self, sem, past=0):
        self.sem, self.past = sem, past

    def count(self, value):
        return self.sem, self.past + value


class Own:

    def __init__(self, eng, sem):
        self.eng, self.sem, self.n, self.loop = eng, sem, 0, 0

    def step(self, ins):
        ins.then_inc(self.sem, 1)
        self.n += 1
        self.eng.wait_ge(self.sem, self.loop + self.n)


def freed(eng, sem, value):
    if isinstance(sem, Signal):
        sem, value = sem.count(value)
    if not isinstance(value, int) or value > 0:
        eng.wait_ge(sem, value)


def used(eng, sig, value, last):
    eng.wait_ge(*sig.count(min(value, last) if isinstance(value, int) else value))


def turns(eng, n, body, own=None):
    body(0)
    before = own.n if own else 0
    body(1)
    steps = own.n - before if own else 0
    with eng.Fori(2, n - 1) as i:
        if own:
            own.loop = (i - 2) * steps
        body(i)
        if own:
            own.loop, own.n = 0, own.n - steps
    if own:
        own.n += (n - 3) * steps
    body(n - 1)
    body(n)


def pipeline(eng, n, parts, own=None):
    def turn(i):
        for b in range(2):
            for c, lag, work in parts:
                size = 2 if c is None else 4
                k = (b if c is None else 2 * b + c) - lag
                at_i, at_b = i + k // size, k % size
                if not isinstance(i, int) or 0 <= at_i < n:
                    work(at_i, at_b)
    turns(eng, n, turn, own)


def gnn(nc, NP, EP, src_cols, x, eidx, keys, skeys, etypes, ntype, w, scratch, out):
    NGN, NGE = NP // G, EP // G
    NT = EP // P
    NHI = max(NP // P, P)
    HALF = NGE // 2
    assert NGN == 2 * NGE
    x1, x2, x2n, x3, rec = (scratch[n] for n in ("x1", "x2", "x2n", "x3", "rec"))
    edge_kinds = scratch["edge_kinds"]
    ctx = ExitStack()
    with ctx:
        def sb(name, shape, dt=F32):
            return ctx.enter_context(nc.sbuf_tensor(name, shape, dt))

        def sem(name):
            return ctx.enter_context(nc.semaphore(name))

        def pair(name):
            return [sem(name + "_0"), sem(name + "_1")]

        ident = sb("ident", [P, P])
        ones1 = sb("ones1", [1, P])
        epsc = sb("epsc", [P, 1])
        kind = sb("kind", [K * K, 1])
        third = sb("third", [K * K, 3])
        rowno = sb("rowno", [P, 1], I32); rownof = sb("rownof", [P, 1])
        head = sb("head", [P, H]); headT = sb("headT", [H, P])
        W0 = sb("W0", [P, D]); W1 = sb("W1", [P, D]); W2 = sb("W2", [P, D]); Wr = sb("Wr", [P, D])
        b0r = sb("b0r", [1, D]); b1c = sb("b1c", [P, 1]); b2r = sb("b2r", [1, D]); brr = sb("brr", [1, D])
        b0x = sb("b0x", [P, D])
        Wq = sb("Wq", [P, K, D]); Wk = sb("Wk", [P, K, D]); Wv = sb("Wv", [P, K, D]); Wu = sb("Wu", [P, K, D])
        tb = sb("tb", [K * K, 6, D]); tbr = sb("tbr", [K * K, 6, D])
        tbp = sb("tbp", [K * K, 6, D], BF16); tparts = sb("tparts", [K * K, 6, D], BF16)
        Ra = sb("Ra", [P, K, D]); Rm = sb("Rm", [P, K, D])
        pri = sb("pri", [H, K]); pric = sb("pric", [P, K])
        W3 = sb("W3", [P, D]); W3T = sb("W3T", [P, P]); ka = sb("ka", [P, 2])
        wsc = sb("wsc", [P, 2]); wtx = sb("wtx", [P, P]); wsx = sb("wsx", [P, P])
        zeros = sb("zeros", [P, P])
        idx_all = sb("idx_all", [P, NGE * 12], I32)

        xs = sb("xs", [P, 2, T, D]); xd = sb("xd", [P, 2, T, D])
        gidx = sb("gidx", [P, 2, 8], I32); sidx = sb("sidx", [P, 2, T], I32)
        same = sb("same", [P, 2, T])
        kb = sb("kb", [P, 2, G + 1], I32); gate = sb("gate", [P, 2, G])
        stats = sb("stats", [P, 3, T, 6]); mv = sb("mv", [P, 2, 3, T, 2])
        sd = sb("sd", [P, 2, 3, T]); rs = sb("rs", [P, 2, 3, T]); nb = sb("nb", [P, 2, 3, T])
        hs = sb("hs", [P, 2, T, D]); hd = sb("hd", [P, 2, T, D])
        agg = sb("agg", [P, 2, G])
        hdT = sb("hdT", [P, 2, G]); sumT = sb("sumT", [P, G]); uT = sb("uT", [P, G])
        row = sb("row", [P, 2, T, D]); keep = sb("keep", [P, 2, T, D])

        ROOM = 26 * 1024
        arena = sb("arena", [P, ROOM])
        room = [0]

        def view(shape, dt=F32):
            words = 1
            for n in shape[1:]:
                words *= n
            part = arena[0:shape[0], room[0]:room[0] + words]
            room[0] += words
            assert room[0] <= ROOM, room[0]
            if dt is not F32:
                part = part.bitcast(dt)
            if len(shape) == 2:
                return part
            names = "abcd"[:len(shape) - 1]
            spaced = " ".join(names)
            return part.rearrange(f"p ({spaced}) -> p {spaced}", **dict(zip(names, shape[1:])))

        xn = view([P, 4, T, D]); yn = view([P, 2, T, D]); on = view([P, 2, T, D]); xo = view([P, 2, T, D])
        hn = view([P, 2, T, D]); hnT = view([P, 2, G]); unT = view([P, G])
        statn = view([P, 2, T, 6]); mvn = view([P, 2, 2, T, 2])
        sdn = view([P, 2, 2, T]); rsn = view([P, 2, 2, T]); nbn = view([P, 2, 2, T])
        ntb = view([K * K, 4, G], I32); ohn = view([K * K, 4, G // 2]).bitcast(BF16)
        scol = view([P, NT], I32); dcol = view([P, NT], I32)
        lo = view([P, NT]); hi = view([P, NT]); digit = view([P, NT], I32); keyf = view([P, NT])
        cnt_i = view([P, NHI], I32); cnt = view([P, NHI])
        below = view([P, P])
        above = view([P, P])
        OL = view([P, 2, P]); OH = view([P, 2, NHI]); OLT = view([P, 2, P])
        table = view([P, NHI]); incl = view([P, NHI]); onesn = view([P, NHI])
        offs = view([P, 1]); skb = view([P, 4, P], I32)
        pick = view([P, NHI]); pickr = view([P, P])
        pos0 = view([P, 4]); rank = view([P, 4])
        posi = view([P, 4], I32); recs = view([P, 4, 2], I32)
        sentinel = sb("sentinel", [1, 2], I32)
        tyi = view([P, 4, 2], I32)
        TYC = -(-2 * NT // P) * P
        tycol = view([P, TYC]); tyrow = view([P, TYC // P, P])
        room[0] = 0
        tyb = view([P, 2, 2, G])
        ohT = view([K * K, 2, 2, G // 2]).bitcast(BF16)
        sT = view([P, K, G]); dT = view([P, K, G])
        eb = view([P, 2, G], I32)
        km = view([P, K, G]); vm = view([P, K, G])
        qT = view([P, G]); prod = view([P, G])
        rst = view([H, 2, G]); mx = view([H, 2, G + 1])
        ein = view([H, 2, G]); eo = view([H, 2, G]); den = view([H, 2, G]); rr = view([P, T, H]); rb = view([P, T, H, DK])
        aS = view([P, G]); vA = view([P, G]); nrm = view([P, G]); gT = view([P, G]); gm = view([P, K, G])
        o2 = view([P, T, D]); y2 = view([P, T, D])
        edge_rec = view([P, 2, T, 6], I32); gcol = view([P, 2, T])
        sc3 = view([P, G]); ex = view([P, 2, G]); hE = view([P, G]); den3 = view([1, 2, G])
        place3 = view([P, 2, T]); rd3 = view([P, T])

        bank = ctx.enter_context(nc.psum_tensor("bank", [P, 8, G], F32))

        w_in, consts, weights = sem("w_in"), sem("consts"), sem("weights")
        prep = {n: sem("prep_" + n) for n in ("pri", "t", "copy", "wsc")}
        p_in, p_out, p_sum = pair("p_in"), pair("p_out"), sem("p_sum")
        singles, pairs = {}, {}

        def stage(prefix, groups, names, transfers, buffers=2):
            signals = {}
            for n in names.split():
                if prefix + n not in singles:
                    singles[prefix + n] = [sem(prefix + n), 0]
                s, past = singles[prefix + n]
                signals[n] = Signal(s, past)
                singles[prefix + n][1] += groups
            for n, total in transfers.items():
                if prefix + n not in pairs:
                    pairs[prefix + n] = [[sem(f"{prefix}{n}_{b}") for b in range(buffers)], 0]
                s, past = pairs[prefix + n]
                signals[n] = [Signal(s[b], past) for b in range(buffers)]
                pairs[prefix + n][1] += total
            return signals

        A = stage("node_", NGN, "var sd ln h t tc u uc z x2", {"in": 16 * HALF, "out": 32 * HALF}, 4)
        B = stage("node_", NGN, "var sd ln h oh bu gb var2 sd2 ln2 y x3", {"in": 32 * HALF, "out": 32 * HALF}, 4)
        four = 16 * T * HALF
        L = {}
        L["l0"] = stage("edge_", NGE, "gidx gate var sd ln h keep t agg z row",
                        {"src": four, "dst": four, "scat": four, "keys": 16 * HALF})
        L["l1"] = stage("edge_", NGE, "gidx gate var sd ln vard sdd lnd h hd keep t td tdc agg sum u uc z row",
                        {"src": four, "dst": four, "scat": four, "keys": 16 * HALF})
        L["l2"] = stage("edge_", NGE, "gidx gate rst var sd ln vard sdd lnd h hd keep s d ms md oh k v q qc km vm kr m prod att "
                        "ein eo a ac c den dent rden rb r va agg nrm g gm u ubg var3 sd3 ln3 y row",
                        {"src": four, "dst": four, "scat": 2 * four, "keys": 16 * HALF, "types": 48 * HALF})
        L["l3"] = stage("edge_", NGE, "gidx gcol gate var sd ln vard sdd lnd h hd keep t td he tdc sco scc clip ex agg z row",
                        {"src": four, "dst": four, "scat": four, "rec": 48 * HALF})
        R = {n: sem("r_" + n) for n in ("digits", "one", "hist", "rowsum", "offs", "olt", "oltc", "look",
                                         "tile", "tab", "pos", "sent", "tycol", "tyturn", "tyrow", "tyout")}
        R.update({n: [sem(f"r_{n}_{m}") for m in range(4)] for n in ("keys", "scat", "types")})
        own_dve = {n: sem("dve_" + n) for n in ("prep", "r1", "r2", "l0", "l1", "l2", "l3")}
        turn, pool_turn, pe_turn = sem("dve_turn"), sem("pool_turn"), sem("pe_turn")
        block = ctx.enter_context(nc.Block())

        def rows(dram, g):
            return dram[bass.ds(g * G, G), :].rearrange("(t p) d -> p t d", p=P)

        def tiles(ap):
            return ap.rearrange("p (t d) -> p t d", t=T)

        def at(i, b):
            return i * 2 + b

        def node(i, m):
            return i * 4 + m

        def stage_done(eng, l, scatters=1):
            for b in range(2):
                eng.wait_ge(*L[l]["scat"][b].count(16 * T * scatters * HALF))

        LOADS = [(W0[:], w["L0_gnn_W"]), (W1[:], w["L1_gnn_W1"]), (W2[:], w["L1_gnn_W2"]), (Wr[:], w["L1_gnn_Wres"]),
                 (b0r[:], w["L0_gnn_b"].rearrange("(a n) -> a n", a=1)),
                 (b1c[:], w["L1_gnn_b1"].rearrange("(n a) -> n a", a=1)),
                 (b2r[:], w["L1_gnn_b2"].rearrange("(a n) -> a n", a=1)),
                 (brr[:], w["L1_gnn_bres"].rearrange("(a n) -> a n", a=1)),
                 (b0x[:], w["L0_gnn_b"].partition_broadcast(P)),
                 (Wq[:], w["L2_gnn_Wq"].rearrange("k i o -> i k o")), (Wk[:], w["L2_gnn_Wk"].rearrange("k i o -> i k o")),
                 (Wv[:], w["L2_gnn_Wv"].rearrange("k i o -> i k o")), (Wu[:], w["L2_gnn_W_upd"].rearrange("k i o -> i k o")),
                 (pri[:], w["L2_gnn_rel_pri"]),
                 (W3[:], w["L3_gnn_kernel"]), (ka[:], w["L3_gnn_kernel_attention"]),
                 (idx_all[:], eidx), (scol[:], src_cols[0]), (dcol[:], src_cols[1])]
        LOADS += [(tb[K * part:K * part + K, n, :], w["L2_gnn_" + name]) for part in range(3)
                  for n, name in enumerate(("bq", "bk", "bv", "b_upd", "ln_gamma", "ln_beta"))]
        REL = [(dst[DK * h:DK * (h + 1), :, DK * h:DK * (h + 1)], w[name][:, h, :, :].rearrange("r d f -> d r f"))
               for dst, name in ((Ra, "L2_gnn_rel_att"), (Rm, "L2_gnn_rel_msg")) for h in range(H)]
        N_IN = 16 * (len(LOADS) + len(REL))
        N_CONST = 19

        @block.sync
        def _(sp):
            for dst, src in LOADS:
                sp.dma_start(dst, src).then_inc(w_in, 16)
            sp.wait_ge(consts, N_CONST)
            for dst, src in REL:
                sp.dma_start(dst, src).then_inc(w_in, 16)
            sp.dma_start(rec[0:1, :], sentinel[:]).then_inc(R["sent"], 16)
            sp.dma_start(rec[EP + 1:EP + 2, :], sentinel[:]).then_inc(R["sent"], 16)

            def sort_keys(i, m):
                freed(sp, R["pos"], node(i, m) - 3)
                sp.dma_start(skb[:, m, :], skeys[bass.ds(node(i, m) * P, P)].partition_broadcast(P))\
                  .then_inc(R["keys"][m], 16)

            def load_p(i, b):
                freed(sp, p_sum, at(i, b) - 1)
                sp.dma_start(xn[:, b], rows(x, at(i, b))).then_inc(p_in[b], 16)
            pipeline(sp, NT // 4, [(None, 0, load_p), (0, 0, sort_keys), (1, 0, sort_keys)])
            for b in range(2):
                sp.wait_ge(p_out[b], 16 * (NGN // 2))

            def load_keys(l):
                S = L[l]

                def load(i, b):
                    freed(sp, S["gate"], at(i, b) - 1)
                    sp.dma_start(kb[:, b, :], keys[bass.ds(at(i, b) * G, G + 1)].partition_broadcast(P))\
                      .then_inc(S["keys"][b].sem, 16)
                return load

            def load_a(i, m):
                freed(sp, A["var"], node(i, m) - 3)
                sp.dma_start(xn[:, m], rows(x, node(i, m))).then_inc(A["in"][m].sem, 16)
            pipeline(sp, HALF, [(None, 0, load_keys("l0")), (0, 0, load_a), (1, 0, load_a)])
            stage_done(sp, "l0")
            for m in range(4):
                sp.wait_ge(*A["out"][m].count(32 * HALF))

            def load_b(i, m):
                freed(sp, B["x3"], node(i, m) - 3)
                sp.dma_start(xn[:, m], rows(x2n, node(i, m))).then_inc(B["in"][m].sem, 16)
                sp.dma_start(ntb[:, m, :], ntype[bass.ds(node(i, m) * G, G), :].rearrange("n a -> (n a)")
                             .partition_broadcast(K * K)).then_inc(B["in"][m].sem, 16)
            pipeline(sp, HALF, [(None, 0, load_keys("l1")), (0, 0, load_b), (1, 0, load_b)])
            stage_done(sp, "l1")

            sp.wait_ge(R["tyrow"], 1)
            for c in range(TYC // P):
                n = min(P, 2 * NT - c * P)
                sp.dma_start(edge_kinds[c * P:c * P + n, :], tyrow[0:n, c, :]).then_inc(R["tyout"], 16)
            sp.wait_ge(R["tyout"], 16 * (TYC // P))
            flat_kinds = edge_kinds.rearrange("n p -> (n p)")

            def load_types(i, b):
                S, g = L["l2"], at(i, b)
                freed(sp, S["vm"], g - 1)
                sp.dma_start(eb[:, b, :], etypes[bass.ds(g * G, G)].partition_broadcast(P)).then_inc(S["types"][b].sem, 16)
                freed(sp, S["gm"], g - 1)
                for k in range(2):
                    sp.dma_start(tyb[:, b, k, :], flat_kinds[bass.ds(g * G + k * EP, G)].partition_broadcast(P))\
                      .then_inc(S["types"][b].sem, 16)
            pipeline(sp, HALF, [(None, 0, load_keys("l2")), (None, 0, load_types)])
            for m in range(4):
                sp.wait_ge(R["scat"][m], 16 * (NT // 4))
            sp.wait_ge(R["sent"], 32)

            def load_records(i, b):
                freed(sp, L["l3"]["gcol"], at(i, b) - 1)
                for k in range(3):
                    sp.dma_start(edge_rec[:, b, :, 2 * k:2 * k + 2],
                                 rec[bass.ds(at(i, b) * G + k, G), :].rearrange("(t p) c -> p t c", p=P))\
                      .then_inc(L["l3"]["rec"][b].sem, 16)
            pipeline(sp, HALF, [(None, 0, load_records)])

        @block.gpsimd
        def _(pool):
            def const(ins):
                ins.then_inc(consts, 1)
            for tile_, value in ((ident, 0.0), (ones1, 1.0), (epsc, EPS), (head, 1.0), (headT, 1.0), (Ra, 0.0), (Rm, 0.0),
                                 (zeros, 0.0), (below, 1.0), (above, 1.0), (onesn, 1.0), (sentinel, -1)):
                const(nc.gpsimd.memset(tile_[:], value))
            const(nc.gpsimd.iota(rowno[:], pattern=[[0, 1]], base=0, channel_multiplier=1))
            const(nc.gpsimd.iota(cnt_i[:], pattern=[[1, NHI]], base=0, channel_multiplier=0))
            pool.wait_ge(consts, 14)

            def select(buf, op, base, pattern, mult, fill):
                return nc.gpsimd.affine_select(out=buf[:], in_=buf[:], compare_op=op, fill=fill, base=base,
                                               pattern=pattern, channel_multiplier=mult)
            const(select(ident, ALU.not_equal, 0, [[-1, P]], 1, 1.0))
            const(select(below, ALU.is_ge, -1, [[-1, P]], 1, 0.0))
            const(select(above, ALU.is_ge, -1, [[1, P]], -1, 0.0))
            select(head, ALU.is_ge, 0, [[-DK, H]], 1, 0.0)
            const(select(headT, ALU.is_ge, 0, [[1, P]], -DK, 0.0))
            pool.wait_ge(consts, 18)
            select(head, ALU.is_ge, DK - 1, [[DK, H]], -1, 0.0)
            const(select(headT, ALU.is_ge, DK - 1, [[-1, P]], DK, 0.0))

            def sort_scatter(i, m):
                t = node(i, m)
                pool.wait_ge(R["pos"], t + 1)
                pool.sem_inc(pool_turn, 1)
                pool.indirect_dma_start(out=rec, out_offset=bass.IndirectOffsetOnAxis(ap=posi[:, m:m + 1], axis=0),
                                        in_=recs[:, m, :], in_offset=None).then_inc(R["scat"][m], 16)
                freed(pool, R["tycol"], t - 3)
                pool.sem_inc(pool_turn, 1)
                for k in range(2):
                    pool.indirect_dma_start(out=tyi[:, m, k:k + 1], out_offset=None, in_=ntype,
                                            in_offset=bass.IndirectOffsetOnAxis(ap=recs[:, m, k:k + 1], axis=0),
                                            bounds_check=NP - 1, oob_is_err=False).then_inc(R["types"][m], 16)
            pipeline(pool, NT // 4, [(0, 0, sort_scatter), (1, 0, sort_scatter)])

            def gather(table, index, dst, bound, done):
                for t in range(T):
                    pool.indirect_dma_start(out=dst[:, t, :], out_offset=None, in_=table,
                                            in_offset=bass.IndirectOffsetOnAxis(ap=index[:, t:t + 1], axis=0),
                                            bounds_check=bound, oob_is_err=False).then_inc(done.sem, 16)

            def scatter(S, table, i, b):
                for t in range(T):
                    pool.indirect_dma_start(out=table, out_offset=bass.IndirectOffsetOnAxis(ap=sidx[:, b, t:t + 1], axis=0),
                                            in_=row[:, b, t, :], in_offset=None, bounds_check=NP - 1,
                                            oob_is_err=False).then_inc(S["scat"][b].sem, 16)

            def edge_stage(l, table, targets, lag):
                S = L[l]

                def gathers(i, b):
                    pool.wait_ge(*S["gidx"].count(at(i, b) + 1))
                    freed(pool, S["keep"] if "keep" in S else S["row"], at(i, b) - 1)
                    pool.sem_inc(pool_turn, 1)
                    gather(table, gidx[:, b, 0:4], xs[:, b], NP - 1, S["src"][b])
                    gather(table, gidx[:, b, 4:8], xd[:, b], NP - 1, S["dst"][b])

                def scatters(i, b):
                    pool.wait_ge(*S["row"].count(at(i, b) + 1))
                    pool.sem_inc(pool_turn, 1)
                    for target in targets:
                        scatter(S, target, i, b)

                gathers(0, 0)
                pipeline(pool, HALF, [(None, -1, gathers), (None, lag, scatters)])
                stage_done(pool, l, len(targets))

            for b in range(2):
                pool.wait_ge(p_out[b], 16 * (NGN // 2))
            edge_stage("l0", x, [x1], 2)
            for m in range(4):
                pool.wait_ge(*A["out"][m].count(32 * HALF))
            edge_stage("l1", x1, [x2], 2)
            for m in range(4):
                pool.wait_ge(*B["out"][m].count(32 * HALF))
            edge_stage("l2", x2, [x3, out], 2)
            edge_stage("l3", x3, [out], 2)

        @block.vector
        def _(dve):
            def ln_stats(own, src, st, m, S, var, shifted, g):
                freed(dve, S[var], g)
                freed(dve, S[shifted], g - 1)
                for t in range(T):
                    last = nc.vector.bn_stats(out=st[:, t, :], in_=src[:, t, :])
                own.step(last)
                dve.sem_inc(turn, 1)
                for t in range(T):
                    last = nc.vector.bn_aggr(out=m[:, t, :], in_=st[:, t, :])
                last.then_inc(S[var].sem, 1)

            def ln_shift(own, S, std_ready, g, b, which, m, s_, r_, n_, ready):
                dve.wait_ge(*S[std_ready].count(g + 1))
                own.step(nc.vector.reciprocal(r_[:, b, which, :], s_[:, b, which, :]))
                nc.vector.scalar_tensor_tensor(out=n_[:, b, which, :], in0=m[:, b, which, :, 0], scalar=-1.0,
                                               in1=r_[:, b, which, :], op0=ALU.mult, op1=ALU.mult).then_inc(S[ready].sem, 1)

            dve.wait_ge(w_in, N_IN)
            dve.wait_ge(consts, N_CONST)
            own = Own(dve, own_dve["prep"])
            own.step(nc.vector.tensor_copy(rownof[:], rowno[:]))
            nc.vector.tensor_copy(cnt[:], cnt_i[:])
            nc.vector.tensor_tensor(out=b2r[:], in0=b2r[:], in1=brr[:], op=ALU.add)
            nc.vector.tensor_copy(keyf[:], scol[:])
            own.step(nc.vector.tensor_scalar_max(b0x[:], b0x[:], 0.0))
            row9 = rownof[0:K * K, :]
            nc.vector.tensor_scalar(third[:, 0:1], row9, float(K), None, ALU.is_ge)
            own.step(nc.vector.tensor_scalar(third[:, 2:3], row9, float(2 * K), None, ALU.is_ge))
            own.step(nc.vector.scalar_tensor_tensor(out=kind[:], in0=third[:, 0:1], scalar=-float(K), in1=row9,
                                                    op0=ALU.mult, op1=ALU.add))
            own.step(nc.vector.scalar_tensor_tensor(out=kind[:], in0=third[:, 2:3], scalar=-float(K), in1=kind[:],
                                                    op0=ALU.mult, op1=ALU.add))
            own.step(nc.vector.tensor_tensor(out=third[:, 1:2], in0=third[:, 0:1], in1=third[:, 2:3], op=ALU.subtract))
            own.step(nc.vector.tensor_scalar(third[:, 0:1], row9, float(K), None, ALU.is_lt))
            for part in range(3):
                own.step(nc.vector.tensor_copy(tbp[:], tb[:]))
                own.step(nc.vector.tensor_tensor(out=tb[:], in0=tb[:], in1=tbp[:], op=ALU.subtract))
                if part == 0:
                    own.step(nc.vector.tensor_scalar(tbr[:], tbp[:], third[:, 0:1], None, ALU.mult))
                else:
                    own.step(nc.vector.scalar_tensor_tensor(out=tbr[:], in0=tbp[:], scalar=third[:, part:part + 1],
                                                            in1=tbr[:], op0=ALU.mult, op1=ALU.add))
            own.step(nc.vector.tensor_copy(tparts[:], tbr[:]))
            own.step(nc.vector.memset(tycol[:], 0.0))
            dve.wait_ge(prep["pri"], 1)
            own.step(nc.vector.tensor_scalar(pric[:], bank[:, 0, 0:K], 1.0 / DK ** 0.5, None, ALU.mult))
            for r in range(K):
                own.step(nc.vector.tensor_scalar(Ra[:, r, :], Ra[:, r, :], pric[:, r:r + 1], None, ALU.mult))
            dve.wait_ge(prep["t"], 1)
            nc.vector.tensor_copy(W3T[:], bank[:, 1, 0:P]).then_inc(prep["copy"], 1)
            dve.wait_ge(prep["wsc"], 1)
            own.step(nc.vector.tensor_copy(wsc[:], bank[:, 2, 0:2]))
            own.step(nc.vector.tensor_scalar(wtx[:], zeros[:], wsc[:, 0:1], None, ALU.add))
            nc.vector.tensor_scalar(wsx[:], zeros[:], wsc[:, 1:2], None, ALU.add).then_inc(weights, 1)
            dve.wait_ge(weights, 1)

            def digits(op, value, dst):
                own.step(nc.vector.tensor_single_scalar(digit[:], scol[:], value, op))
                own.step(nc.vector.tensor_copy(dst[:], digit[:]))
            digits(ALU.bitwise_and, P - 1, lo)
            digits(ALU.logical_shift_right, P.bit_length() - 1, hi)

            def one_hots(t, b):
                nc.vector.tensor_scalar(OL[:, b, :], cnt[:, 0:P], lo[:, bass.ds(t, 1)], None, ALU.is_equal)
                nc.vector.tensor_scalar(OH[:, b, :], cnt[:], hi[:, bass.ds(t, 1)], None, ALU.is_equal)\
                  .then_inc(R["one"], 1)

            def count(i, b):
                freed(dve, R["hist"], at(i, b) - 1)
                one_hots(at(i, b), b)
            pipeline(dve, NT // 2, [(None, 0, count)])
            dve.wait_ge(R["hist"], NT)
            own = Own(dve, own_dve["r1"])
            own.step(nc.vector.tensor_copy(table[:], bank[:, 5, 0:NHI]))
            own.step(nc.vector.tensor_tensor_scan(out=incl[:], data0=onesn[:], data1=table[:], initial=0.0,
                                                  op0=ALU.mult, op1=ALU.add))
            nc.vector.tensor_copy(offs[:], incl[:, NHI - 1:NHI]).then_inc(R["rowsum"], 1)
            dve.wait_ge(R["offs"], 1)
            own.step(nc.vector.tensor_copy(offs[:], bank[:, 6, 0:1]))
            nc.vector.scalar_tensor_tensor(out=table[:], in0=incl[:], scalar=offs[:, 0:1], in1=table[:],
                                           op0=ALU.add, op1=ALU.subtract).then_inc(R["tab"], 1)

            relu_b0 = b0x[:, :].unsqueeze(1).to_broadcast([P, T, D])
            own = Own(dve, own_dve["r2"])

            def place_hots(i, m):
                t = node(i, m)
                freed(dve, R["tile"], t - 1)
                one_hots(t, m % 2)

            def place_rank(i, m):
                t = node(i, m)
                dve.wait_ge(R["keys"][m], 16 * i + 16)
                freed(dve, R["scat"][m], 16 * i)
                freed(dve, R["types"][m], 32 * i)
                own.step(nc.vector.scalar_tensor_tensor(
                    out=pickr[:], in0=skb[:, m, :], scalar=keyf[:, bass.ds(t, 1)], in1=below[:],
                    op0=ALU.is_equal, op1=ALU.mult, accum_out=rank[:, m:m + 1]))
                nc.vector.tensor_copy(recs[:, m, 0:1], scol[:, bass.ds(t, 1)])
                nc.vector.tensor_copy(recs[:, m, 1:2], dcol[:, bass.ds(t, 1)])

            def place_add(i, m):
                t = node(i, m)
                dve.wait_ge(R["look"], t + 1)
                dve.wait_ge(R["tab"], t + 1)
                nc.vector.tensor_tensor(out=table[:], in0=table[:], in1=bank[:, 4 + m % 2, 0:NHI], op=ALU.add)\
                  .then_inc(R["tab"], 1)

            def place_row(i, m):
                t = node(i, m)
                own.step(nc.vector.scalar_tensor_tensor(
                    out=pick[:], in0=cnt[:], scalar=hi[:, bass.ds(t, 1)], in1=bank[:, 6 + m % 2, 0:NHI],
                    op0=ALU.is_equal, op1=ALU.mult, accum_out=pos0[:, m:m + 1]))
                nc.vector.scalar_tensor_tensor(out=posi[:, m:m + 1], in0=pos0[:, m:m + 1], scalar=1.0,
                                               in1=rank[:, m:m + 1], op0=ALU.add, op1=ALU.add).then_inc(R["pos"], 1)

            def place_types(i, m):
                dve.wait_ge(R["types"][m], 32 * i + 32)
                nc.vector.tensor_copy(tycol[:, bass.ds(node(i, m), 1)], tyi[:, m, 0:1])
                nc.vector.tensor_copy(tycol[:, bass.ds(node(i, m) + NT, 1)], tyi[:, m, 1:2]).then_inc(R["tycol"], 1)

            def sum_p(i, b):
                dve.wait_ge(p_in[b], 16 * i + 16)
                freed(dve, p_out[b], 16 * i)
                nc.vector.tensor_tensor(out=yn[:, b], in0=xn[:, b], in1=relu_b0, op=ALU.add).then_inc(p_sum, 1)
            pipeline(dve, NT // 4, [(c, lag, work) for c in range(2) for lag, work in
                                    ((0, place_hots), (0, place_rank), (1, place_add), (1, place_row),
                                     (4, place_types))] + [(None, 0, sum_p)], own)
            dve.wait_ge(R["tyturn"], 1)
            nc.vector.tensor_copy(tyrow[:], bank[:, 0, 0:TYC].rearrange("p (c e) -> p c e", e=P)).then_inc(R["tyrow"], 1)
            for b in range(2):
                dve.wait_ge(p_out[b], 16 * (NGN // 2))

            def next_gather(S, i, b):
                freed(dve, S["src"][b], 16 * T * i)
                freed(dve, S["dst"][b], 16 * T * i)
                nc.vector.tensor_copy(gidx[:, b, :], idx_all[:, bass.ds(at(i, b) * 12, 8)]).then_inc(S["gidx"].sem, 1)

            def scatter_idx(own, S, i, b, targets, key, following):
                freed(dve, S["scat"][b], 16 * T * targets * i)
                own.step(nc.vector.tensor_tensor(out=same[:, b, :], in0=key, in1=following, op=ALU.is_equal))
                own.step(nc.vector.scalar_tensor_tensor(out=sidx[:, b, :], in0=same[:, b, :], scalar=float(FAR),
                                                        in1=key, op0=ALU.mult, op1=ALU.add))

            def edge_keys(i, b):
                return (idx_all[:, bass.ds(at(i, b) * 12 + 4, 4)], idx_all[:, bass.ds(at(i, b) * 12 + 8, 4)])

            def gates(S, i, b, parts, buf):
                dve.wait_ge(*S["keys"][b].count(16 * i + 16))
                freed(dve, S["agg"], at(i, b) - 1)
                nc.vector.tensor_tensor(out=buf, in0=kb[0:parts, b, 1:G + 1], in1=kb[0:parts, b, 0:G], op=ALU.is_equal)\
                  .then_inc(S["gate"].sem, 1)

            def segment_sum(S, i, b, values):
                g = at(i, b)
                dve.wait_ge(*S["gate"].count(g + 1))
                dve.wait_ge(*S["t"].count(g + 1))
                freed(dve, S["agg"], g)
                nc.vector.tensor_tensor_scan(out=agg[:, b, :], data0=gate[:, b, :], data1=values,
                                             initial=agg[:, 1 - b, G - 1:G], op0=ALU.mult, op1=ALU.add)\
                  .then_inc(S["agg"].sem, 1)

            def affine(own, S, gamma, beta, y, x_in, out_, ready):
                own.step(nc.vector.tensor_tensor(out=y, in0=y, in1=gamma, op=ALU.mult))
                own.step(nc.vector.tensor_tensor(out=y, in0=y, in1=beta, op=ALU.add))
                nc.vector.tensor_tensor(out=out_, in0=y, in1=x_in, op=ALU.add).then_inc(S[ready].sem, 1)

            own = Own(dve, own_dve["l0"])
            S0 = L["l0"]

            def l0_next(i, b):
                next_gather(S0, i, b)

            def l0_stats(i, b):
                dve.wait_ge(*S0["src"][b].count(16 * T * (i + 1)))
                ln_stats(own, xs[:, b], stats[:, 0], mv[:, b, 0], S0, "var", "ln", at(i, b))

            def l0_shift(i, b):
                ln_shift(own, S0, "sd", at(i, b), b, 0, mv, sd, rs, nb, "ln")
                gates(S0, i, b, P, gate[:, b, :])

            def l0_sum(i, b):
                segment_sum(S0, i, b, bank[:, 3, :])

            def l0_rows(i, b):
                g = at(i, b)
                scatter_idx(own, S0, i, b, 1, *edge_keys(i, b))
                dve.wait_ge(*S0["z"].count(g + 1))
                nc.vector.scalar_tensor_tensor(out=row[:, b], in0=tiles(bank[:, 4, :]), scalar=0.0, in1=keep[:, b],
                                               op0=ALU.max, op1=ALU.add).then_inc(S0["row"].sem, 1)

            def a_stats(i, m):
                q = node(i, m)
                dve.wait_ge(*A["in"][m].count(16 * i + 16))
                freed(dve, A["x2"], q - 1)
                own.step(nc.vector.tensor_tensor(out=yn[:, m % 2], in0=xn[:, m], in1=relu_b0, op=ALU.add))
                ln_stats(own, yn[:, m % 2], statn[:, 0], mvn[:, m % 2, 0], A, "var", "ln", node(i, m))

            def a_shift(i, m):
                ln_shift(own, A, "sd", node(i, m), m % 2, 0, mvn, sdn, rsn, nbn, "ln")

            def a_rows(i, m):
                dve.wait_ge(*A["z"].count(node(i, m) + 1))
                if m >= 2:
                    freed(dve, A["out"][m - 2], 32 * i + 32)
                else:
                    freed(dve, A["out"][m + 2], 32 * i)
                nc.vector.tensor_tensor(out=on[:, m % 2], in0=yn[:, m % 2], in1=tiles(bank[:, 2, :]), op=ALU.add)\
                  .then_inc(A["x2"].sem, 1)

            nc.vector.memset(agg[:, 1, :], 0.0).then_inc(weights, 1)
            dve.wait_ge(weights, 2)
            l0_next(0, 0)
            l0_next(0, 1)
            pipeline(dve, HALF, [(None, -2, l0_next), (0, 0, a_stats), (None, 0, l0_stats), (0, 0, a_shift),
                                 (None, 0, l0_shift), (0, 1, a_rows), (1, 0, a_stats), (None, 1, l0_rows),
                                 (1, 0, a_shift), (None, 0, l0_sum), (1, 1, a_rows)], own)
            stage_done(dve, "l0")
            for m in range(4):
                dve.wait_ge(*A["out"][m].count(32 * HALF))

            own = Own(dve, own_dve["l1"])
            S1 = L["l1"]

            def l1_next(i, b):
                next_gather(S1, i, b)

            def l1_stats(i, b):
                dve.wait_ge(*S1["src"][b].count(16 * T * (i + 1)))
                ln_stats(own, xs[:, b], stats[:, 0], mv[:, b, 0], S1, "var", "ln", at(i, b))
                dve.wait_ge(*S1["dst"][b].count(16 * T * (i + 1)))
                dve.wait_ge(*S1["var"].count(at(i, b) + 1))
                ln_stats(own, xd[:, b], stats[:, 1], mv[:, b, 1], S1, "vard", "lnd", at(i, b))

            def l1_shift(i, b):
                ln_shift(own, S1, "sd", at(i, b), b, 0, mv, sd, rs, nb, "ln")
                ln_shift(own, S1, "sdd", at(i, b), b, 1, mv, sd, rs, nb, "lnd")
                gates(S1, i, b, P, gate[:, b, :])

            def l1_sum(i, b):
                g = at(i, b)
                segment_sum(S1, i, b, bank[:, 0, :])
                dve.wait_ge(*S1["agg"].count(g + 1))
                dve.wait_ge(*S1["tdc"].count(g + 1))
                freed(dve, S1["u"], g)
                nc.vector.tensor_tensor(out=sumT[:], in0=agg[:, b, :], in1=hdT[:, b, :], op=ALU.add)\
                  .then_inc(S1["sum"].sem, 1)

            def l1_rows(i, b):
                scatter_idx(own, S1, i, b, 1, *edge_keys(i, b))
                dve.wait_ge(*S1["z"].count(at(i, b) + 1))
                nc.vector.tensor_tensor(out=row[:, b], in0=tiles(bank[:, 3, :]), in1=keep[:, b], op=ALU.add)\
                  .then_inc(S1["row"].sem, 1)

            def b_stats(i, m):
                q = node(i, m)
                dve.wait_ge(*B["in"][m].count(32 * i + 32))
                ln_stats(own, xn[:, m], statn[:, 0], mvn[:, m % 2, 0], B, "var", "ln", node(i, m))
                freed(dve, B["gb"], q - 3)
                nc.vector.tensor_scalar(ohn[:, m, :], ntb[:, m, :], kind[:, 0:1], None, ALU.is_equal)\
                  .then_inc(B["oh"].sem, 1)

            def b_shift(i, m):
                ln_shift(own, B, "sd", node(i, m), m % 2, 0, mvn, sdn, rsn, nbn, "ln")

            def b_mid(i, m):
                q = node(i, m)
                dve.wait_ge(*B["h"].count(q + 1))
                dve.wait_ge(*B["bu"].count(q + 1))
                freed(dve, B["y"], q - 1)
                own.step(nc.vector.tensor_tensor(out=on[:, m % 2], in0=hn[:, m % 2], in1=tiles(bank[:, 4, :]), op=ALU.add))
                ln_stats(own, on[:, m % 2], statn[:, 1], mvn[:, m % 2, 1], B, "var2", "ln2", node(i, m))

            def b_shift2(i, m):
                ln_shift(own, B, "sd2", node(i, m), m % 2, 1, mvn, sdn, rsn, nbn, "ln2")

            def b_rows(i, m):
                dve.wait_ge(*B["y"].count(node(i, m) + 1))
                dve.wait_ge(*B["gb"].count(node(i, m) + 1))
                if m >= 2:
                    freed(dve, B["out"][m - 2], 32 * i + 32)
                else:
                    freed(dve, B["out"][m + 2], 32 * i)
                affine(own, B, tiles(bank[:, 5, :]), tiles(bank[:, 6, :]), yn[:, m % 2], xn[:, m], xo[:, m % 2], "x3")

            nc.vector.memset(agg[:, 1, :], 0.0).then_inc(weights, 1)
            dve.wait_ge(weights, 3)
            l1_next(0, 0)
            l1_next(0, 1)
            pipeline(dve, HALF, [(None, -2, l1_next),
                                 (0, 2, b_rows), (None, 1, l1_sum), (0, 0, b_stats), (0, 1, b_mid), (None, 0, l1_stats),
                                 (0, 0, b_shift), (0, 1, b_shift2), (None, 0, l1_shift),
                                 (1, 2, b_rows), (1, 0, b_stats), (1, 1, b_mid), (None, 1, l1_rows),
                                 (1, 0, b_shift), (1, 1, b_shift2)], own)
            stage_done(dve, "l1")
            for m in range(4):
                dve.wait_ge(*B["out"][m].count(32 * HALF))

            S2 = L["l2"]

            def l2_next(i, b):
                next_gather(S2, i, b)

            def l2_stats(i, b):
                dve.wait_ge(*S2["src"][b].count(16 * T * (i + 1)))
                ln_stats(own, xs[:, b], stats[:, 0], mv[:, b, 0], S2, "var", "ln", at(i, b))
                dve.wait_ge(*S2["dst"][b].count(16 * T * (i + 1)))
                dve.wait_ge(*S2["var"].count(at(i, b) + 1))
                ln_stats(own, xd[:, b], stats[:, 1], mv[:, b, 1], S2, "vard", "lnd", at(i, b))

            def l2_restarts(i, b):
                g = at(i, b)
                gates(S2, i, b, H, gate[0:H, b, :])
                dve.wait_ge(*S2["gate"].count(g + 1))
                freed(dve, S2["ein"], g - 1)
                nc.vector.tensor_scalar(rst[:, b, :], gate[0:H, b, :], -NEVER, NEVER, ALU.mult, ALU.add)\
                  .then_inc(S2["rst"].sem, 1)

            def l2_shift(i, b):
                ln_shift(own, S2, "sd", at(i, b), b, 0, mv, sd, rs, nb, "ln")
                ln_shift(own, S2, "sdd", at(i, b), b, 1, mv, sd, rs, nb, "lnd")

            def l2_one_hots(i, b):
                g = at(i, b)
                dve.wait_ge(*S2["types"][b].count(48 * (i + 1)))
                freed(dve, S2["ubg"], g - 1)
                nc.vector.tensor_scalar(ohT[:, b].rearrange("p k e -> p (k e)"),
                                        tyb[0:K * K, b].rearrange("p k e -> p (k e)"), kind[:, 0:1], None, ALU.is_equal)\
                  .then_inc(S2["oh"].sem, 1)

            def masks(types_, src, dst_, done):
                for k in range(K):
                    last = nc.vector.scalar_tensor_tensor(out=dst_[:, k, :], in0=types_, scalar=float(k), in1=src,
                                                          op0=ALU.is_equal, op1=ALU.mult)
                last.then_inc(done.sem, 1)

            def l2_mask_src(i, b):
                g = at(i, b)
                dve.wait_ge(*S2["types"][b].count(48 * (i + 1)))
                dve.wait_ge(*S2["s"].count(g + 1))
                freed(dve, S2["v"], g)
                masks(tyb[:, b, 0, :], bank[:, 0, :], sT, S2["ms"])

            def l2_mask_dst(i, b):
                g = at(i, b)
                dve.wait_ge(*S2["d"].count(g + 1))
                freed(dve, S2["q"], g)
                masks(tyb[:, b, 1, :], bank[:, 1, :], dT, S2["md"])

            def l2_mask_k(i, b):
                dve.wait_ge(*S2["k"].count(at(i, b) + 1))
                freed(dve, S2["kr"], at(i, b))
                masks(eb[:, b, :], bank[:, 2, :], km, S2["km"])

            def l2_mask_v(i, b):
                dve.wait_ge(*S2["v"].count(at(i, b) + 1))
                freed(dve, S2["m"], at(i, b))
                masks(eb[:, b, :], bank[:, 3, :], vm, S2["vm"])

            def l2_prod(i, b):
                g = at(i, b)
                dve.wait_ge(*S2["kr"].count(g + 1))
                dve.wait_ge(*S2["qc"].count(g + 1))
                freed(dve, S2["att"], g)
                nc.vector.tensor_tensor(out=prod[:], in0=bank[:, 2, :], in1=qT[:], op=ALU.mult).then_inc(S2["prod"].sem, 1)

            def l2_max(i, b):
                g = at(i, b)
                dve.wait_ge(*S2["att"].count(g + 1))
                dve.wait_ge(*S2["rst"].count(g + 1))
                freed(dve, S2["eo"], g)
                att = bank[0:H, 7, :]
                own.step(nc.vector.tensor_copy(mx[:, b, 0:1], mx[:, 1 - b, G:G + 1]))
                own.step(nc.vector.tensor_tensor_scan(out=mx[:, b, 1:G + 1], data0=rst[:, b, :], data1=att,
                                                      initial=mx[:, b, 0:1], op0=ALU.add, op1=ALU.max))
                nc.vector.tensor_tensor(out=ein[:, 0, :], in0=att, in1=mx[:, b, 1:G + 1], op=ALU.subtract)
                own.step(nc.vector.tensor_tensor(out=ein[:, 1, :], in0=mx[:, b, 0:G], in1=mx[:, b, 1:G + 1],
                                                 op=ALU.subtract))
                nc.vector.tensor_tensor(out=ein[:, 1, :], in0=ein[:, 1, :], in1=rst[:, b, :], op=ALU.add)\
                  .then_inc(S2["ein"].sem, 1)

            def l2_den(i, b):
                g = at(i, b)
                dve.wait_ge(*S2["eo"].count(g + 1))
                freed(dve, S2["dent"], g - 1)
                freed(dve, S2["den"], g)
                nc.vector.tensor_tensor_scan(out=den[:, b, :], data0=eo[:, 1, :], data1=eo[:, 0, :],
                                             initial=den[:, 1 - b, G - 1:G], op0=ALU.mult, op1=ALU.add)\
                  .then_inc(S2["den"].sem, 1)

            def l2_rden(i, b):
                g = at(i, b)
                dve.wait_ge(*S2["dent"].count(g + 1))
                freed(dve, S2["rb"], g)
                own.step(nc.vector.tensor_scalar(rr[:], bank[:, 6, 0:T * H].rearrange("p (t h) -> p t h", t=T),
                                                 1e-16, None, ALU.add))
                nc.vector.reciprocal(rr[:], rr[:]).then_inc(S2["rden"].sem, 1)

            def l2_agg(i, b):
                g = at(i, b)
                dve.wait_ge(*S2["ac"].count(g + 1))
                dve.wait_ge(*S2["m"].count(g + 1))
                freed(dve, S2["agg"], g)
                nc.vector.tensor_tensor(out=vA[:], in0=bank[:, 5, :], in1=aS[:], op=ALU.mult).then_inc(S2["va"].sem, 1)
                dve.wait_ge(*S2["va"].count(g + 1))
                dve.wait_ge(*S2["c"].count(g + 1))
                nc.vector.tensor_tensor_scan(out=agg[:, b, :], data0=bank[:, 1, :], data1=vA[:],
                                             initial=agg[:, 1 - b, G - 1:G], op0=ALU.mult, op1=ALU.add)\
                  .then_inc(S2["agg"].sem, 1)
                dve.wait_ge(*S2["agg"].count(g + 1))
                dve.wait_ge(*S2["r"].count(g + 1))
                freed(dve, S2["g"], g)
                nc.vector.tensor_tensor(out=nrm[:], in0=bank[:, 7, :], in1=agg[:, b, :], op=ALU.mult)\
                  .then_inc(S2["nrm"].sem, 1)

            def l2_mask_upd(i, b):
                dve.wait_ge(*S2["g"].count(at(i, b) + 1))
                freed(dve, S2["u"], at(i, b))
                masks(tyb[:, b, 1, :], gT[:], gm, S2["gm"])

            def l2_sum(i, b):
                g = at(i, b)
                dve.wait_ge(*S2["u"].count(g + 1))
                freed(dve, S2["y"], g)
                own.step(nc.vector.tensor_tensor(out=o2[:], in0=hd[:, b], in1=tiles(bank[:, 6, :]), op=ALU.add))
                ln_stats(own, o2, stats[:, 2], mv[:, b, 2], S2, "var3", "ln3", g)

            def l2_shift3(i, b):
                ln_shift(own, S2, "sd3", at(i, b), b, 2, mv, sd, rs, nb, "ln3")
                scatter_idx(own, S2, i, b, 2, *edge_keys(i, b))

            def l2_rows(i, b):
                g = at(i, b)
                dve.wait_ge(*S2["y"].count(g + 1))
                dve.wait_ge(*S2["ubg"].count(g + 1))
                affine(own, S2, tiles(bank[:, 4, :]), tiles(bank[:, 3, :]), y2[:], keep[:, b], row[:, b], "row")

            own = Own(dve, own_dve["l2"])
            nc.vector.memset(agg[:, 1, :], 0.0)
            nc.vector.memset(mx[:, 1, :], 0.0)
            nc.vector.memset(den[:, 1, :], 0.0).then_inc(weights, 1)
            dve.wait_ge(weights, 4)
            l2_next(0, 0)
            l2_next(0, 1)
            pipeline(dve, HALF, [(None, lag, work) for lag, work in (
                (-2, l2_next), (1, l2_mask_src), (2, l2_max), (1, l2_mask_dst), (1, l2_mask_k), (2, l2_den),
                (1, l2_mask_v), (2, l2_rden), (2, l2_agg), (0, l2_stats), (2, l2_mask_upd), (1, l2_prod),
                (0, l2_restarts), (2, l2_sum), (0, l2_shift), (2, l2_shift3), (0, l2_one_hots), (2, l2_rows))], own)
            stage_done(dve, "l2", 2)

            S3 = L["l3"]

            def l3_next(i, b):
                g = at(i, b)
                dve.wait_ge(*S3["rec"][b].count(48 * i + 48))
                freed(dve, S3["src"][b], 16 * T * i)
                freed(dve, S3["dst"][b], 16 * T * i)
                nc.vector.tensor_copy(gidx[:, b, 0:4], edge_rec[:, b, :, 3])
                nc.vector.tensor_copy(gidx[:, b, 4:8], edge_rec[:, b, :, 2]).then_inc(S3["gidx"].sem, 1)
                key = edge_rec[:, b, :, 2]
                own.step(nc.vector.tensor_tensor(out=same[:, b, :], in0=key, in1=edge_rec[:, b, :, 4], op=ALU.is_equal))
                nc.vector.scalar_tensor_tensor(out=place3[:, b, :], in0=same[:, b, :], scalar=float(FAR),
                                               in1=key, op0=ALU.mult, op1=ALU.add)
                freed(dve, S3["gate"], g - 1)
                nc.vector.tensor_tensor(out=gcol[:, b, :], in0=key, in1=edge_rec[:, b, :, 0], op=ALU.is_equal)\
                  .then_inc(S3["gcol"].sem, 1)

            def l3_places(i, b):
                freed(dve, S3["scat"][b], 16 * T * i)
                own.step(nc.vector.tensor_copy(sidx[:, b, :], place3[:, b, :]))

            def l3_stats(i, b):
                g = at(i, b)
                dve.wait_ge(*S3["src"][b].count(16 * T * (i + 1)))
                ln_stats(own, xs[:, b], stats[:, 0], mv[:, b, 0], S3, "var", "ln", g)
                dve.wait_ge(*S3["dst"][b].count(16 * T * (i + 1)))
                dve.wait_ge(*S3["var"].count(g + 1))
                ln_stats(own, xd[:, b], stats[:, 1], mv[:, b, 1], S3, "vard", "lnd", g)

            def l3_shift(i, b):
                ln_shift(own, S3, "sd", at(i, b), b, 0, mv, sd, rs, nb, "ln")
                ln_shift(own, S3, "sdd", at(i, b), b, 1, mv, sd, rs, nb, "lnd")

            def l3_clip(i, b):
                dve.wait_ge(*S3["scc"].count(at(i, b) + 1))
                own.step(nc.vector.scalar_tensor_tensor(out=sc3[:], in0=sc3[:], scalar=0.2, in1=sc3[:],
                                                        op0=ALU.mult, op1=ALU.max))
                nc.vector.tensor_scalar(sc3[:], sc3[:], -2.0, 2.0, ALU.max, ALU.min).then_inc(S3["clip"].sem, 1)

            def l3_sums(i, b):
                g = at(i, b)
                dve.wait_ge(*S3["ex"].count(g + 1))
                dve.wait_ge(*S3["t"].count(g + 1))
                own.step(nc.vector.tensor_tensor(out=hE[:], in0=bank[:, 6 * b, :], in1=ex[:, b, :], op=ALU.mult))
                dve.wait_ge(*S3["gate"].count(g + 1))
                freed(dve, S3["z"], g - 1)
                freed(dve, S3["agg"], g)
                nc.vector.tensor_tensor_scan(out=agg[:, b, :], data0=bank[:, 3, :], data1=hE[:],
                                             initial=agg[:, 1 - b, G - 1:G], op0=ALU.mult, op1=ALU.add)
                nc.vector.tensor_tensor_scan(out=den3[:, b, :], data0=bank[0:1, 3, :], data1=ex[0:1, b, :],
                                             initial=den3[:, 1 - b, G - 1:G], op0=ALU.mult, op1=ALU.add)\
                  .then_inc(S3["agg"].sem, 1)

            def l3_rows(i, b):
                dve.wait_ge(*S3["z"].count(at(i, b) + 1))
                own.step(nc.vector.tensor_scalar(rd3[:], bank[:, 5, 0:T], 1e-9, None, ALU.add))
                own.step(nc.vector.reciprocal(rd3[:], rd3[:]))
                for t in range(T):
                    last = nc.vector.scalar_tensor_tensor(out=row[:, b, t, :], in0=bank[:, 4, t * P:(t + 1) * P],
                                                          scalar=rd3[:, t:t + 1], in1=keep[:, b, t, :],
                                                          op0=ALU.mult, op1=ALU.add)
                last.then_inc(S3["row"].sem, 1)

            own = Own(dve, own_dve["l3"])
            nc.vector.memset(agg[:, 1, :], 0.0)
            nc.vector.memset(den3[:, 1, :], 0.0).then_inc(weights, 1)
            dve.wait_ge(weights, 5)
            l3_next(0, 0)
            pipeline(dve, HALF, [(None, lag, work) for lag, work in (
                (2, l3_rows), (1, l3_places), (-1, l3_next), (0, l3_stats), (1, l3_clip), (0, l3_shift), (1, l3_sums))], own)

        @block.scalar
        def _(act):
            def std(S, var_ready, g, m, s_, ready):
                act.wait_ge(*S[var_ready].count(g + 1))
                nc.scalar.activation(s_, m[:, :, 1], ACT.Sqrt, bias=epsc[:, 0:1]).then_inc(S[ready].sem, 1)

            def normed(S, ln_ready, g, dst, src, r_, n_, func, ready):
                act.wait_ge(*S[ln_ready].count(g + 1))
                for t in range(T):
                    last = nc.scalar.activation(dst[:, t, :], src[:, t, :], func, bias=n_[:, t:t + 1], scale=r_[:, t:t + 1])
                last.then_inc(S[ready].sem, 1)

            def copy(S, wanted, g, dst, src, ready, func=ACT.Copy, **kw):
                act.wait_ge(*S[wanted].count(g + 1))
                nc.scalar.activation(dst, src, func, **kw).then_inc(S[ready].sem, 1)

            act.wait_ge(w_in, N_IN)
            act.wait_ge(consts, N_CONST)

            def store_p(i, b):
                act.wait_ge(p_sum, at(i, b) + 1)
                act.dma_start(rows(x1, at(i, b)), yn[:, b]).then_inc(p_out[b], 16)

            def place_turned(i, m):
                t = node(i, m)
                act.wait_ge(R["olt"], t + 1)
                freed(act, R["look"], t - 1)
                nc.scalar.activation(OLT[:, m % 2, :], bank[:, 3, 0:P], ACT.Copy).then_inc(R["oltc"], 1)
            pipeline(act, NT // 4, [(0, 0, place_turned), (1, 0, place_turned), (None, 0, store_p)])

            def keep_rows(l):
                S = L[l]

                def work(i, b):
                    act.wait_ge(*S["dst"][b].count(16 * T * (i + 1)))
                    freed(act, S["row"], at(i, b) - 1)
                    nc.scalar.activation(keep[:, b], xd[:, b], ACT.Copy).then_inc(S["keep"].sem, 1)
                return work

            def a_norm(i, m):
                q = node(i, m)
                std(A, "var", q, mvn[:, m % 2, 0], sdn[:, m % 2, 0, :], "sd")
                freed(act, A["t"], q - 1)
                normed(A, "ln", q, hn[:, m % 2], yn[:, m % 2], rsn[:, m % 2, 0], nbn[:, m % 2, 0], ACT.Relu, "h")

            def a_turned(i, m):
                freed(act, A["z"], node(i, m) - 1)
                copy(A, "t", node(i, m), hnT[:, m % 2, :], bank[:, 0, :], "tc")

            def a_hidden(i, m):
                freed(act, A["z"], node(i, m))
                copy(A, "u", node(i, m), unT[:], bank[:, 1, :], "uc", ACT.Relu, bias=b1c[:, 0:1])

            def a_store(i, m):
                act.wait_ge(*A["x2"].count(node(i, m) + 1))
                for target in (x2, x2n):
                    act.dma_start(rows(target, node(i, m)), on[:, m % 2]).then_inc(A["out"][m].sem, 16)

            def l0_norm(i, b):
                S, g = L["l0"], at(i, b)
                std(S, "var", g, mv[:, b, 0], sd[:, b, 0, :], "sd")
                freed(act, S["t"], g - 1)
                normed(S, "ln", g, hs[:, b], xs[:, b], rs[:, b, 0], nb[:, b, 0], ACT.Relu, "h")
            pipeline(act, HALF, [(0, 2, a_store), (0, 0, a_norm), (0, 1, a_hidden), (None, 0, l0_norm), (0, 0, a_turned),
                                 (1, 2, a_store), (1, 0, a_norm), (1, 1, a_hidden), (None, 0, keep_rows("l0")),
                                 (1, 0, a_turned)])
            stage_done(act, "l0")
            for m in range(4):
                act.wait_ge(*A["out"][m].count(32 * HALF))

            def b_norm(i, m):
                q = node(i, m)
                std(B, "var", q, mvn[:, m % 2, 0], sdn[:, m % 2, 0, :], "sd")
                freed(act, B["var2"], q - 1)
                normed(B, "ln", q, hn[:, m % 2], xn[:, m], rsn[:, m % 2, 0], nbn[:, m % 2, 0], ACT.Relu, "h")

            def b_norm2(i, m):
                q = node(i, m)
                std(B, "var2", q, mvn[:, m % 2, 1], sdn[:, m % 2, 1, :], "sd2")
                freed(act, B["x3"], q - 1)
                normed(B, "ln2", q, yn[:, m % 2], on[:, m % 2], rsn[:, m % 2, 1], nbn[:, m % 2, 1], ACT.Identity, "y")

            def b_store(i, m):
                act.wait_ge(*B["x3"].count(node(i, m) + 1))
                for target in (x3, out):
                    act.dma_start(rows(target, node(i, m)), xo[:, m % 2]).then_inc(B["out"][m].sem, 16)

            def l1_norm(i, b):
                S, g = L["l1"], at(i, b)
                std(S, "var", g, mv[:, b, 0], sd[:, b, 0, :], "sd")
                std(S, "vard", g, mv[:, b, 1], sd[:, b, 1, :], "sdd")
                freed(act, S["t"], g - 1)
                normed(S, "ln", g, hs[:, b], xs[:, b], rs[:, b, 0], nb[:, b, 0], ACT.Relu, "h")
                freed(act, S["td"], g - 1)
                normed(S, "lnd", g, hd[:, b], xd[:, b], rs[:, b, 1], nb[:, b, 1], ACT.Relu, "hd")

            def l1_turned(i, b):
                freed(act, L["l1"]["z"], at(i, b) - 1)
                copy(L["l1"], "td", at(i, b), hdT[:, b, :], bank[:, 1, :], "tdc")

            def l1_hidden(i, b):
                freed(act, L["l1"]["z"], at(i, b))
                copy(L["l1"], "u", at(i, b), uT[:], bank[:, 2, :], "uc", ACT.Relu, bias=b1c[:, 0:1])
            pipeline(act, HALF, [(0, 3, b_store), (None, 1, l1_hidden), (0, 0, b_norm), (0, 1, b_norm2), (None, 0, l1_norm),
                                 (None, 0, keep_rows("l1")), (None, 0, l1_turned),
                                 (1, 3, b_store), (1, 0, b_norm), (1, 1, b_norm2)])
            stage_done(act, "l1")
            for m in range(4):
                act.wait_ge(*B["out"][m].count(32 * HALF))

            S2 = L["l2"]

            def l2_exp(i, b):
                freed(act, S2["c"], at(i, b))
                freed(act, S2["den"], at(i, b))
                copy(S2, "ein", at(i, b), eo[:], ein[:], "eo", ACT.Exp)

            def l2_weights(i, b):
                freed(act, S2["va"], at(i, b))
                copy(S2, "a", at(i, b), aS[:], bank[:, 0, :], "ac")

            def l2_spread_rden(i, b):
                freed(act, S2["r"], at(i, b))
                copy(S2, "rden", at(i, b), rb[:], rr[:, :, :].unsqueeze(3).to_broadcast([P, T, H, DK]), "rb")

            def l2_query(i, b):
                freed(act, S2["prod"], at(i, b))
                copy(S2, "q", at(i, b), qT[:], bank[:, 4, :], "qc")

            def l2_gelu(i, b):
                freed(act, S2["gm"], at(i, b))
                copy(S2, "nrm", at(i, b), gT[:], nrm[:], "g", ACT.Gelu)

            def l2_std(i, b):
                std(S2, "var", at(i, b), mv[:, b, 0], sd[:, b, 0, :], "sd")
                std(S2, "vard", at(i, b), mv[:, b, 1], sd[:, b, 1, :], "sdd")

            def l2_norm(i, b):
                g = at(i, b)
                freed(act, S2["s"], g - 1)
                normed(S2, "ln", g, hs[:, b], xs[:, b], rs[:, b, 0], nb[:, b, 0], ACT.Relu, "h")
                freed(act, S2["d"], g - 1)
                freed(act, S2["var3"], g - 1)
                normed(S2, "lnd", g, hd[:, b], xd[:, b], rs[:, b, 1], nb[:, b, 1], ACT.Relu, "hd")

            def l2_std3(i, b):
                std(S2, "var3", at(i, b), mv[:, b, 2], sd[:, b, 2, :], "sd3")

            def l2_norm3(i, b):
                freed(act, S2["row"], at(i, b))
                normed(S2, "ln3", at(i, b), y2, o2, rs[:, b, 2], nb[:, b, 2], ACT.Identity, "y")
            pipeline(act, HALF, [(None, lag, work) for lag, work in (
                (2, l2_exp), (2, l2_weights), (2, l2_spread_rden), (1, l2_query), (2, l2_gelu), (0, l2_std), (2, l2_std3), (0, l2_norm),
                (2, l2_norm3), (0, keep_rows("l2")))])
            stage_done(act, "l2", 2)

            S3 = L["l3"]

            def l3_std(i, b):
                std(S3, "var", at(i, b), mv[:, b, 0], sd[:, b, 0, :], "sd")
                std(S3, "vard", at(i, b), mv[:, b, 1], sd[:, b, 1, :], "sdd")

            def l3_norm(i, b):
                g = at(i, b)
                freed(act, S3["t"], g - 1)
                normed(S3, "ln", g, hs[:, b], xs[:, b], rs[:, b, 0], nb[:, b, 0], ACT.Relu, "h")
                freed(act, S3["td"], g - 1)
                normed(S3, "lnd", g, hd[:, b], xd[:, b], rs[:, b, 1], nb[:, b, 1], ACT.Relu, "hd")

            def l3_turned(i, b):
                freed(act, S3["sco"], at(i, b))
                copy(S3, "t", at(i, b), uT[:], bank[:, 6 * b, :], "he")
                copy(S3, "td", at(i, b), hdT[:, b, :], bank[:, 1, :], "tdc")

            def l3_scores(i, b):
                freed(act, S3["ex"], at(i, b))
                copy(S3, "sco", at(i, b), sc3[:], bank[:, 2, :], "scc")

            def l3_exp(i, b):
                freed(act, S3["agg"], at(i, b) - 1)
                copy(S3, "clip", at(i, b), ex[:, b, :], sc3[:], "ex", ACT.Exp)
            pipeline(act, HALF, [(None, lag, work) for lag, work in (
                (0, l3_std), (1, l3_exp), (0, l3_norm), (0, keep_rows("l3")), (0, l3_turned), (0, l3_scores))])

        @block.tensor
        def _(pe):
            def transposes(dst, src, ready):
                for t in range(T):
                    last = nc.tensor.transpose(dst[:, t * P:(t + 1) * P], src[:, t, :], ident[:])
                last.then_inc(ready.sem, 1)

            def project(dst, terms, bias, ready):
                for t in range(T):
                    c = slice(t * P, (t + 1) * P)
                    for n, (colsT, W) in enumerate(terms):
                        last = nc.tensor.matmul(dst[:, c], colsT[:, c], W[:], start=(n == 0),
                                                stop=(bias is None and n == len(terms) - 1))
                    if bias is not None:
                        last = nc.tensor.matmul(dst[:, c], ones1[:], bias[:], start=False, stop=True)
                last.then_inc(ready.sem, 1)

            pe.wait_ge(w_in, N_IN)
            pe.wait_ge(consts, N_CONST)
            nc.tensor.matmul(bank[:, 0, 0:K], headT[:], pri[:], start=True, stop=True).then_inc(prep["pri"], 1)
            nc.tensor.transpose(bank[:, 1, 0:P], W3[:], ident[:]).then_inc(prep["t"], 1)
            pe.wait_ge(prep["copy"], 1)
            nc.tensor.matmul(bank[:, 2, 0:2], W3T[:], ka[:], start=True, stop=True).then_inc(prep["wsc"], 1)
            pe.wait_ge(weights, 1)

            def count(i, b):
                t = at(i, b)
                pe.wait_ge(R["one"], t + 1)
                nc.tensor.matmul(bank[:, 5, 0:NHI], OL[:, b, :], OH[:, b, :], start=isinstance(t, int) and t == 0,
                                 stop=isinstance(t, int) and t == NT - 1).then_inc(R["hist"], 1)
            pipeline(pe, NT // 2, [(None, 0, count)])
            pe.wait_ge(R["rowsum"], 1)
            nc.tensor.matmul(bank[:, 6, 0:1], above[:], offs[:], start=True, stop=True).then_inc(R["offs"], 1)

            def place_tile(i, m):
                t = node(i, m)
                pe.wait_ge(R["one"], t + 1 + NT)
                freed(pe, R["oltc"], t)
                nc.tensor.transpose(bank[:, 3, 0:P], OL[:, m % 2, :], ident[:]).then_inc(R["olt"], 1)
                freed(pe, R["tab"], t)
                nc.tensor.matmul(bank[:, 4 + m % 2, 0:NHI], OL[:, m % 2, :], OH[:, m % 2, :], start=True, stop=True)\
                  .then_inc(R["tile"], 1)

            def place_look(i, m):
                t = node(i, m)
                pe.wait_ge(R["oltc"], t + 1)
                pe.wait_ge(R["tab"], t + 1)
                freed(pe, R["pos"], t - 1)
                nc.tensor.matmul(bank[:, 6 + m % 2, 0:NHI], OLT[:, m % 2, :], table[:], start=True, stop=True)\
                  .then_inc(R["look"], 1)
            pipeline(pe, NT // 4, [(c, lag, work) for c in range(2) for lag, work in ((0, place_tile), (1, place_look))])
            pe.wait_ge(R["tycol"], NT)
            for c in range(TYC // P):
                last = nc.tensor.transpose(bank[:, 0, c * P:(c + 1) * P], tycol[:, c * P:(c + 1) * P], ident[:])
            last.then_inc(R["tyturn"], 1)
            pe.wait_ge(R["tyrow"], 1)

            def a_turn(i, m):
                pe.wait_ge(*A["h"].count(node(i, m) + 1))
                freed(pe, A["tc"], node(i, m))
                transposes(bank[:, 0, :], hn[:, m % 2], A["t"])

            def a_hidden(i, m):
                pe.wait_ge(*A["tc"].count(node(i, m) + 1))
                freed(pe, A["uc"], node(i, m))
                nc.tensor.matmul(bank[:, 1, :], W1[:], hnT[:, m % 2, :], start=True, stop=True).then_inc(A["u"].sem, 1)

            def a_rows(i, m):
                pe.wait_ge(*A["uc"].count(node(i, m) + 1))
                freed(pe, A["x2"], node(i, m))
                project(bank[:, 2, :], [(unT, W2), (hnT[:, m % 2, :], Wr)], b2r, A["z"])

            def l0_turn(i, b):
                pe.wait_ge(*L["l0"]["h"].count(at(i, b) + 1))
                freed(pe, L["l0"]["agg"], at(i, b))
                transposes(bank[:, 3, :], hs[:, b], L["l0"]["t"])

            def l0_rows(i, b):
                pe.wait_ge(*L["l0"]["agg"].count(at(i, b) + 1))
                freed(pe, L["l0"]["row"], at(i, b))
                project(bank[:, 4, :], [(agg[:, b, :], W0)], b0r, L["l0"]["z"])
            pipeline(pe, HALF, [(0, 1, a_hidden), (0, 0, a_turn), (0, 1, a_rows), (None, 1, l0_rows),
                                (None, 0, l0_turn), (1, 1, a_hidden), (1, 0, a_turn), (1, 1, a_rows)])
            stage_done(pe, "l0")
            for m in range(4):
                pe.wait_ge(*A["out"][m].count(32 * HALF))

            def type_rows(n, oh, which):
                for t in range(T):
                    last = nc.tensor.matmul(bank[:, n, t * P:(t + 1) * P], oh[:, t * P:(t + 1) * P], tparts[:, 3 + which, :],
                                            start=True, stop=True)
                return last

            def b_bias(i, m):
                pe.wait_ge(*B["oh"].count(node(i, m) + 1))
                freed(pe, B["var2"], node(i, m))
                type_rows(4, ohn[:, m, :], 0).then_inc(B["bu"].sem, 1)

            def b_affine(i, m):
                freed(pe, B["x3"], node(i, m))
                type_rows(5, ohn[:, m, :], 1)
                type_rows(6, ohn[:, m, :], 2).then_inc(B["gb"].sem, 1)

            def l1_turn(i, b):
                S, g = L["l1"], at(i, b)
                pe.wait_ge(*S["h"].count(g + 1))
                freed(pe, S["agg"], g)
                transposes(bank[:, 0, :], hs[:, b], S["t"])
                pe.wait_ge(*S["hd"].count(g + 1))
                freed(pe, S["tdc"], g)
                transposes(bank[:, 1, :], hd[:, b], S["td"])

            def l1_hidden(i, b):
                S, g = L["l1"], at(i, b)
                pe.wait_ge(*S["sum"].count(g + 1))
                freed(pe, S["uc"], g)
                nc.tensor.matmul(bank[:, 2, :], W1[:], sumT[:], start=True, stop=True).then_inc(S["u"].sem, 1)

            def l1_rows(i, b):
                S, g = L["l1"], at(i, b)
                pe.wait_ge(*S["uc"].count(g + 1))
                freed(pe, S["row"], g)
                project(bank[:, 3, :], [(uT, W2), (hdT[:, b, :], Wr)], b2r, S["z"])
            pipeline(pe, HALF, [(0, 1, b_affine), (None, 1, l1_hidden), (0, 0, b_bias), (None, 1, l1_rows),
                                (None, 0, l1_turn), (1, 1, b_affine), (1, 0, b_bias)])
            stage_done(pe, "l1")
            for m in range(4):
                pe.wait_ge(*B["out"][m].count(32 * HALF))

            S2 = L["l2"]

            def typed(n, W, which, cols, oh, ready):
                for k in range(K):
                    nc.tensor.matmul(bank[:, n, :], W[:, k, :], cols[:, k, :], start=(k == 0), stop=False)
                nc.tensor.matmul(bank[:, n, :], tparts[:, which, :], oh, start=False, stop=True).then_inc(ready.sem, 1)

            def related(n, W, cols, ready):
                for r in range(K):
                    last = nc.tensor.matmul(bank[:, n, :], W[:, r, :], cols[:, r, :], start=(r == 0), stop=(r == K - 1))
                last.then_inc(ready.sem, 1)

            def l2_turn(i, b):
                g = at(i, b)
                pe.wait_ge(*S2["h"].count(g + 1))
                freed(pe, S2["ac"], g - 1)
                transposes(bank[:, 0, :], hs[:, b], S2["s"])
                pe.wait_ge(*S2["hd"].count(g + 1))
                freed(pe, S2["agg"], g - 1)
                transposes(bank[:, 1, :], hd[:, b], S2["d"])

            def l2_key(i, b):
                g = at(i, b)
                pe.wait_ge(*S2["ms"].count(g + 1))
                pe.wait_ge(*S2["oh"].count(g + 1))
                freed(pe, S2["prod"], g)
                typed(2, Wk, 1, sT, ohT[:, b, 0, :], S2["k"])

            def l2_value(i, b):
                freed(pe, S2["row"], at(i, b) - 1)
                typed(3, Wv, 2, sT, ohT[:, b, 0, :], S2["v"])

            def l2_query(i, b):
                pe.wait_ge(*S2["md"].count(at(i, b) + 1))
                typed(4, Wq, 0, dT, ohT[:, b, 1, :], S2["q"])

            def l2_relate(i, b):
                g = at(i, b)
                pe.wait_ge(*S2["km"].count(g + 1))
                related(2, Ra, km, S2["kr"])
                pe.wait_ge(*S2["vm"].count(g + 1))
                freed(pe, S2["va"], g)
                related(5, Rm, vm, S2["m"])

            def l2_att(i, b):
                g = at(i, b)
                pe.wait_ge(*S2["prod"].count(g + 1))
                freed(pe, S2["nrm"], g)
                nc.tensor.matmul(bank[0:H, 7, :], head[:], prod[:], start=True, stop=True).then_inc(S2["att"].sem, 1)

            def l2_spread(i, b):
                g = at(i, b)
                pe.wait_ge(*S2["eo"].count(g + 1))
                used(pe, S2["ms"], g + 2, NGE)
                nc.tensor.matmul(bank[:, 0, :], headT[:], eo[:, 0, :], start=True, stop=True).then_inc(S2["a"].sem, 1)
                used(pe, S2["md"], g + 2, NGE)
                nc.tensor.matmul(bank[:, 1, :], headT[:], eo[:, 1, :], start=True, stop=True).then_inc(S2["c"].sem, 1)
                pe.wait_ge(*S2["den"].count(g + 1))
                freed(pe, S2["var3"], g)
                pe.sem_inc(pe_turn, 1)
                for t in range(T):
                    last = nc.tensor.matmul(bank[:, 6, t * H:(t + 1) * H], den[:, b, t * P:(t + 1) * P], ident[0:H, 0:H],
                                            start=True, stop=True)
                last.then_inc(S2["dent"].sem, 1)

            def l2_rden(i, b):
                pe.wait_ge(*S2["rb"].count(at(i, b) + 1))
                for t in range(T):
                    last = nc.tensor.transpose(bank[:, 7, t * P:(t + 1) * P], rb[:, t].rearrange("p h d -> p (h d)"),
                                               ident[:])
                last.then_inc(S2["r"].sem, 1)

            def l2_update(i, b):
                g = at(i, b)
                used(pe, S2["vm"], g + 2, NGE)
                used(pe, S2["qc"], g + 2, NGE)
                type_rows(4, ohT[:, b, 1, :], 1)
                type_rows(3, ohT[:, b, 1, :], 2).then_inc(S2["ubg"].sem, 1)
                pe.wait_ge(*S2["gm"].count(g + 1))
                for t in range(T):
                    c = slice(t * P, (t + 1) * P)
                    for k in range(K):
                        nc.tensor.matmul(bank[:, 6, c], gm[:, k, c], Wu[:, k, :], start=(k == 0), stop=False)
                    last = nc.tensor.matmul(bank[:, 6, c], ohT[:, b, 1, c], tparts[:, 3, :], start=False, stop=True)
                last.then_inc(S2["u"].sem, 1)
            pipeline(pe, HALF, [(None, lag, work) for lag, work in (
                (2, l2_att), (1, l2_key), (1, l2_value), (2, l2_spread), (1, l2_query), (2, l2_rden), (1, l2_relate),
                (2, l2_update), (0, l2_turn))])
            stage_done(pe, "l2", 2)

            S3 = L["l3"]

            def l3_turn(i, b):
                g = at(i, b)
                pe.wait_ge(*S3["h"].count(g + 1))
                freed(pe, S3["agg"], g - 1)
                transposes(bank[:, 6 * b, :], hs[:, b], S3["t"])
                pe.wait_ge(*S3["hd"].count(g + 1))
                freed(pe, S3["tdc"], g)
                transposes(bank[:, 1, :], hd[:, b], S3["td"])

            def l3_scores(i, b):
                g = at(i, b)
                pe.wait_ge(*S3["he"].count(g + 1))
                pe.wait_ge(*S3["tdc"].count(g + 1))
                freed(pe, S3["scc"], g)
                nc.tensor.matmul(bank[:, 2, :], wtx[:], hdT[:, b, :], start=True, stop=False)
                nc.tensor.matmul(bank[:, 2, :], wsx[:], uT[:], start=False, stop=True).then_inc(S3["sco"].sem, 1)

            def l3_gate(i, b):
                g = at(i, b)
                pe.wait_ge(*S3["gcol"].count(g + 1))
                freed(pe, S3["agg"], g)
                for t in range(T):
                    last = nc.tensor.transpose(bank[:, 3, t * P:(t + 1) * P], gcol[:, b, t:t + 1].to_broadcast([P, P]),
                                               ident[:])
                last.then_inc(S3["gate"].sem, 1)

            def l3_rows(i, b):
                g = at(i, b)
                pe.wait_ge(*S3["agg"].count(g + 1))
                freed(pe, S3["row"], g)
                pe.sem_inc(pe_turn, 1)
                for t in range(T):
                    nc.tensor.matmul(bank[:, 5, t:t + 1], den3[0:1, b, t * P:(t + 1) * P], ones1[0:1, 0:1],
                                     start=True, stop=True)
                project(bank[:, 4, :], [(agg[:, b, :], W3)], None, S3["z"])
            pipeline(pe, HALF, [(None, lag, work) for lag, work in (
                (0, l3_turn), (0, l3_scores), (1, l3_rows), (0, l3_gate))])


def kernel(**inputs):
    import numpy as np
    import concourse.bacc as bacc
    from concourse.bass_utils import run_bass_kernel_spmd as run

    x, src, dst = (np.asarray(inputs[n]) for n in ("x", "src", "dst"))
    N, E = x.shape[0], src.shape[0]
    EP = 2 * G * max(-(-E // (2 * G)), -(-(N + 1) // (4 * G)))
    NP = 2 * EP

    def pad(a, n, value):
        return np.concatenate([a, np.full((n - len(a),) + a.shape[1:], value, a.dtype)])

    srcp, dstp = pad(src, EP, NP - 1), pad(dst, EP, NP - 1)
    etype = pad(np.asarray(inputs["edge_type_3"]), EP, 0)
    ntype = pad(np.asarray(inputs["node_type_3"]), NP, 0)
    end = np.full(1, -1, dst.dtype)
    following = np.concatenate([dstp[1:], end])

    def columns(a):
        return a.reshape(EP // P, P).T

    eidx = np.stack([a.reshape(EP // G, T, P).transpose(2, 0, 1) for a in (srcp, dstp, following)], axis=2).reshape(P, -1)
    feed = {"x": pad(x, NP, 0), "eidx": eidx, "keys": np.concatenate([end, dstp]), "skeys": srcp, "scol": columns(srcp),
            "dcol": columns(dstp), "etype": etype, "ntype": ntype.reshape(NP, 1)}
    names = [n for n in inputs if n[0] == "L"]
    feed.update({n: np.asarray(inputs[n]) for n in names})
    feed["L2_gnn_rel_pri"] = feed["L2_gnn_rel_pri"].T
    feed["L3_gnn_kernel_attention"] = feed["L3_gnn_kernel_attention"].reshape(2, D).T
    feed = {k: np.ascontiguousarray(v) for k, v in feed.items()}

    nc = bacc.Bacc("TRN2", target_bir_lowering=False, num_devices=1)
    ap = {k: nc.dram_tensor("in_" + k, v.shape, mybir.dt.from_np(v.dtype), kind="ExternalInput").ap() for k, v in feed.items()}
    scratch = {n: nc.dram_tensor("mem_" + n, (NP, D), F32, kind="Internal").ap() for n in ("x1", "x2", "x2n", "x3")}
    scratch["edge_kinds"] = nc.dram_tensor("mem_edge_kinds", (2 * EP // P, P), F32, kind="Internal").ap()
    scratch["rec"] = nc.dram_tensor("mem_rec", (EP + 2, 2), I32, kind="Internal").ap()
    out = nc.dram_tensor("out_x", (NP, D), F32, kind="ExternalOutput").ap()
    gnn(nc, NP, EP, (ap["scol"], ap["dcol"]), ap["x"], ap["eidx"], ap["keys"], ap["skeys"], ap["etype"], ap["ntype"],
        {n: ap[n] for n in names}, scratch, out)
    r = run(nc, [{"in_" + k: v for k, v in feed.items()}], core_ids=[0])
    return r.results[0]["out_x"][:N]
```

```python
import concourse.bass as bass
from concourse import mybir
from concourse.alu_op_type import AluOpType as ALU
from contextlib import ExitStack

F32 = mybir.dt.float32
I32 = mybir.dt.int32
BF16 = mybir.dt.bfloat16
ACT = mybir.ActivationFunctionType

P = 128
D = 128
T = 4
G = P * T
H = 8
DK = D // H
K = 3
EPS = 1e-5
FAR = 1 << 17
NEVER = -1e30


class Signal:

    def __init__(self, sem, past=0):
        self.sem, self.past = sem, past

    def count(self, value):
        return self.sem, self.past + value


class Own:

    def __init__(self, eng, sem):
        self.eng, self.sem, self.n, self.loop = eng, sem, 0, 0

    def step(self, ins):
        ins.then_inc(self.sem, 1)
        self.n += 1
        self.eng.wait_ge(self.sem, self.loop + self.n)


def freed(eng, sem, value):
    if isinstance(sem, Signal):
        sem, value = sem.count(value)
    if not isinstance(value, int) or value > 0:
        eng.wait_ge(sem, value)


def used(eng, sig, value, last):
    eng.wait_ge(*sig.count(min(value, last) if isinstance(value, int) else value))


def turns(eng, n, body, own=None):
    for i in range(3):
        before = own.n if own else 0
        body(i)
    steps = own.n - before if own else 0
    with eng.Fori(3, n - 1) as i:
        if own:
            own.loop = (i - 3) * steps
        body(i)
        if own:
            own.loop, own.n = 0, own.n - steps
    if own:
        own.n += (n - 4) * steps
    for i in range(n - 1, n + 2):
        body(i)


def pipeline(eng, n, parts, own=None):
    def turn(i):
        for b in range(2):
            for c, lag, work in parts:
                size = 2 if c is None else 4
                k = (b if c is None else 2 * b + c) - lag
                at_i, at_b = i + k // size, k % size
                if not isinstance(i, int) or 0 <= at_i < n:
                    work(at_i, at_b)
    turns(eng, n, turn, own)


def gnn(nc, NP, EP, edge_ends, x, eidx, keys, skeys, etypes, ntype, w, scratch, out):
    NGN, NGE = NP // G, EP // G
    NT = EP // P
    NHI = max(NP // P, P)
    HALF = NGE // 2
    assert NGN == 2 * NGE
    x1, x2, x2n, x3, rec = (scratch[n] for n in ("x1", "x2", "x2n", "x3", "rec"))
    edge_kinds = scratch["edge_kinds"]
    ctx = ExitStack()
    with ctx:
        def sb(name, shape, dt=F32):
            return ctx.enter_context(nc.sbuf_tensor(name, shape, dt))

        def sem(name):
            return ctx.enter_context(nc.semaphore(name))

        def pair(name):
            return [sem(name + "_0"), sem(name + "_1")]

        ident = sb("ident", [P, P])
        ones1 = sb("ones1", [1, P]); identb = sb("identb", [P, P], BF16)
        epsc = sb("epsc", [P, 1])
        kind = sb("kind", [K * K, 1])
        third = sb("third", [K * K, 3])
        rowno = sb("rowno", [P, 1], I32); rownof = sb("rownof", [P, 1])
        head = sb("head", [P, H]); headT = sb("headT", [H, P])
        W0 = sb("W0", [P, D]); W1 = sb("W1", [P, D]); W2 = sb("W2", [P, D]); Wr = sb("Wr", [P, D])
        b1c = sb("b1c", [P, 1])
        rowb = sb("rowb", [K, 3, D])
        rowr = sb("rowr", [K, 3, D]); rowp = sb("rowp", [K, 3, D], BF16); rowparts = sb("rowparts", [K, 3, D], BF16)
        rowsel = sb("rowsel", [K, 3]); onesb = sb("onesb", [K, P], BF16)
        b0x = sb("b0x", [P, D])
        Wq = sb("Wq", [P, K, D]); Wk = sb("Wk", [P, K, D]); Wv = sb("Wv", [P, K, D]); Wu = sb("Wu", [P, K, D])
        tb = sb("tb", [K * K, 6, D]); tbr = sb("tbr", [K * K, 6, D])
        tbp = sb("tbp", [K * K, 6, D], BF16); tparts = sb("tparts", [K * K, 6, D], BF16)
        Ra = sb("Ra", [P, K, D]); Rm = sb("Rm", [P, K, D])
        pri = sb("pri", [H, K]); pric = sb("pric", [P, K])
        W3 = sb("W3", [P, D]); W3T = sb("W3T", [P, P]); ka = sb("ka", [P, 2])
        wsc = sb("wsc", [P, 2]); wtx = sb("wtx", [P, P]); wsx = sb("wsx", [P, P])
        zeros = sb("zeros", [P, P])
        idx_all = sb("idx_all", [P, NGE * 12], I32)

        xs = sb("xs", [P, 2, T, D]); xd = sb("xd", [P, 2, T, D])
        gidx = sb("gidx", [P, 2, 8], I32); sidx = sb("sidx", [P, 2, T], I32)
        same = sb("same", [P, 2, T])
        kb = sb("kb", [P, 2, G + 1], I32); gate = sb("gate", [P, 2, G])
        stats = sb("stats", [P, 3, T, 6]); mv = sb("mv", [P, 2, 3, T, 2])
        sd = sb("sd", [P, 2, 3, T]); rs = sb("rs", [P, 2, 3, T]); nb = sb("nb", [P, 2, 3, T])
        hs = sb("hs", [P, 2, T, D]); hd = sb("hd", [P, 2, T, D])
        agg = sb("agg", [P, 2, G])
        hdT = sb("hdT", [P, 2, G]); uT = sb("uT", [P, G])
        row = sb("row", [P, 2, T, D]); keep = sb("keep", [P, 2, T, D])

        ROOM = 26 * 1024
        arena = sb("arena", [P, ROOM])
        room = [0]

        def view(shape, dt=F32):
            words = 1
            for n in shape[1:]:
                words *= n
            part = arena[0:shape[0], room[0]:room[0] + words]
            room[0] += words
            assert room[0] <= ROOM, room[0]
            if dt is not F32:
                part = part.bitcast(dt)
            if len(shape) == 2:
                return part
            names = "abcd"[:len(shape) - 1]
            spaced = " ".join(names)
            return part.rearrange(f"p ({spaced}) -> p {spaced}", **dict(zip(names, shape[1:])))

        xn = view([P, 4, T, D]); yn = view([P, 4, T, D]); on = view([P, 2, T, D]); xo = view([P, 2, T, D])
        hn = view([P, 2, T, D]); hnT = view([P, 4, G]); unT = view([P, 2, G])
        statn = view([P, 2, T, 6]); mvn = view([P, 2, 2, T, 2])
        sdn = view([P, 2, 2, T]); rsn = view([P, 2, 2, T]); nbn = view([P, 2, 2, T])
        ntb = view([K * K, 4, G], I32); ohn = view([K * K, 4, G // 2]).bitcast(BF16)
        ends = view([P, NT, 2], I32)
        lo = view([P, NT]); hi = view([P, NT]); digit = view([P, NT], I32); keyf = view([P, NT])
        cnt_i = view([P, NHI], I32); cnt = view([P, NHI])
        below = view([P, P])
        above = view([P, P])
        OL = view([P, 2, P // 2]).bitcast(BF16); OH = view([P, 2, NHI // 2]).bitcast(BF16); OLT = view([P, 2, P])
        table = view([P, NHI]); incl = view([P, NHI]); onesn = view([P, NHI])
        offs = view([P, 1]); skb = view([P, 4, P], I32)
        pick = view([P, NHI]); pickr = view([P, P])
        pos0 = view([P, 4]); rank = view([P, 4])
        posi = view([P, 4], I32); recs = view([P, 4, 2], I32)
        sentinel = sb("sentinel", [1, 2], I32)
        tyi = view([P, 4, 2], I32)
        TYC = -(-2 * NT // P) * P
        tycol = view([P, TYC]); tyrow = view([P, TYC // P, P])
        room[0] = 0
        edge_rec = view([P, 2, T, 6], I32); gcol = view([P, 2, T])
        mark = room[0]
        tyb = view([P, 2, 2, G])
        ohT = view([K * K, 2, 2, G // 2]).bitcast(BF16)
        sT = view([P, K, G]); dT = view([P, K, G])
        eb = view([P, 2, G], I32)
        km = view([P, K, G]); vm = view([P, K, G])
        qT = view([P, G]); prod = view([P, G])
        rst = view([H, 2, G]); mx = view([H, 2, G + 1])
        ein = view([H, 2, G]); eo = view([H, 2, G]); den = view([H, 2, G]); rr = view([P, T, H]); rb = view([P, T, H, DK])
        aS = view([P, G]); vA = view([P, G]); nrm = view([P, G]); gT = view([P, G]); gm = view([P, K, G])
        o2 = view([P, T, D]); y2 = view([P, T, D])
        held = view([P, 2, T, D])
        gain = view([P, 2, T, D])
        room[0] = mark
        sc3 = view([P, G]); ex = view([P, 2, G]); hE = view([P, G]); den3 = view([1, 2, G])
        place3 = view([P, 2, T]); place4 = view([P, 2, T]); rd3 = view([P, T])

        bank = ctx.enter_context(nc.psum_tensor("bank", [P, 8, G], F32))

        w_in, consts, weights = sem("w_in"), sem("consts"), sem("weights")
        prep = {n: sem("prep_" + n) for n in ("pri", "t", "copy", "wsc")}
        p_in, p_out, p_sum, p_copy = pair("p_in"), pair("p_out"), sem("p_sum"), sem("p_copy")
        singles, pairs = {}, {}

        def stage(prefix, groups, names, transfers, buffers=2):
            signals = {}
            for n in names.split():
                if prefix + n not in singles:
                    singles[prefix + n] = [sem(prefix + n), 0]
                s, past = singles[prefix + n]
                signals[n] = Signal(s, past)
                singles[prefix + n][1] += groups
            for n, total in transfers.items():
                if prefix + n not in pairs:
                    pairs[prefix + n] = [[sem(f"{prefix}{n}_{b}") for b in range(buffers)], 0]
                s, past = pairs[prefix + n]
                signals[n] = [Signal(s[b], past) for b in range(buffers)]
                pairs[prefix + n][1] += total
            return signals

        A = stage("node_", NGN, "var sd ln h t tc u uc z x2", {"in": 16 * HALF, "out": 32 * HALF}, 4)
        B = stage("node_", NGN, "var sd ln h oh bu gb var2 sd2 ln2 y x3", {"in": 32 * HALF, "out": 32 * HALF}, 4)
        four = 16 * T * HALF
        L = {}
        L["l0"] = stage("edge_", NGE, "gidx gate var sd ln h keep t agg z row",
                        {"src": four, "dst": four, "scat": four, "keys": 16 * HALF})
        L["l1"] = stage("edge_", NGE, "gidx gate var sd ln vard sdd lnd h hd keep t td tdc agg u uc z row",
                        {"src": four, "dst": four, "scat": four, "keys": 16 * HALF})
        L["l2"] = stage("edge_", NGE,
                        "gidx gate rst var sd ln vard sdd lnd h hd keep s d ms md oh k v q qc km vm kr m prod att "
                        "ein eo a ac c den dent rden rb r va agg nrm g gm u ubg ubgc hold var3 sd3 ln3 y row",
                        {"src": four, "dst": four, "scat": 2 * four, "keys": 16 * HALF, "types": 48 * HALF})
        L["l3"] = stage("edge_", NGE,
                        "gidx gcol gate var sd ln vard sdd lnd h hd keep t td he tdc sco scc clip ex agg z row",
                        {"src": four, "dst": four, "scat": four, "rec": 48 * HALF})
        R = {n: sem("r_" + n) for n in ("digits", "one", "hist", "rowsum", "offs", "olt", "oltc", "look",
                                         "tile", "tab", "pos", "sent", "tycol", "tyturn", "tyrow", "tyout")}
        R.update({n: [sem(f"r_{n}_{m}") for m in range(4)] for n in ("keys", "scat", "types")})
        own_dve = {n: sem("dve_" + n) for n in ("prep", "r1", "r2", "l0", "l1", "l2", "l3")}
        dve_turn, pool_turn, pe_turn = sem("dve_turn"), sem("pool_turn"), sem("pe_turn")
        block = ctx.enter_context(nc.Block())

        def rows(dram, g):
            return dram[bass.ds(g * G, G), :].rearrange("(t p) d -> p t d", p=P)

        def tiles(ap):
            return ap.rearrange("p (t d) -> p t d", t=T)

        def at(i, b):
            return i * 2 + b

        def node(i, m):
            return i * 4 + m

        def stage_done(eng, l, scatters=1):
            for b in range(2):
                eng.wait_ge(*L[l]["scat"][b].count(16 * T * scatters * HALF))

        LOADS = [(W0[:], w["L0_gnn_W"]), (W1[:], w["L1_gnn_W1"]), (W2[:], w["L1_gnn_W2"]), (Wr[:], w["L1_gnn_Wres"]),
                 (b1c[:], w["L1_gnn_b1"].rearrange("(n a) -> n a", a=1)),
                 (rowb[:, 0, :], w["L0_gnn_b"].partition_broadcast(K)),
                 (rowb[:, 1, :], w["L1_gnn_b2"].partition_broadcast(K)),
                 (rowb[:, 2, :], w["L1_gnn_bres"].partition_broadcast(K)),
                 (b0x[:], w["L0_gnn_b"].partition_broadcast(P)),
                 (Wq[:], w["L2_gnn_Wq"].rearrange("k i o -> i k o")), (Wk[:], w["L2_gnn_Wk"].rearrange("k i o -> i k o")),
                 (Wv[:], w["L2_gnn_Wv"].rearrange("k i o -> i k o")), (Wu[:], w["L2_gnn_W_upd"].rearrange("k i o -> i k o")),
                 (pri[:], w["L2_gnn_rel_pri"]),
                 (W3[:], w["L3_gnn_kernel"]), (ka[:], w["L3_gnn_kernel_attention"]),
                 (idx_all[:], eidx), (ends[:], edge_ends)]
        LOADS += [(tb[K * part:K * part + K, n, :], w["L2_gnn_" + name]) for part in range(3)
                  for n, name in enumerate(("bq", "bk", "bv", "b_upd", "ln_gamma", "ln_beta"))]
        REL = [(dst[DK * h:DK * (h + 1), :, DK * h:DK * (h + 1)], w[name][:, h, :, :].rearrange("r d f -> d r f"))
               for dst, name in ((Ra, "L2_gnn_rel_att"), (Rm, "L2_gnn_rel_msg")) for h in range(H)]
        N_IN = 16 * (len(LOADS) + len(REL))
        N_CONST = 19

        @block.sync
        def _(sp):
            for dst, src in LOADS:
                sp.dma_start(dst, src).then_inc(w_in, 16)
            sp.wait_ge(consts, N_CONST)
            for dst, src in REL:
                sp.dma_start(dst, src).then_inc(w_in, 16)
            sp.dma_start(rec[0:1, :], sentinel[:]).then_inc(R["sent"], 16)
            sp.dma_start(rec[EP + 1:EP + 2, :], sentinel[:]).then_inc(R["sent"], 16)

            def sort_keys(i, m):
                freed(sp, R["pos"], node(i, m) - 3)
                sp.dma_start(skb[:, m, :], skeys[bass.ds(node(i, m) * P, P)].partition_broadcast(P))\
                  .then_inc(R["keys"][m], 16)

            def load_p(i, b):
                freed(sp, p_sum, at(i, b) - 1)
                sp.dma_start(xn[:, b], rows(x, at(i, b))).then_inc(p_in[b], 16)
            pipeline(sp, NT // 4, [(None, 0, load_p), (0, 0, sort_keys), (1, 0, sort_keys)])
            for b in range(2):
                sp.wait_ge(p_out[b], 16 * (NGN // 2))

            def load_keys(l):
                S = L[l]

                def load(i, b):
                    freed(sp, S["gate"], at(i, b) - 1)
                    sp.dma_start(kb[:, b, :], keys[bass.ds(at(i, b) * G, G + 1)].partition_broadcast(P))\
                      .then_inc(S["keys"][b].sem, 16)
                return load

            def load_a(i, m):
                freed(sp, A["var"], node(i, m) - 3)
                sp.dma_start(xn[:, m], rows(x, node(i, m))).then_inc(A["in"][m].sem, 16)
            pipeline(sp, HALF, [(None, 0, load_keys("l0")), (0, 0, load_a), (1, 0, load_a)])
            stage_done(sp, "l0")
            for m in range(4):
                sp.wait_ge(*A["out"][m].count(32 * HALF))

            def load_b(i, m):
                freed(sp, B["x3"], node(i, m) - 3)
                sp.dma_start(xn[:, m], rows(x2n, node(i, m))).then_inc(B["in"][m].sem, 16)
                sp.dma_start(ntb[:, m, :], ntype[bass.ds(node(i, m) * G, G), :].rearrange("n a -> (n a)")
                             .partition_broadcast(K * K)).then_inc(B["in"][m].sem, 16)
            pipeline(sp, HALF, [(None, 0, load_keys("l1")), (0, 0, load_b), (1, 0, load_b)])
            stage_done(sp, "l1")

            sp.wait_ge(R["tyrow"], 1)
            for c in range(TYC // P):
                n = min(P, 2 * NT - c * P)
                sp.dma_start(edge_kinds[c * P:c * P + n, :], tyrow[0:n, c, :]).then_inc(R["tyout"], 16)
            sp.wait_ge(R["tyout"], 16 * (TYC // P))
            flat_kinds = edge_kinds.rearrange("n p -> (n p)")

            def load_types(i, b):
                S, g = L["l2"], at(i, b)
                freed(sp, S["vm"], g - 1)
                sp.dma_start(eb[:, b, :], etypes[bass.ds(g * G, G)].partition_broadcast(P)).then_inc(S["types"][b].sem, 16)
                freed(sp, S["gm"], g - 1)
                for k in range(2):
                    sp.dma_start(tyb[:, b, k, :], flat_kinds[bass.ds(g * G + k * EP, G)].partition_broadcast(P))\
                      .then_inc(S["types"][b].sem, 16)
            pipeline(sp, HALF, [(None, 0, load_keys("l2")), (None, 0, load_types)])
            for m in range(4):
                sp.wait_ge(R["scat"][m], 16 * (NT // 4))
            sp.wait_ge(R["sent"], 32)

            def load_records(i, b):
                freed(sp, L["l3"]["gcol"], at(i, b) - 1)
                for k in range(3):
                    sp.dma_start(edge_rec[:, b, :, 2 * k:2 * k + 2],
                                 rec[bass.ds(at(i, b) * G + k, G), :].rearrange("(t p) c -> p t c", p=P))\
                      .then_inc(L["l3"]["rec"][b].sem, 16)
            pipeline(sp, HALF, [(None, 0, load_records)])

        @block.gpsimd
        def _(pool):
            def const(ins):
                ins.then_inc(consts, 1)
            for tile_, value in ((ident, 0.0), (ones1, 1.0), (epsc, EPS), (head, 1.0), (headT, 1.0), (Ra, 0.0), (Rm, 0.0),
                                 (zeros, 0.0), (below, 1.0), (above, 1.0), (onesn, 1.0), (sentinel, -1)):
                const(nc.gpsimd.memset(tile_[:], value))
            const(nc.gpsimd.iota(rowno[:], pattern=[[0, 1]], base=0, channel_multiplier=1))
            const(nc.gpsimd.iota(cnt_i[:], pattern=[[1, NHI]], base=0, channel_multiplier=0))
            pool.wait_ge(consts, 14)

            def select(buf, op, base, pattern, mult, fill):
                return nc.gpsimd.affine_select(out=buf[:], in_=buf[:], compare_op=op, fill=fill, base=base,
                                               pattern=pattern, channel_multiplier=mult)
            const(select(ident, ALU.not_equal, 0, [[-1, P]], 1, 1.0))
            const(select(below, ALU.is_ge, -1, [[-1, P]], 1, 0.0))
            const(select(above, ALU.is_ge, -1, [[1, P]], -1, 0.0))
            select(head, ALU.is_ge, 0, [[-DK, H]], 1, 0.0)
            const(select(headT, ALU.is_ge, 0, [[1, P]], -DK, 0.0))
            pool.wait_ge(consts, 18)
            select(head, ALU.is_ge, DK - 1, [[DK, H]], -1, 0.0)
            const(select(headT, ALU.is_ge, DK - 1, [[-1, P]], DK, 0.0))

            def gather_types(m, k):
                pool.indirect_dma_start(out=tyi[:, m, k:k + 1], out_offset=None, in_=ntype,
                                        in_offset=bass.IndirectOffsetOnAxis(ap=recs[:, m, k:k + 1], axis=0),
                                        bounds_check=NP - 1, oob_is_err=False).then_inc(R["types"][m], 16)

            def source_types(i, m):
                t = node(i, m)
                pool.wait_ge(R["one"], t + 1)
                freed(pool, R["tycol"], t - 3)
                pool.sem_inc(pool_turn, 1)
                gather_types(m, 0)
            pipeline(pool, NT // 4, [(0, 0, source_types), (1, 0, source_types)])

            def sort_scatter(i, m):
                t = node(i, m)
                pool.wait_ge(R["pos"], t + 1)
                pool.sem_inc(pool_turn, 1)
                pool.indirect_dma_start(out=rec, out_offset=bass.IndirectOffsetOnAxis(ap=posi[:, m:m + 1], axis=0),
                                        in_=recs[:, m, :], in_offset=None).then_inc(R["scat"][m], 16)
                pool.wait_ge(R["tycol"], NT + t - 3)
                pool.sem_inc(pool_turn, 1)
                gather_types(m, 1)
            pipeline(pool, NT // 4, [(0, 0, sort_scatter), (1, 0, sort_scatter)])

            def gather(table, index, dst, bound, done):
                for t in range(T):
                    pool.indirect_dma_start(out=dst[:, t, :], out_offset=None, in_=table,
                                            in_offset=bass.IndirectOffsetOnAxis(ap=index[:, t:t + 1], axis=0),
                                            bounds_check=bound, oob_is_err=False).then_inc(done.sem, 16)

            def scatter(S, table, i, b):
                for t in range(T):
                    pool.indirect_dma_start(out=table, out_offset=bass.IndirectOffsetOnAxis(ap=sidx[:, b, t:t + 1], axis=0),
                                            in_=row[:, b, t, :], in_offset=None, bounds_check=NP - 1,
                                            oob_is_err=False).then_inc(S["scat"][b].sem, 16)

            def edge_stage(l, table, targets, lag):
                S = L[l]

                def gathers(i, b):
                    pool.wait_ge(*S["gidx"].count(at(i, b) + 1))
                    freed(pool, S["keep"] if "keep" in S else S["row"], at(i, b) - 1)
                    pool.sem_inc(pool_turn, 1)
                    gather(table, gidx[:, b, 0:4], xs[:, b], NP - 1, S["src"][b])
                    gather(table, gidx[:, b, 4:8], xd[:, b], NP - 1, S["dst"][b])

                def scatters(i, b):
                    pool.wait_ge(*S["row"].count(at(i, b) + 1))
                    pool.sem_inc(pool_turn, 1)
                    for target in targets:
                        scatter(S, target, i, b)

                gathers(0, 0)
                pipeline(pool, HALF, [(None, -1, gathers), (None, lag, scatters)])
                stage_done(pool, l, len(targets))

            for b in range(2):
                pool.wait_ge(p_out[b], 16 * (NGN // 2))
            edge_stage("l0", x, [x1], 2)
            for m in range(4):
                pool.wait_ge(*A["out"][m].count(32 * HALF))
            edge_stage("l1", x1, [x2], 2)
            for m in range(4):
                pool.wait_ge(*B["out"][m].count(32 * HALF))
            edge_stage("l2", x2, [x3, out], 3)
            edge_stage("l3", x3, [out], 2)

        @block.vector
        def _(dve):
            def ln_stats(own, src, st, m, S, var, shifted, g):
                freed(dve, S[var], g)
                freed(dve, S[shifted], g - 1)
                for t in range(T):
                    last = nc.vector.bn_stats(out=st[:, t, :], in_=src[:, t, :])
                own.step(last)
                dve.sem_inc(dve_turn, 1)
                for t in range(T):
                    last = nc.vector.bn_aggr(out=m[:, t, :], in_=st[:, t, :])
                last.then_inc(S[var].sem, 1)

            def ln_shift(own, S, std_ready, g, b, which, m, s_, r_, n_, ready):
                dve.wait_ge(*S[std_ready].count(g + 1))
                own.step(nc.vector.reciprocal(r_[:, b, which, :], s_[:, b, which, :]))
                nc.vector.scalar_tensor_tensor(out=n_[:, b, which, :], in0=m[:, b, which, :, 0], scalar=-1.0,
                                               in1=r_[:, b, which, :], op0=ALU.mult, op1=ALU.mult).then_inc(S[ready].sem, 1)

            dve.wait_ge(w_in, N_IN)
            dve.wait_ge(consts, N_CONST)
            own = Own(dve, own_dve["prep"])
            own.step(nc.vector.tensor_copy(rownof[:], rowno[:]))
            nc.vector.tensor_copy(cnt[:], cnt_i[:])
            nc.vector.tensor_copy(identb[:], ident[:])
            nc.vector.tensor_tensor(out=rowb[:, 1, :], in0=rowb[:, 1, :], in1=rowb[:, 2, :], op=ALU.add)
            own.step(nc.vector.memset(onesb[:], 1.0))
            own.step(nc.vector.tensor_scalar_max(rowb[:, 2, :], rowb[:, 0, :], 0.0))
            nc.vector.tensor_copy(keyf[:], ends[:, :, 0])
            own.step(nc.vector.tensor_scalar_max(b0x[:], b0x[:], 0.0))
            row9 = rownof[0:K * K, :]
            nc.vector.tensor_scalar(third[:, 0:1], row9, float(K), None, ALU.is_ge)
            own.step(nc.vector.tensor_scalar(third[:, 2:3], row9, float(2 * K), None, ALU.is_ge))
            own.step(nc.vector.scalar_tensor_tensor(out=kind[:], in0=third[:, 0:1], scalar=-float(K), in1=row9,
                                                    op0=ALU.mult, op1=ALU.add))
            own.step(nc.vector.scalar_tensor_tensor(out=kind[:], in0=third[:, 2:3], scalar=-float(K), in1=kind[:],
                                                    op0=ALU.mult, op1=ALU.add))
            own.step(nc.vector.tensor_tensor(out=third[:, 1:2], in0=third[:, 0:1], in1=third[:, 2:3], op=ALU.subtract))
            own.step(nc.vector.tensor_scalar(third[:, 0:1], row9, float(K), None, ALU.is_lt))
            for part in range(3):
                own.step(nc.vector.tensor_scalar(rowsel[:, part:part + 1], rownof[0:K, :], float(part), None, ALU.is_equal))

            def split(values, rounded, total, parts, select):
                for part in range(3):
                    own.step(nc.vector.tensor_copy(rounded, values))
                    own.step(nc.vector.tensor_tensor(out=values, in0=values, in1=rounded, op=ALU.subtract))
                    if part == 0:
                        own.step(nc.vector.tensor_scalar(total, rounded, select[:, 0:1], None, ALU.mult))
                    else:
                        own.step(nc.vector.scalar_tensor_tensor(out=total, in0=rounded, scalar=select[:, part:part + 1],
                                                                in1=total, op0=ALU.mult, op1=ALU.add))
                own.step(nc.vector.tensor_copy(parts, total))
            split(tb[:], tbp[:], tbr[:], tparts[:], third)
            split(rowb[:], rowp[:], rowr[:], rowparts[:], rowsel)
            own.step(nc.vector.memset(tycol[:], 0.0))
            dve.wait_ge(prep["pri"], 1)
            own.step(nc.vector.tensor_scalar(pric[:], bank[:, 0, 0:K], 1.0 / DK ** 0.5, None, ALU.mult))
            for r in range(K):
                own.step(nc.vector.tensor_scalar(Ra[:, r, :], Ra[:, r, :], pric[:, r:r + 1], None, ALU.mult))
            dve.wait_ge(prep["t"], 1)
            nc.vector.tensor_copy(W3T[:], bank[:, 1, 0:P]).then_inc(prep["copy"], 1)
            dve.wait_ge(prep["wsc"], 1)
            own.step(nc.vector.tensor_copy(wsc[:], bank[:, 2, 0:2]))
            own.step(nc.vector.tensor_scalar(wtx[:], zeros[:], wsc[:, 0:1], None, ALU.add))
            nc.vector.tensor_scalar(wsx[:], zeros[:], wsc[:, 1:2], None, ALU.add).then_inc(weights, 1)
            dve.wait_ge(weights, 1)

            def digits(op, value, dst):
                own.step(nc.vector.tensor_single_scalar(digit[:], ends[:, :, 0], value, op))
                own.step(nc.vector.tensor_copy(dst[:], digit[:]))
            digits(ALU.bitwise_and, P - 1, lo)
            digits(ALU.logical_shift_right, P.bit_length() - 1, hi)

            def one_hots(t, b):
                nc.vector.tensor_scalar(OL[:, b, :], cnt[:, 0:P], lo[:, bass.ds(t, 1)], None, ALU.is_equal)
                nc.vector.tensor_scalar(OH[:, b, :], cnt[:], hi[:, bass.ds(t, 1)], None, ALU.is_equal)\
                  .then_inc(R["one"], 1)

            def count(i, m):
                t = node(i, m)
                freed(dve, R["types"][m], 16 * i)
                nc.vector.tensor_copy(recs[:, m, 0:1], ends[:, bass.ds(t, 1), 0])
                freed(dve, R["hist"], t - 1)
                one_hots(t, m % 2)

            def source_types(i, m):
                dve.wait_ge(R["types"][m], 16 * i + 16)
                nc.vector.tensor_copy(tycol[:, bass.ds(node(i, m), 1)], tyi[:, m, 0:1]).then_inc(R["tycol"], 1)
            pipeline(dve, NT // 4, [(c, lag, work) for c in range(2) for lag, work in ((4, source_types), (0, count))])
            dve.wait_ge(R["hist"], NT)
            own = Own(dve, own_dve["r1"])
            own.step(nc.vector.tensor_copy(table[:], bank[:, 5, 0:NHI]))
            own.step(nc.vector.tensor_tensor_scan(out=incl[:], data0=onesn[:], data1=table[:], initial=0.0,
                                                  op0=ALU.mult, op1=ALU.add))
            nc.vector.tensor_copy(offs[:], incl[:, NHI - 1:NHI]).then_inc(R["rowsum"], 1)
            dve.wait_ge(R["offs"], 1)
            own.step(nc.vector.tensor_copy(offs[:], bank[:, 6, 0:1]))
            nc.vector.scalar_tensor_tensor(out=table[:], in0=incl[:], scalar=offs[:, 0:1], in1=table[:],
                                           op0=ALU.add, op1=ALU.subtract).then_inc(R["tab"], 1)

            relu_b0 = b0x[:, :].unsqueeze(1).to_broadcast([P, T, D])
            own = Own(dve, own_dve["r2"])

            def place_hots(i, m):
                t = node(i, m)
                freed(dve, R["tile"], t - 1)
                one_hots(t, m % 2)

            def place_rank(i, m):
                t = node(i, m)
                dve.wait_ge(R["keys"][m], 16 * i + 16)
                freed(dve, R["scat"][m], 16 * i)
                dve.wait_ge(R["types"][m], 16 * (NT // 4) + 16 * i)
                own.step(nc.vector.scalar_tensor_tensor(
                    out=pickr[:], in0=skb[:, m, :], scalar=keyf[:, bass.ds(t, 1)], in1=below[:],
                    op0=ALU.is_equal, op1=ALU.mult, accum_out=rank[:, m:m + 1]))
                nc.vector.tensor_copy(recs[:, m, :], ends[:, bass.ds(t, 1), :].rearrange("p t k -> p (t k)"))

            def place_add(i, m):
                t = node(i, m)
                dve.wait_ge(R["look"], t + 1)
                dve.wait_ge(R["tab"], t + 1)
                nc.vector.tensor_tensor(out=table[:], in0=table[:], in1=bank[:, 4 + m % 2, 0:NHI], op=ALU.add)\
                  .then_inc(R["tab"], 1)

            def place_row(i, m):
                t = node(i, m)
                own.step(nc.vector.scalar_tensor_tensor(
                    out=pick[:], in0=cnt[:], scalar=hi[:, bass.ds(t, 1)], in1=bank[:, 6 + m % 2, 0:NHI],
                    op0=ALU.is_equal, op1=ALU.mult, accum_out=pos0[:, m:m + 1]))
                nc.vector.scalar_tensor_tensor(out=posi[:, m:m + 1], in0=pos0[:, m:m + 1], scalar=1.0,
                                               in1=rank[:, m:m + 1], op0=ALU.add, op1=ALU.add).then_inc(R["pos"], 1)

            def target_types(i, m):
                dve.wait_ge(R["types"][m], 16 * (NT // 4) + 16 * i + 16)
                nc.vector.tensor_copy(tycol[:, bass.ds(node(i, m) + NT, 1)], tyi[:, m, 1:2]).then_inc(R["tycol"], 1)

            pipeline(dve, NT // 4, [(c, lag, work) for c in range(2) for lag, work in
                                    ((0, place_hots), (0, place_rank), (1, place_add), (1, place_row),
                                     (4, target_types))], own)
            dve.wait_ge(R["tyturn"], 1)
            nc.vector.tensor_copy(tyrow[:], bank[:, 0, 0:TYC].rearrange("p (c e) -> p c e", e=P)).then_inc(R["tyrow"], 1)
            for b in range(2):
                dve.wait_ge(p_out[b], 16 * (NGN // 2))

            def next_gather(S, i, b):
                freed(dve, S["src"][b], 16 * T * i)
                freed(dve, S["dst"][b], 16 * T * i)
                nc.vector.tensor_copy(gidx[:, b, :], idx_all[:, bass.ds(at(i, b) * 12, 8)]).then_inc(S["gidx"].sem, 1)

            def scatter_idx(own, S, i, b, targets, key, following):
                freed(dve, S["scat"][b], 16 * T * targets * i)
                own.step(nc.vector.tensor_tensor(out=same[:, b, :], in0=key, in1=following, op=ALU.is_equal))
                own.step(nc.vector.scalar_tensor_tensor(out=sidx[:, b, :], in0=same[:, b, :], scalar=float(FAR),
                                                        in1=key, op0=ALU.mult, op1=ALU.add))

            def edge_keys(i, b):
                return (idx_all[:, bass.ds(at(i, b) * 12 + 4, 4)], idx_all[:, bass.ds(at(i, b) * 12 + 8, 4)])

            def gates(S, i, b, parts, buf):
                dve.wait_ge(*S["keys"][b].count(16 * i + 16))
                freed(dve, S["agg"], at(i, b) - 1)
                nc.vector.tensor_tensor(out=buf, in0=kb[0:parts, b, 1:G + 1], in1=kb[0:parts, b, 0:G], op=ALU.is_equal)\
                  .then_inc(S["gate"].sem, 1)

            def segment_sum(S, i, b, values):
                g = at(i, b)
                dve.wait_ge(*S["gate"].count(g + 1))
                dve.wait_ge(*S["t"].count(g + 1))
                freed(dve, S["agg"], g)
                nc.vector.tensor_tensor_scan(out=agg[:, b, :], data0=gate[:, b, :], data1=values,
                                             initial=agg[:, 1 - b, G - 1:G], op0=ALU.mult, op1=ALU.add)\
                  .then_inc(S["agg"].sem, 1)

            def affine(own, S, gamma, beta, y, x_in, out_, ready):
                own.step(nc.vector.tensor_tensor(out=y, in0=y, in1=gamma, op=ALU.mult))
                own.step(nc.vector.tensor_tensor(out=y, in0=y, in1=beta, op=ALU.add))
                nc.vector.tensor_tensor(out=out_, in0=y, in1=x_in, op=ALU.add).then_inc(S[ready].sem, 1)

            own = Own(dve, own_dve["l0"])
            S0 = L["l0"]

            def l0_next(i, b):
                next_gather(S0, i, b)

            def l0_stats(i, b):
                dve.wait_ge(*S0["src"][b].count(16 * T * (i + 1)))
                ln_stats(own, xs[:, b], stats[:, 0], mv[:, b, 0], S0, "var", "ln", at(i, b))

            def l0_shift(i, b):
                ln_shift(own, S0, "sd", at(i, b), b, 0, mv, sd, rs, nb, "ln")
                gates(S0, i, b, P, gate[:, b, :])

            def l0_sum(i, b):
                segment_sum(S0, i, b, bank[:, 3, :])

            def l0_rows(i, b):
                g = at(i, b)
                scatter_idx(own, S0, i, b, 1, *edge_keys(i, b))
                dve.wait_ge(*S0["z"].count(g + 1))
                nc.vector.scalar_tensor_tensor(out=row[:, b], in0=tiles(bank[:, 4, :]), scalar=0.0, in1=keep[:, b],
                                               op0=ALU.max, op1=ALU.add).then_inc(S0["row"].sem, 1)

            def a_stats(i, m):
                q = node(i, m)
                dve.wait_ge(*A["in"][m].count(16 * i + 16))
                freed(dve, A["x2"], q - 3)
                own.step(nc.vector.tensor_tensor(out=yn[:, m], in0=xn[:, m], in1=relu_b0, op=ALU.add))
                ln_stats(own, yn[:, m], statn[:, 0], mvn[:, m % 2, 0], A, "var", "ln", node(i, m))

            def a_shift(i, m):
                ln_shift(own, A, "sd", node(i, m), m % 2, 0, mvn, sdn, rsn, nbn, "ln")

            def a_rows(i, m):
                dve.wait_ge(*A["z"].count(node(i, m) + 1))
                if m >= 2:
                    freed(dve, A["out"][m - 2], 32 * i + 32)
                else:
                    freed(dve, A["out"][m + 2], 32 * i)
                nc.vector.tensor_tensor(out=on[:, m % 2], in0=yn[:, m], in1=tiles(bank[:, 2, :]), op=ALU.add)\
                  .then_inc(A["x2"].sem, 1)

            nc.vector.memset(agg[:, 1, :], 0.0).then_inc(weights, 1)
            dve.wait_ge(weights, 2)
            l0_next(0, 0)
            l0_next(0, 1)
            pipeline(dve, HALF, [(0, 4, a_rows), (0, 0, a_stats), (None, 2, l0_rows), (None, 1, l0_sum),
                                 (None, 0, l0_stats), (0, 0, a_shift), (None, -2, l0_next),
                                 (1, 4, a_rows), (1, 0, a_stats), (None, 0, l0_shift), (1, 0, a_shift)], own)
            stage_done(dve, "l0")
            for m in range(4):
                dve.wait_ge(*A["out"][m].count(32 * HALF))

            own = Own(dve, own_dve["l1"])
            S1 = L["l1"]

            def l1_next(i, b):
                next_gather(S1, i, b)

            def l1_stats(i, b):
                dve.wait_ge(*S1["src"][b].count(16 * T * (i + 1)))
                ln_stats(own, xs[:, b], stats[:, 0], mv[:, b, 0], S1, "var", "ln", at(i, b))
                dve.wait_ge(*S1["dst"][b].count(16 * T * (i + 1)))
                dve.wait_ge(*S1["var"].count(at(i, b) + 1))
                ln_stats(own, xd[:, b], stats[:, 1], mv[:, b, 1], S1, "vard", "lnd", at(i, b))

            def l1_shift(i, b):
                ln_shift(own, S1, "sd", at(i, b), b, 0, mv, sd, rs, nb, "ln")
                ln_shift(own, S1, "sdd", at(i, b), b, 1, mv, sd, rs, nb, "lnd")
                gates(S1, i, b, P, gate[:, b, :])

            def l1_sum(i, b):
                g = at(i, b)
                freed(dve, S1["u"], g - 1)
                segment_sum(S1, i, b, bank[:, 0, :])

            def l1_rows(i, b):
                scatter_idx(own, S1, i, b, 1, *edge_keys(i, b))
                dve.wait_ge(*S1["z"].count(at(i, b) + 1))
                nc.vector.tensor_tensor(out=row[:, b], in0=tiles(bank[:, 3, :]), in1=keep[:, b], op=ALU.add)\
                  .then_inc(S1["row"].sem, 1)

            def b_stats(i, m):
                q = node(i, m)
                dve.wait_ge(*B["in"][m].count(32 * i + 32))
                ln_stats(own, xn[:, m], statn[:, 0], mvn[:, m % 2, 0], B, "var", "ln", node(i, m))
                freed(dve, B["gb"], q - 3)
                nc.vector.tensor_scalar(ohn[:, m, :], ntb[:, m, :], kind[:, 0:1], None, ALU.is_equal)\
                  .then_inc(B["oh"].sem, 1)

            def b_shift(i, m):
                ln_shift(own, B, "sd", node(i, m), m % 2, 0, mvn, sdn, rsn, nbn, "ln")

            def b_mid(i, m):
                dve.wait_ge(*B["bu"].count(node(i, m) + 1))
                ln_stats(own, tiles(bank[:, 4 + 3 * (m % 2), :]), statn[:, 1], mvn[:, m % 2, 1], B, "var2", "ln2",
                         node(i, m))

            def b_shift2(i, m):
                ln_shift(own, B, "sd2", node(i, m), m % 2, 1, mvn, sdn, rsn, nbn, "ln2")

            def b_rows(i, m):
                dve.wait_ge(*B["y"].count(node(i, m) + 1))
                dve.wait_ge(*B["gb"].count(node(i, m) + 1))
                if m >= 2:
                    freed(dve, B["out"][m - 2], 32 * i + 32)
                else:
                    freed(dve, B["out"][m + 2], 32 * i)
                own.step(nc.vector.tensor_tensor(out=yn[:, m], in0=yn[:, m], in1=tiles(bank[:, 5, :]), op=ALU.mult))
                nc.vector.tensor_tensor(out=xo[:, m % 2], in0=yn[:, m], in1=tiles(bank[:, 6, :]), op=ALU.add)\
                  .then_inc(B["x3"].sem, 1)

            nc.vector.memset(agg[:, 1, :], 0.0).then_inc(weights, 1)
            dve.wait_ge(weights, 3)
            l1_next(0, 0)
            l1_next(0, 1)
            pipeline(dve, HALF, [(0, 3, b_rows), (0, 0, b_stats), (None, 1, l1_sum), (0, 1, b_mid), (0, 0, b_shift),
                                 (None, 0, l1_stats), (0, 1, b_shift2), (None, -2, l1_next),
                                 (1, 3, b_rows), (1, 0, b_stats), (None, 2, l1_rows), (1, 1, b_mid), (1, 0, b_shift),
                                 (None, 0, l1_shift), (1, 1, b_shift2)], own)
            stage_done(dve, "l1")
            for m in range(4):
                dve.wait_ge(*B["out"][m].count(32 * HALF))

            S2 = L["l2"]

            def l2_next(i, b):
                next_gather(S2, i, b)

            def l2_stats(i, b):
                dve.wait_ge(*S2["src"][b].count(16 * T * (i + 1)))
                ln_stats(own, xs[:, b], stats[:, 0], mv[:, b, 0], S2, "var", "ln", at(i, b))
                dve.wait_ge(*S2["dst"][b].count(16 * T * (i + 1)))
                dve.wait_ge(*S2["var"].count(at(i, b) + 1))
                ln_stats(own, xd[:, b], stats[:, 1], mv[:, b, 1], S2, "vard", "lnd", at(i, b))

            def l2_restarts(i, b):
                g = at(i, b)
                gates(S2, i, b, H, gate[0:H, b, :])
                dve.wait_ge(*S2["gate"].count(g + 1))
                freed(dve, S2["ein"], g - 1)
                nc.vector.tensor_scalar(rst[:, b, :], gate[0:H, b, :], -NEVER, NEVER, ALU.mult, ALU.add)\
                  .then_inc(S2["rst"].sem, 1)

            def l2_shift(i, b):
                ln_shift(own, S2, "sd", at(i, b), b, 0, mv, sd, rs, nb, "ln")
                ln_shift(own, S2, "sdd", at(i, b), b, 1, mv, sd, rs, nb, "lnd")

            def l2_one_hots(i, b):
                g = at(i, b)
                dve.wait_ge(*S2["types"][b].count(48 * (i + 1)))
                freed(dve, S2["u"], g - 1)
                nc.vector.tensor_scalar(ohT[:, b].rearrange("p k e -> p (k e)"),
                                        tyb[0:K * K, b].rearrange("p k e -> p (k e)"), kind[:, 0:1], None, ALU.is_equal)\
                  .then_inc(S2["oh"].sem, 1)

            def masks(types_, src, dst_, done):
                for k in range(K):
                    last = nc.vector.scalar_tensor_tensor(out=dst_[:, k, :], in0=types_, scalar=float(k), in1=src,
                                                          op0=ALU.is_equal, op1=ALU.mult)
                last.then_inc(done.sem, 1)

            def l2_mask_src(i, b):
                g = at(i, b)
                dve.wait_ge(*S2["types"][b].count(48 * (i + 1)))
                dve.wait_ge(*S2["s"].count(g + 1))
                freed(dve, S2["v"], g)
                masks(tyb[:, b, 0, :], bank[:, 0, :], sT, S2["ms"])

            def l2_mask_dst(i, b):
                g = at(i, b)
                dve.wait_ge(*S2["d"].count(g + 1))
                freed(dve, S2["q"], g)
                masks(tyb[:, b, 1, :], bank[:, 1, :], dT, S2["md"])

            def l2_mask_k(i, b):
                dve.wait_ge(*S2["k"].count(at(i, b) + 1))
                freed(dve, S2["kr"], at(i, b))
                masks(eb[:, b, :], bank[:, 2, :], km, S2["km"])

            def l2_mask_v(i, b):
                dve.wait_ge(*S2["v"].count(at(i, b) + 1))
                freed(dve, S2["m"], at(i, b))
                masks(eb[:, b, :], bank[:, 3, :], vm, S2["vm"])

            def l2_prod(i, b):
                g = at(i, b)
                dve.wait_ge(*S2["kr"].count(g + 1))
                dve.wait_ge(*S2["qc"].count(g + 1))
                freed(dve, S2["att"], g)
                nc.vector.tensor_tensor(out=prod[:], in0=bank[:, 2, :], in1=qT[:], op=ALU.mult).then_inc(S2["prod"].sem, 1)

            def l2_max(i, b):
                g = at(i, b)
                dve.wait_ge(*S2["att"].count(g + 1))
                dve.wait_ge(*S2["rst"].count(g + 1))
                freed(dve, S2["eo"], g)
                att = bank[0:H, 7, :]
                own.step(nc.vector.tensor_copy(mx[:, b, 0:1], mx[:, 1 - b, G:G + 1]))
                own.step(nc.vector.tensor_tensor_scan(out=mx[:, b, 1:G + 1], data0=rst[:, b, :], data1=att,
                                                      initial=mx[:, b, 0:1], op0=ALU.add, op1=ALU.max))
                nc.vector.tensor_tensor(out=ein[:, 0, :], in0=att, in1=mx[:, b, 1:G + 1], op=ALU.subtract)
                own.step(nc.vector.tensor_tensor(out=ein[:, 1, :], in0=mx[:, b, 0:G], in1=mx[:, b, 1:G + 1],
                                                 op=ALU.subtract))
                nc.vector.tensor_tensor(out=ein[:, 1, :], in0=ein[:, 1, :], in1=rst[:, b, :], op=ALU.add)\
                  .then_inc(S2["ein"].sem, 1)

            def l2_den(i, b):
                g = at(i, b)
                dve.wait_ge(*S2["eo"].count(g + 1))
                freed(dve, S2["dent"], g - 1)
                freed(dve, S2["den"], g)
                nc.vector.tensor_tensor_scan(out=den[:, b, :], data0=eo[:, 1, :], data1=eo[:, 0, :],
                                             initial=den[:, 1 - b, G - 1:G], op0=ALU.mult, op1=ALU.add)\
                  .then_inc(S2["den"].sem, 1)

            def l2_rden(i, b):
                g = at(i, b)
                dve.wait_ge(*S2["dent"].count(g + 1))
                freed(dve, S2["rb"], g)
                own.step(nc.vector.tensor_scalar(rr[:], bank[:, 6, 0:T * H].rearrange("p (t h) -> p t h", t=T),
                                                 1e-16, None, ALU.add))
                nc.vector.reciprocal(rr[:], rr[:]).then_inc(S2["rden"].sem, 1)

            def l2_agg(i, b):
                g = at(i, b)
                dve.wait_ge(*S2["ac"].count(g + 1))
                dve.wait_ge(*S2["m"].count(g + 1))
                freed(dve, S2["agg"], g)
                nc.vector.tensor_tensor(out=vA[:], in0=bank[:, 5, :], in1=aS[:], op=ALU.mult).then_inc(S2["va"].sem, 1)
                dve.wait_ge(*S2["va"].count(g + 1))
                dve.wait_ge(*S2["c"].count(g + 1))
                nc.vector.tensor_tensor_scan(out=agg[:, b, :], data0=bank[:, 1, :], data1=vA[:],
                                             initial=agg[:, 1 - b, G - 1:G], op0=ALU.mult, op1=ALU.add)\
                  .then_inc(S2["agg"].sem, 1)

            def l2_divide(i, b):
                g = at(i, b)
                dve.wait_ge(*S2["agg"].count(g + 1))
                dve.wait_ge(*S2["r"].count(g + 1))
                freed(dve, S2["g"], g)
                nc.vector.tensor_tensor(out=nrm[:], in0=bank[:, 7, :], in1=agg[:, b, :], op=ALU.mult)\
                  .then_inc(S2["nrm"].sem, 1)

            def l2_mask_upd(i, b):
                dve.wait_ge(*S2["g"].count(at(i, b) + 1))
                freed(dve, S2["u"], at(i, b))
                masks(tyb[:, b, 1, :], gT[:], gm, S2["gm"])

            def l2_sum(i, b):
                g = at(i, b)
                dve.wait_ge(*S2["u"].count(g + 1))
                dve.wait_ge(*S2["hold"].count(g + 1))
                freed(dve, S2["y"], g)
                own.step(nc.vector.tensor_tensor(out=o2[:], in0=held[:, 0], in1=tiles(bank[:, 6, :]), op=ALU.add))
                ln_stats(own, o2, stats[:, 2], mv[:, b, 2], S2, "var3", "ln3", g)

            def l2_shift3(i, b):
                ln_shift(own, S2, "sd3", at(i, b), b, 2, mv, sd, rs, nb, "ln3")
                scatter_idx(own, S2, i, b, 2, *edge_keys(i, b))

            def l2_rows(i, b):
                g = at(i, b)
                dve.wait_ge(*S2["y"].count(g + 1))
                dve.wait_ge(*S2["ubgc"].count(g + 1))
                affine(own, S2, gain[:, 1], gain[:, 0], y2[:], held[:, 1], row[:, b], "row")

            own = Own(dve, own_dve["l2"])
            dve.wait_ge(R["tyout"], 16 * (TYC // P))
            nc.vector.memset(agg[:, 1, :], 0.0)
            nc.vector.memset(mx[:, 1, :], 0.0)
            nc.vector.memset(den[:, 1, :], 0.0).then_inc(weights, 1)
            dve.wait_ge(weights, 4)
            l2_next(0, 0)
            l2_next(0, 1)
            pipeline(dve, HALF, [(None, lag, work) for lag, work in (
                (1, l2_mask_src), (1, l2_one_hots), (1, l2_mask_dst), (3, l2_sum),
                (1, l2_mask_k), (2, l2_den), (1, l2_mask_v), (2, l2_rden), (3, l2_shift3), (2, l2_agg),
                (0, l2_stats), (-2, l2_next), (2, l2_divide), (3, l2_rows), (1, l2_prod), (2, l2_mask_upd),
                (0, l2_shift), (1, l2_max), (0, l2_restarts))], own)
            stage_done(dve, "l2", 2)

            S3 = L["l3"]

            def l3_next(i, b):
                g = at(i, b)
                dve.wait_ge(*S3["rec"][b].count(48 * i + 48))
                freed(dve, S3["src"][b], 16 * T * i)
                freed(dve, S3["dst"][b], 16 * T * i)
                nc.vector.tensor_copy(gidx[:, b, 0:4], edge_rec[:, b, :, 3])
                nc.vector.tensor_copy(gidx[:, b, 4:8], edge_rec[:, b, :, 2]).then_inc(S3["gidx"].sem, 1)
                key = edge_rec[:, b, :, 2]
                own.step(nc.vector.tensor_tensor(out=same[:, b, :], in0=key, in1=edge_rec[:, b, :, 4], op=ALU.is_equal))
                nc.vector.scalar_tensor_tensor(out=place3[:, b, :], in0=same[:, b, :], scalar=float(FAR),
                                               in1=key, op0=ALU.mult, op1=ALU.add)
                freed(dve, S3["gate"], g - 1)
                nc.vector.tensor_tensor(out=gcol[:, b, :], in0=key, in1=edge_rec[:, b, :, 0], op=ALU.is_equal)\
                  .then_inc(S3["gcol"].sem, 1)

            def l3_places(i, b):
                own.step(nc.vector.tensor_copy(place4[:, b, :], place3[:, b, :]))

            def l3_stats(i, b):
                g = at(i, b)
                dve.wait_ge(*S3["src"][b].count(16 * T * (i + 1)))
                ln_stats(own, xs[:, b], stats[:, 0], mv[:, b, 0], S3, "var", "ln", g)
                dve.wait_ge(*S3["dst"][b].count(16 * T * (i + 1)))
                dve.wait_ge(*S3["var"].count(g + 1))
                ln_stats(own, xd[:, b], stats[:, 1], mv[:, b, 1], S3, "vard", "lnd", g)

            def l3_shift(i, b):
                ln_shift(own, S3, "sd", at(i, b), b, 0, mv, sd, rs, nb, "ln")
                ln_shift(own, S3, "sdd", at(i, b), b, 1, mv, sd, rs, nb, "lnd")

            def l3_clip(i, b):
                dve.wait_ge(*S3["scc"].count(at(i, b) + 1))
                own.step(nc.vector.scalar_tensor_tensor(out=sc3[:], in0=sc3[:], scalar=0.2, in1=sc3[:],
                                                        op0=ALU.mult, op1=ALU.max))
                nc.vector.tensor_scalar(sc3[:], sc3[:], -2.0, 2.0, ALU.max, ALU.min).then_inc(S3["clip"].sem, 1)

            def l3_sums(i, b):
                g = at(i, b)
                dve.wait_ge(*S3["ex"].count(g + 1))
                dve.wait_ge(*S3["t"].count(g + 1))
                own.step(nc.vector.tensor_tensor(out=hE[:], in0=bank[:, 6 * b, :], in1=ex[:, b, :], op=ALU.mult))
                dve.wait_ge(*S3["gate"].count(g + 1))
                freed(dve, S3["z"], g - 1)
                freed(dve, S3["agg"], g)
                nc.vector.tensor_tensor_scan(out=agg[:, b, :], data0=bank[:, 3 + 4 * b, :], data1=hE[:],
                                             initial=agg[:, 1 - b, G - 1:G], op0=ALU.mult, op1=ALU.add)
                nc.vector.tensor_tensor_scan(out=den3[:, b, :], data0=bank[0:1, 3 + 4 * b, :], data1=ex[0:1, b, :],
                                             initial=den3[:, 1 - b, G - 1:G], op0=ALU.mult, op1=ALU.add)\
                  .then_inc(S3["agg"].sem, 1)

            def l3_rows(i, b):
                freed(dve, S3["scat"][b], 16 * T * i)
                own.step(nc.vector.tensor_copy(sidx[:, b, :], place4[:, b, :]))
                dve.wait_ge(*S3["z"].count(at(i, b) + 1))
                own.step(nc.vector.tensor_scalar(rd3[:], bank[:, 5, 0:T], 1e-9, None, ALU.add))
                own.step(nc.vector.reciprocal(rd3[:], rd3[:]))
                for t in range(T):
                    last = nc.vector.scalar_tensor_tensor(out=row[:, b, t, :], in0=bank[:, 4, t * P:(t + 1) * P],
                                                          scalar=rd3[:, t:t + 1], in1=keep[:, b, t, :],
                                                          op0=ALU.mult, op1=ALU.add)
                last.then_inc(S3["row"].sem, 1)

            own = Own(dve, own_dve["l3"])
            nc.vector.memset(agg[:, 1, :], 0.0)
            nc.vector.memset(den3[:, 1, :], 0.0).then_inc(weights, 1)
            dve.wait_ge(weights, 5)
            l3_next(0, 0)
            pipeline(dve, HALF, [(None, lag, work) for lag, work in (
                (1, l3_places), (-1, l3_next), (2, l3_sums), (0, l3_stats), (1, l3_clip), (0, l3_shift),
                (2, l3_rows))], own)

        @block.scalar
        def _(act):
            def std(S, var_ready, g, m, s_, ready):
                act.wait_ge(*S[var_ready].count(g + 1))
                nc.scalar.activation(s_, m[:, :, 1], ACT.Sqrt, bias=epsc[:, 0:1]).then_inc(S[ready].sem, 1)

            def normed(S, ln_ready, g, dst, src, r_, n_, func, ready):
                act.wait_ge(*S[ln_ready].count(g + 1))
                for t in range(T):
                    last = nc.scalar.activation(dst[:, t, :], src[:, t, :], func, bias=n_[:, t:t + 1], scale=r_[:, t:t + 1])
                last.then_inc(S[ready].sem, 1)

            def copy(S, wanted, g, dst, src, ready, func=ACT.Copy, **kw):
                act.wait_ge(*S[wanted].count(g + 1))
                nc.scalar.activation(dst, src, func, **kw).then_inc(S[ready].sem, 1)

            act.wait_ge(w_in, N_IN)
            act.wait_ge(consts, N_CONST)

            def store_p(i, b):
                act.wait_ge(p_sum, at(i, b) + 1)
                freed(act, p_out[b], 16 * i)
                nc.scalar.activation(yn[:, b], tiles(bank[:, b, :]), ACT.Copy).then_inc(p_copy, 1)
                act.wait_ge(p_copy, at(i, b) + 1)
                act.dma_start(rows(x1, at(i, b)), yn[:, b]).then_inc(p_out[b], 16)

            def place_turned(i, m):
                t = node(i, m)
                act.wait_ge(R["olt"], t + 1)
                freed(act, R["look"], t - 1)
                nc.scalar.activation(OLT[:, m % 2, :], bank[:, 3, 0:P], ACT.Copy).then_inc(R["oltc"], 1)
            pipeline(act, NT // 4, [(0, 0, place_turned), (1, 0, place_turned), (None, 0, store_p)])

            def keep_rows(l, last="row"):
                S = L[l]

                def work(i, b):
                    act.wait_ge(*S["dst"][b].count(16 * T * (i + 1)))
                    freed(act, S[last], at(i, b) - 1)
                    nc.scalar.activation(keep[:, b], xd[:, b], ACT.Copy).then_inc(S["keep"].sem, 1)
                return work

            def a_norm(i, m):
                q = node(i, m)
                std(A, "var", q, mvn[:, m % 2, 0], sdn[:, m % 2, 0, :], "sd")
                freed(act, A["t"], q - 1)
                normed(A, "ln", q, hn[:, m % 2], yn[:, m], rsn[:, m % 2, 0], nbn[:, m % 2, 0], ACT.Relu, "h")

            def a_turned(i, m):
                freed(act, A["z"], node(i, m) - 3)
                copy(A, "t", node(i, m), hnT[:, m, :], bank[:, 0, :], "tc")

            def a_hidden(i, m):
                freed(act, A["z"], node(i, m) - 1)
                copy(A, "u", node(i, m), unT[:, m % 2, :], bank[:, 1, :], "uc", ACT.Relu, bias=b1c[:, 0:1])

            def a_store(i, m):
                act.wait_ge(*A["x2"].count(node(i, m) + 1))
                for target in (x2, x2n):
                    act.dma_start(rows(target, node(i, m)), on[:, m % 2]).then_inc(A["out"][m].sem, 16)

            def l0_std(i, b):
                std(L["l0"], "var", at(i, b), mv[:, b, 0], sd[:, b, 0, :], "sd")

            def l0_norm(i, b):
                S, g = L["l0"], at(i, b)
                freed(act, S["t"], g - 1)
                normed(S, "ln", g, hs[:, b], xs[:, b], rs[:, b, 0], nb[:, b, 0], ACT.Relu, "h")
            pipeline(act, HALF, [(0, 1, a_turned), (0, 4, a_store), (0, 2, a_hidden), (0, 0, a_norm), (None, 0, l0_std),
                                 (1, 1, a_turned), (1, 4, a_store), (1, 2, a_hidden), (None, 0, l0_norm),
                                 (1, 0, a_norm), (None, 0, keep_rows("l0"))])
            stage_done(act, "l0")
            for m in range(4):
                act.wait_ge(*A["out"][m].count(32 * HALF))

            def b_std(i, m):
                std(B, "var", node(i, m), mvn[:, m % 2, 0], sdn[:, m % 2, 0, :], "sd")

            def b_std2(i, m):
                std(B, "var2", node(i, m), mvn[:, m % 2, 1], sdn[:, m % 2, 1, :], "sd2")

            def b_norm(i, m):
                q = node(i, m)
                freed(act, B["bu"], q - 1)
                normed(B, "ln", q, hn[:, m % 2], xn[:, m], rsn[:, m % 2, 0], nbn[:, m % 2, 0], ACT.Relu, "h")

            def b_norm2(i, m):
                q = node(i, m)
                freed(act, B["x3"], q - 3)
                normed(B, "ln2", q, yn[:, m], tiles(bank[:, 4 + 3 * (m % 2), :]), rsn[:, m % 2, 1], nbn[:, m % 2, 1],
                       ACT.Identity, "y")

            def b_store(i, m):
                act.wait_ge(*B["x3"].count(node(i, m) + 1))
                for target in (x3, out):
                    act.dma_start(rows(target, node(i, m)), xo[:, m % 2]).then_inc(B["out"][m].sem, 16)

            def l1_std(i, b):
                std(L["l1"], "var", at(i, b), mv[:, b, 0], sd[:, b, 0, :], "sd")
                std(L["l1"], "vard", at(i, b), mv[:, b, 1], sd[:, b, 1, :], "sdd")

            def l1_norm(i, b):
                S, g = L["l1"], at(i, b)
                freed(act, S["t"], g - 1)
                normed(S, "ln", g, hs[:, b], xs[:, b], rs[:, b, 0], nb[:, b, 0], ACT.Relu, "h")
                freed(act, S["td"], g - 1)
                normed(S, "lnd", g, hd[:, b], xd[:, b], rs[:, b, 1], nb[:, b, 1], ACT.Relu, "hd")

            def l1_turned(i, b):
                freed(act, L["l1"]["z"], at(i, b) - 1)
                copy(L["l1"], "td", at(i, b), hdT[:, b, :], bank[:, 1, :], "tdc")

            def l1_hidden(i, b):
                freed(act, L["l1"]["z"], at(i, b))
                copy(L["l1"], "u", at(i, b), uT[:], bank[:, 2, :], "uc", ACT.Relu, bias=b1c[:, 0:1])
            pipeline(act, HALF, [(None, 1, l1_turned), (0, 3, b_store), (0, 0, b_std), (0, 1, b_std2), (0, 0, b_norm),
                                 (0, 1, b_norm2), (None, 0, l1_std),
                                 (1, 3, b_store), (1, 0, b_std), (1, 1, b_std2), (1, 0, b_norm), (None, 0, l1_norm),
                                 (None, 1, l1_hidden), (1, 1, b_norm2), (None, 0, keep_rows("l1"))])
            stage_done(act, "l1")
            for m in range(4):
                act.wait_ge(*B["out"][m].count(32 * HALF))

            S2 = L["l2"]

            def l2_exp(i, b):
                freed(act, S2["c"], at(i, b))
                freed(act, S2["den"], at(i, b))
                copy(S2, "ein", at(i, b), eo[:], ein[:], "eo", ACT.Exp)

            def l2_weights(i, b):
                freed(act, S2["va"], at(i, b))
                copy(S2, "a", at(i, b), aS[:], bank[:, 0, :], "ac")

            def l2_spread_rden(i, b):
                freed(act, S2["r"], at(i, b))
                copy(S2, "rden", at(i, b), rb[:], rr[:, :, :].unsqueeze(3).to_broadcast([P, T, H, DK]), "rb")

            def l2_query(i, b):
                freed(act, S2["prod"], at(i, b))
                copy(S2, "q", at(i, b), qT[:], bank[:, 4, :], "qc")

            def l2_gelu(i, b):
                freed(act, S2["gm"], at(i, b))
                copy(S2, "nrm", at(i, b), gT[:], nrm[:], "g", ACT.Gelu)

            def l2_std(i, b):
                std(S2, "var", at(i, b), mv[:, b, 0], sd[:, b, 0, :], "sd")
                std(S2, "vard", at(i, b), mv[:, b, 1], sd[:, b, 1, :], "sdd")

            def l2_norm(i, b):
                g = at(i, b)
                freed(act, S2["s"], g - 1)
                normed(S2, "ln", g, hs[:, b], xs[:, b], rs[:, b, 0], nb[:, b, 0], ACT.Relu, "h")
                freed(act, S2["d"], g - 1)
                freed(act, S2["hold"], g - 1)
                normed(S2, "lnd", g, hd[:, b], xd[:, b], rs[:, b, 1], nb[:, b, 1], ACT.Relu, "hd")

            def l2_std3(i, b):
                std(S2, "var3", at(i, b), mv[:, b, 2], sd[:, b, 2, :], "sd3")

            def l2_norm3(i, b):
                freed(act, S2["row"], at(i, b))
                normed(S2, "ln3", at(i, b), y2, o2, rs[:, b, 2], nb[:, b, 2], ACT.Identity, "y")

            def l2_hold(i, b):
                g = at(i, b)
                act.wait_ge(*S2["hd"].count(g + 1))
                act.wait_ge(*S2["keep"].count(g + 1))
                freed(act, S2["row"], g)
                nc.scalar.activation(held[:, 0], hd[:, b], ACT.Copy)
                nc.scalar.activation(held[:, 1], keep[:, b], ACT.Copy).then_inc(S2["hold"].sem, 1)

            def l2_gain(i, b):
                freed(act, S2["row"], at(i, b))
                copy(S2, "ubg", at(i, b), gain[:], bank[:, 3:5, :].rearrange("p k (t d) -> p k t d", t=T), "ubgc")
            pipeline(act, HALF, [(None, lag, work) for lag, work in (
                (2, l2_exp), (3, l2_std3), (2, l2_weights), (2, l2_spread_rden), (3, l2_norm3), (1, l2_query),
                (0, l2_std), (2, l2_gelu), (2, l2_hold), (0, l2_norm), (0, keep_rows("l2", "hold")), (2, l2_gain))])
            stage_done(act, "l2", 2)

            S3 = L["l3"]

            def l3_std(i, b):
                std(S3, "var", at(i, b), mv[:, b, 0], sd[:, b, 0, :], "sd")
                std(S3, "vard", at(i, b), mv[:, b, 1], sd[:, b, 1, :], "sdd")

            def l3_norm(i, b):
                g = at(i, b)
                freed(act, S3["t"], g - 1)
                normed(S3, "ln", g, hs[:, b], xs[:, b], rs[:, b, 0], nb[:, b, 0], ACT.Relu, "h")
                freed(act, S3["td"], g - 1)
                normed(S3, "lnd", g, hd[:, b], xd[:, b], rs[:, b, 1], nb[:, b, 1], ACT.Relu, "hd")

            def l3_turned(i, b):
                freed(act, S3["sco"], at(i, b))
                copy(S3, "t", at(i, b), uT[:], bank[:, 6 * b, :], "he")
                copy(S3, "td", at(i, b), hdT[:, b, :], bank[:, 1, :], "tdc")

            def l3_scores(i, b):
                freed(act, S3["ex"], at(i, b))
                copy(S3, "sco", at(i, b), sc3[:], bank[:, 2, :], "scc")

            def l3_exp(i, b):
                freed(act, S3["agg"], at(i, b) - 1)
                copy(S3, "clip", at(i, b), ex[:, b, :], sc3[:], "ex", ACT.Exp)
            pipeline(act, HALF, [(None, lag, work) for lag, work in (
                (1, l3_turned), (1, l3_scores), (0, l3_std), (0, l3_norm), (0, keep_rows("l3")), (1, l3_exp))])

        @block.tensor
        def _(pe):
            def transposes(dst, src, ready):
                for t in range(T):
                    last = nc.tensor.transpose(dst[:, t * P:(t + 1) * P], src[:, t, :], ident[:])
                last.then_inc(ready.sem, 1)

            def project(dst, terms, bias, ready):
                for t in range(T):
                    c = slice(t * P, (t + 1) * P)
                    for n, (colsT, W) in enumerate(terms):
                        last = nc.tensor.matmul(dst[:, c], colsT[:, c], W[:], start=(n == 0),
                                                stop=(bias is None and n == len(terms) - 1))
                    if bias is not None:
                        last = nc.tensor.matmul(dst[:, c], onesb[:], rowparts[:, bias, :], start=False, stop=True)
                last.then_inc(ready.sem, 1)

            pe.wait_ge(w_in, N_IN)
            pe.wait_ge(consts, N_CONST)
            nc.tensor.matmul(bank[:, 0, 0:K], headT[:], pri[:], start=True, stop=True).then_inc(prep["pri"], 1)
            nc.tensor.transpose(bank[:, 1, 0:P], W3[:], ident[:]).then_inc(prep["t"], 1)
            pe.wait_ge(prep["copy"], 1)
            nc.tensor.matmul(bank[:, 2, 0:2], W3T[:], ka[:], start=True, stop=True).then_inc(prep["wsc"], 1)
            pe.wait_ge(weights, 1)

            def count(i, m):
                t = node(i, m)
                pe.wait_ge(R["one"], t + 1)
                nc.tensor.matmul(bank[:, 5, 0:NHI], OL[:, m % 2, :], OH[:, m % 2, :], start=isinstance(t, int) and t == 0,
                                 stop=isinstance(t, int) and t == NT - 1).then_inc(R["hist"], 1)
            pipeline(pe, NT // 4, [(0, 0, count), (1, 0, count)])
            pe.wait_ge(R["rowsum"], 1)
            nc.tensor.matmul(bank[:, 6, 0:1], above[:], offs[:], start=True, stop=True).then_inc(R["offs"], 1)

            def place_tile(i, m):
                t = node(i, m)
                pe.wait_ge(R["one"], t + 1 + NT)
                freed(pe, R["oltc"], t)
                nc.tensor.matmul(bank[:, 3, 0:P], OL[:, m % 2, :], identb[:], start=True, stop=True).then_inc(R["olt"], 1)
                freed(pe, R["tab"], t)
                nc.tensor.matmul(bank[:, 4 + m % 2, 0:NHI], OL[:, m % 2, :], OH[:, m % 2, :], start=True, stop=True)\
                  .then_inc(R["tile"], 1)

            def rows_p(i, b):
                pe.wait_ge(p_in[b], 16 * i + 16)
                freed(pe, p_copy, at(i, b) - 1)
                nc.tensor.matmul(bank[:, b, :], ident[:], xn[:, b].rearrange("p t d -> p (t d)"), start=True, stop=False)
                for t in range(T):
                    last = nc.tensor.matmul(bank[:, b, t * P:(t + 1) * P], onesb[:], rowparts[:, 2, :],
                                            start=False, stop=(t == T - 1))
                last.then_inc(p_sum, 1)

            def place_look(i, m):
                t = node(i, m)
                pe.wait_ge(R["oltc"], t + 1)
                pe.wait_ge(R["tab"], t + 1)
                freed(pe, R["pos"], t - 1)
                nc.tensor.matmul(bank[:, 6 + m % 2, 0:NHI], OLT[:, m % 2, :], table[:], start=True, stop=True)\
                  .then_inc(R["look"], 1)
            pipeline(pe, NT // 4, [(c, lag, work) for c in range(2) for lag, work in ((1, place_look), (0, place_tile))]
                     + [(None, 0, rows_p)])
            pe.wait_ge(R["tycol"], 2 * NT)
            for c in range(TYC // P):
                last = nc.tensor.transpose(bank[:, 0, c * P:(c + 1) * P], tycol[:, c * P:(c + 1) * P], ident[:])
            last.then_inc(R["tyturn"], 1)
            pe.wait_ge(R["tyrow"], 1)

            def a_turn(i, m):
                pe.wait_ge(*A["h"].count(node(i, m) + 1))
                freed(pe, A["tc"], node(i, m))
                transposes(bank[:, 0, :], hn[:, m % 2], A["t"])

            def a_hidden(i, m):
                pe.wait_ge(*A["tc"].count(node(i, m) + 1))
                freed(pe, A["uc"], node(i, m))
                nc.tensor.matmul(bank[:, 1, :], W1[:], hnT[:, m, :], start=True, stop=True).then_inc(A["u"].sem, 1)

            def a_rows(i, m):
                pe.wait_ge(*A["uc"].count(node(i, m) + 1))
                freed(pe, A["x2"], node(i, m))
                project(bank[:, 2, :], [(unT[:, m % 2, :], W2), (hnT[:, m, :], Wr)], 1, A["z"])

            def l0_turn(i, b):
                pe.wait_ge(*L["l0"]["h"].count(at(i, b) + 1))
                freed(pe, L["l0"]["agg"], at(i, b))
                transposes(bank[:, 3, :], hs[:, b], L["l0"]["t"])

            def l0_rows(i, b):
                pe.wait_ge(*L["l0"]["agg"].count(at(i, b) + 1))
                freed(pe, L["l0"]["row"], at(i, b))
                project(bank[:, 4, :], [(agg[:, b, :], W0)], 0, L["l0"]["z"])
            pipeline(pe, HALF, [(None, 1, l0_turn), (0, 1, a_turn), (0, 2, a_hidden), (0, 3, a_rows), (None, 1, l0_rows),
                                (1, 1, a_turn), (1, 2, a_hidden), (1, 3, a_rows)])
            stage_done(pe, "l0")
            for m in range(4):
                pe.wait_ge(*A["out"][m].count(32 * HALF))

            def type_rows(n, oh, which, added=False):
                for t in range(T):
                    last = nc.tensor.matmul(bank[:, n, t * P:(t + 1) * P], oh[:, t * P:(t + 1) * P], tparts[:, 3 + which, :],
                                            start=not added, stop=not added or t == T - 1)
                return last

            def plus_rows(n, src):
                return nc.tensor.matmul(bank[:, n, :], ident[:], src.rearrange("p t d -> p (t d)"), start=True, stop=False)

            def b_bias(i, m):
                q = node(i, m)
                pe.wait_ge(*B["h"].count(q + 1))
                pe.wait_ge(*B["oh"].count(q + 1))
                freed(pe, B["y"], q - 1)
                plus_rows(4 + 3 * (m % 2), hn[:, m % 2])
                type_rows(4 + 3 * (m % 2), ohn[:, m, :], 0, added=True).then_inc(B["bu"].sem, 1)

            def b_affine(i, m):
                freed(pe, B["x3"], node(i, m))
                type_rows(5, ohn[:, m, :], 1)
                plus_rows(6, xn[:, m])
                type_rows(6, ohn[:, m, :], 2, added=True).then_inc(B["gb"].sem, 1)

            def l1_turn(i, b):
                S, g = L["l1"], at(i, b)
                pe.wait_ge(*S["h"].count(g + 1))
                freed(pe, S["agg"], g)
                transposes(bank[:, 0, :], hs[:, b], S["t"])
                pe.wait_ge(*S["hd"].count(g + 1))
                freed(pe, S["tdc"], g)
                transposes(bank[:, 1, :], hd[:, b], S["td"])

            def l1_hidden(i, b):
                S, g = L["l1"], at(i, b)
                pe.wait_ge(*S["tdc"].count(g + 1))
                pe.wait_ge(*S["agg"].count(g + 1))
                freed(pe, S["uc"], g)
                nc.tensor.matmul(bank[:, 2, :], W1[:], hdT[:, b, :], start=True, stop=False)
                nc.tensor.matmul(bank[:, 2, :], W1[:], agg[:, b, :], start=False, stop=True).then_inc(S["u"].sem, 1)

            def l1_rows(i, b):
                S, g = L["l1"], at(i, b)
                pe.wait_ge(*S["uc"].count(g + 1))
                freed(pe, S["row"], g)
                project(bank[:, 3, :], [(uT, W2), (hdT[:, b, :], Wr)], 1, S["z"])
            pipeline(pe, HALF, [(0, 1, b_bias), (None, 1, l1_turn), (None, 2, l1_rows), (0, 2, b_affine),
                                (1, 1, b_bias), (None, 1, l1_hidden), (1, 2, b_affine)])
            stage_done(pe, "l1")
            for m in range(4):
                pe.wait_ge(*B["out"][m].count(32 * HALF))

            S2 = L["l2"]

            def typed(n, W, which, cols, oh, g, ready):
                for k in range(K):
                    nc.tensor.matmul(bank[:, n, :], W[:, k, :], cols[:, k, :], start=(k == 0), stop=False)
                pe.wait_ge(*S2["oh"].count(g + 1))
                nc.tensor.matmul(bank[:, n, :], tparts[:, which, :], oh, start=False, stop=True).then_inc(ready.sem, 1)

            def related(n, W, cols, ready):
                for r in range(K):
                    last = nc.tensor.matmul(bank[:, n, :], W[:, r, :], cols[:, r, :], start=(r == 0), stop=(r == K - 1))
                last.then_inc(ready.sem, 1)

            def l2_turn(i, b):
                g = at(i, b)
                pe.wait_ge(*S2["h"].count(g + 1))
                freed(pe, S2["ac"], g - 1)
                transposes(bank[:, 0, :], hs[:, b], S2["s"])
                pe.wait_ge(*S2["hd"].count(g + 1))
                freed(pe, S2["agg"], g - 1)
                transposes(bank[:, 1, :], hd[:, b], S2["d"])

            def l2_key(i, b):
                g = at(i, b)
                pe.wait_ge(*S2["ms"].count(g + 1))
                freed(pe, S2["prod"], g)
                typed(2, Wk, 1, sT, ohT[:, b, 0, :], g, S2["k"])

            def l2_value(i, b):
                freed(pe, S2["ubgc"], at(i, b) - 1)
                typed(3, Wv, 2, sT, ohT[:, b, 0, :], at(i, b), S2["v"])

            def l2_query(i, b):
                pe.wait_ge(*S2["md"].count(at(i, b) + 1))
                typed(4, Wq, 0, dT, ohT[:, b, 1, :], at(i, b), S2["q"])

            def l2_relate(i, b):
                g = at(i, b)
                pe.wait_ge(*S2["km"].count(g + 1))
                related(2, Ra, km, S2["kr"])
                pe.wait_ge(*S2["vm"].count(g + 1))
                freed(pe, S2["va"], g)
                related(5, Rm, vm, S2["m"])

            def l2_att(i, b):
                g = at(i, b)
                pe.wait_ge(*S2["prod"].count(g + 1))
                freed(pe, S2["nrm"], g)
                nc.tensor.matmul(bank[0:H, 7, :], head[:], prod[:], start=True, stop=True).then_inc(S2["att"].sem, 1)

            def l2_spread(i, b):
                g = at(i, b)
                pe.wait_ge(*S2["eo"].count(g + 1))
                used(pe, S2["ms"], g + 2, NGE)
                nc.tensor.matmul(bank[:, 0, :], headT[:], eo[:, 0, :], start=True, stop=True).then_inc(S2["a"].sem, 1)
                used(pe, S2["md"], g + 2, NGE)
                nc.tensor.matmul(bank[:, 1, :], headT[:], eo[:, 1, :], start=True, stop=True).then_inc(S2["c"].sem, 1)
                pe.wait_ge(*S2["den"].count(g + 1))
                freed(pe, S2["var3"], g)
                pe.sem_inc(pe_turn, 1)
                for t in range(T):
                    last = nc.tensor.matmul(bank[:, 6, t * H:(t + 1) * H], den[:, b, t * P:(t + 1) * P], ident[0:H, 0:H],
                                            start=True, stop=True)
                last.then_inc(S2["dent"].sem, 1)

            def l2_rden(i, b):
                pe.wait_ge(*S2["rb"].count(at(i, b) + 1))
                for t in range(T):
                    last = nc.tensor.transpose(bank[:, 7, t * P:(t + 1) * P], rb[:, t].rearrange("p h d -> p (h d)"),
                                               ident[:])
                last.then_inc(S2["r"].sem, 1)

            def l2_affine(i, b):
                g = at(i, b)
                used(pe, S2["vm"], g + 2, NGE)
                used(pe, S2["qc"], g + 2, NGE)
                type_rows(4, ohT[:, b, 1, :], 1)
                type_rows(3, ohT[:, b, 1, :], 2).then_inc(S2["ubg"].sem, 1)

            def l2_update(i, b):
                g = at(i, b)
                pe.wait_ge(*S2["gm"].count(g + 1))
                for t in range(T):
                    c = slice(t * P, (t + 1) * P)
                    for k in range(K):
                        nc.tensor.matmul(bank[:, 6, c], gm[:, k, c], Wu[:, k, :], start=(k == 0), stop=False)
                    last = nc.tensor.matmul(bank[:, 6, c], ohT[:, b, 1, c], tparts[:, 3, :], start=False, stop=True)
                last.then_inc(S2["u"].sem, 1)
            pipeline(pe, HALF, [(None, lag, work) for lag, work in (
                (1, l2_key), (1, l2_value), (2, l2_spread), (1, l2_query), (2, l2_rden), (1, l2_relate), (2, l2_affine),
                (1, l2_att), (2, l2_update), (0, l2_turn))])
            stage_done(pe, "l2", 2)

            S3 = L["l3"]

            def l3_turn(i, b):
                g = at(i, b)
                pe.wait_ge(*S3["h"].count(g + 1))
                freed(pe, S3["agg"], g - 1)
                transposes(bank[:, 6 * b, :], hs[:, b], S3["t"])
                pe.wait_ge(*S3["hd"].count(g + 1))
                freed(pe, S3["tdc"], g)
                transposes(bank[:, 1, :], hd[:, b], S3["td"])

            def l3_scores(i, b):
                g = at(i, b)
                pe.wait_ge(*S3["he"].count(g + 1))
                pe.wait_ge(*S3["tdc"].count(g + 1))
                freed(pe, S3["scc"], g)
                nc.tensor.matmul(bank[:, 2, :], wtx[:], hdT[:, b, :], start=True, stop=False)
                nc.tensor.matmul(bank[:, 2, :], wsx[:], uT[:], start=False, stop=True).then_inc(S3["sco"].sem, 1)

            def l3_gate(i, b):
                g = at(i, b)
                pe.wait_ge(*S3["gcol"].count(g + 1))
                freed(pe, S3["agg"], g - 1)
                for t in range(T):
                    last = nc.tensor.transpose(bank[:, 3 + 4 * b, t * P:(t + 1) * P], gcol[:, b, t:t + 1].to_broadcast([P, P]),
                                               ident[:])
                last.then_inc(S3["gate"].sem, 1)

            def l3_rows(i, b):
                g = at(i, b)
                pe.wait_ge(*S3["agg"].count(g + 1))
                freed(pe, S3["row"], g)
                pe.sem_inc(pe_turn, 1)
                for t in range(T):
                    nc.tensor.matmul(bank[:, 5, t:t + 1], den3[0:1, b, t * P:(t + 1) * P], ones1[0:1, 0:1],
                                     start=True, stop=True)
                project(bank[:, 4, :], [(agg[:, b, :], W3)], None, S3["z"])
            pipeline(pe, HALF, [(None, lag, work) for lag, work in (
                (1, l3_scores), (2, l3_rows), (0, l3_gate), (0, l3_turn))])


def kernel(**inputs):
    import numpy as np
    import concourse.bacc as bacc
    from concourse.bass_utils import run_bass_kernel_spmd as run

    x, src, dst = (np.asarray(inputs[n]) for n in ("x", "src", "dst"))
    N, E = x.shape[0], src.shape[0]
    EP = 2 * G * max(-(-E // (2 * G)), -(-(N + 1) // (4 * G)))
    NP = 2 * EP

    def pad(a, n, value):
        return np.concatenate([a, np.full((n - len(a),) + a.shape[1:], value, a.dtype)])

    srcp, dstp = pad(src, EP, NP - 1), pad(dst, EP, NP - 1)
    etype = pad(np.asarray(inputs["edge_type_3"]), EP, 0)
    ntype = pad(np.asarray(inputs["node_type_3"]), NP, 0)
    end = np.full(1, -1, dst.dtype)
    following = np.concatenate([dstp[1:], end])

    def columns(a):
        return a.reshape(EP // P, P).T

    eidx = np.stack([a.reshape(EP // G, T, P).transpose(2, 0, 1) for a in (srcp, dstp, following)], axis=2).reshape(P, -1)
    feed = {"x": pad(x, NP, 0), "eidx": eidx, "keys": np.concatenate([end, dstp]), "skeys": srcp, 
            "ends": np.stack([columns(srcp), columns(dstp)], axis=2), "etype": etype, "ntype": ntype.reshape(NP, 1)}
    names = [n for n in inputs if n[0] == "L"]
    feed.update({n: np.asarray(inputs[n]) for n in names})
    feed["L2_gnn_rel_pri"] = feed["L2_gnn_rel_pri"].T
    feed["L3_gnn_kernel_attention"] = feed["L3_gnn_kernel_attention"].reshape(2, D).T
    feed = {k: np.ascontiguousarray(v) for k, v in feed.items()}

    nc = bacc.Bacc("TRN2", target_bir_lowering=False, num_devices=1)
    ap = {k: nc.dram_tensor("in_" + k, v.shape, mybir.dt.from_np(v.dtype), kind="ExternalInput").ap() for k, v in feed.items()}
    scratch = {n: nc.dram_tensor("mem_" + n, (NP, D), F32, kind="Internal").ap() for n in ("x1", "x2", "x2n", "x3")}
    scratch["edge_kinds"] = nc.dram_tensor("mem_edge_kinds", (2 * EP // P, P), F32, kind="Internal").ap()
    scratch["rec"] = nc.dram_tensor("mem_rec", (EP + 2, 2), I32, kind="Internal").ap()
    out = nc.dram_tensor("out_x", (NP, D), F32, kind="ExternalOutput").ap()
    gnn(nc, NP, EP, ap["ends"], ap["x"], ap["eidx"], ap["keys"], ap["skeys"], ap["etype"], ap["ntype"],
        {n: ap[n] for n in names}, scratch, out)
    r = run(nc, [{"in_" + k: v for k, v in feed.items()}], core_ids=[0])
    return r.results[0]["out_x"][:N]
```
